# Optimizing a Trainium2 kernel written in Bass

```python
import numpy as np
import jax
import jax.numpy as jnp

def _softmax(x, axis=-1):
    return jax.nn.softmax(x, axis=axis)

def _gelu(x):
    return jax.nn.gelu(x, approximate=True)

def _silu(x):
    return jax.nn.silu(x)

def _sigmoid(x):
    return jax.nn.sigmoid(x)

def _layernorm(x, axis=-1, eps=1e-05):
    m = jnp.mean(x, axis=axis, keepdims=True)
    v = jnp.var(x, axis=axis, keepdims=True)
    return (x - m) / jnp.sqrt(v + eps)

def _scatter_add(tgt, idx, src, axis=0):
    return tgt.at[idx].add(src)

def _segment_sum(src, seg, n):
    return jax.ops.segment_sum(src, seg, n)
kernel_name = 'mk_early_fusion_d1_tok_img768_r4_84658f'

def setup_inputs(seed: int=0):
    np.random.seed(seed)
    _w = jnp.asarray

    def _rec_inputs():
        import jax
        import jax.numpy as jnp
        _rk = jax.random.key(seed)
        x = -0.000147625 + 0.999875 * jax.random.normal(jax.random.fold_in(_rk, 1), (32, 3, 224, 224), jnp.float32)
        txt = 0.000756012 + 0.999479 * jax.random.normal(jax.random.fold_in(_rk, 2), (32, 77, 192), jnp.float32)
        return (x, txt)
    x, txt = _rec_inputs()

    def _L0_tok_setup():
        import jax, jax.numpy as jnp
        import numpy as np
        N_PATCHES = 14

        def _patchify(images, n_patches):
            n, c, h, w = images.shape
            ps = h // n_patches
            x = images.reshape(n, c, n_patches, ps, n_patches, ps)
            x = x.transpose(0, 2, 4, 1, 3, 5)
            return x.reshape(n, n_patches * n_patches, c * ps * ps)
        key = jax.random.key(seed)
        k1, k2, k3 = jax.random.split(key, 3)
        batch, c, h, w = (64, 3, 224, 224)
        input_dim = c * (h // N_PATCHES) * (w // N_PATCHES)
        hidden_d = 192
        images = jax.random.normal(k1, (batch, c, h, w), dtype=jnp.float32)
        W = jax.random.normal(k2, (hidden_d, input_dim), dtype=jnp.float32) * input_dim ** (-0.5)
        b = jax.random.normal(k3, (hidden_d,), dtype=jnp.float32) * 0.01
        return {'images': images, 'W': W, 'b': b}
    _L0_tok_all = _L0_tok_setup()
    _L0_tok_in = {k: v for k, v in _L0_tok_all.items() if k in ('W', 'b')}
    del _L0_tok_all

    def _L0_attn_setup():
        import jax, jax.numpy as jnp
        import numpy as np
        EMBED_DIM = 192
        NUM_HEADS = 12
        HEAD_DIM = EMBED_DIM // NUM_HEADS
        SCALING = HEAD_DIM ** (-0.5)
        B, S = (2, 512)
        key = jax.random.key(seed)
        k1, k2, k3 = jax.random.split(key, 3)
        x_q = jax.random.normal(k1, (B, S, EMBED_DIM), dtype=jnp.float32)
        lim_qkv = (6.0 / (EMBED_DIM + 3 * EMBED_DIM)) ** 0.5
        lim_out = (6.0 / (2 * EMBED_DIM)) ** 0.5
        w_qkv = jax.random.uniform(k2, (3 * EMBED_DIM, EMBED_DIM), jnp.float32, -lim_qkv, lim_qkv)
        b_qkv = jnp.zeros((3 * EMBED_DIM,), jnp.float32)
        w_out = jax.random.uniform(k3, (EMBED_DIM, EMBED_DIM), jnp.float32, -lim_out, lim_out)
        b_out = jnp.zeros((EMBED_DIM,), jnp.float32)
        return {'x_q': x_q, 'w_qkv': w_qkv, 'b_qkv': b_qkv, 'w_out': w_out, 'b_out': b_out}
    _L0_attn_all = _L0_attn_setup()
    _L0_attn_in = {k: v for k, v in _L0_attn_all.items() if k in ('w_qkv', 'b_qkv', 'w_out', 'b_out')}
    del _L0_attn_all

    def _L0_ffn_setup():
        import jax, jax.numpy as jnp
        import numpy as np
        B, T, C, H, E, TOPK, DR = (2, 512, 192, 768, 8, 2, 24)

        def _normalize(v, axis=-1, eps=1e-12):
            return v / jnp.maximum(jnp.linalg.norm(v, axis=axis, keepdims=True), eps)
        key = jax.random.key(seed)
        ks = jax.random.split(key, 16)
        std = 0.02
        n = lambda k, shape, s=std: (s * jax.random.normal(k, shape)).astype(jnp.float32)
        emb = jax.random.normal(ks[3], (E, DR), dtype=jnp.float32)
        emb = emb / (jnp.linalg.norm(emb, axis=-1, keepdims=True) + 1e-08)
        return {'x': jax.random.normal(ks[0], (B, T, C), dtype=jnp.float32), 'router_w': n(ks[1], (E, C)), 'probe_w': n(ks[2], (DR, C)), 'router_emb': emb, 'fatigue': jnp.zeros((E,), jnp.float32), 'energy': jnp.ones((E,), jnp.float32), 'w_fast1': n(ks[4], (E, C, H)), 'w_slow1': n(ks[5], (E, C, H)), 'h_fast1': n(ks[6], (E, C, H), 0.005), 'm_gate1': jax.random.uniform(ks[7], (E,), dtype=jnp.float32), 'b1': jnp.zeros((E, H), jnp.float32), 'w_fast2': n(ks[8], (E, H, C)), 'w_slow2': n(ks[9], (E, H, C)), 'h_fast2': n(ks[10], (E, H, C), 0.005), 'm_gate2': jax.random.uniform(ks[11], (E,), dtype=jnp.float32), 'b2': jnp.zeros((E, C), jnp.float32)}
    _L0_ffn_all = _L0_ffn_setup()
    _L0_ffn_in = {k: v for k, v in _L0_ffn_all.items() if k in ('router_w', 'probe_w', 'router_emb', 'fatigue', 'energy', 'w_fast1', 'w_slow1', 'h_fast1', 'm_gate1', 'b1', 'w_fast2', 'w_slow2', 'h_fast2', 'm_gate2', 'b2')}
    del _L0_ffn_all
    return {'x': x, 'txt': txt, 'L0_tok_W': _L0_tok_in['W'], 'L0_tok_b': _L0_tok_in['b'], 'L0_attn_w_qkv': _L0_attn_in['w_qkv'], 'L0_attn_b_qkv': _L0_attn_in['b_qkv'], 'L0_attn_w_out': _L0_attn_in['w_out'], 'L0_attn_b_out': _L0_attn_in['b_out'], 'L0_ffn_router_w': _L0_ffn_in['router_w'], 'L0_ffn_probe_w': _L0_ffn_in['probe_w'], 'L0_ffn_router_emb': _L0_ffn_in['router_emb'], 'L0_ffn_fatigue': _L0_ffn_in['fatigue'], 'L0_ffn_energy': _L0_ffn_in['energy'], 'L0_ffn_w_fast1': _L0_ffn_in['w_fast1'], 'L0_ffn_w_slow1': _L0_ffn_in['w_slow1'], 'L0_ffn_h_fast1': _L0_ffn_in['h_fast1'], 'L0_ffn_m_gate1': _L0_ffn_in['m_gate1'], 'L0_ffn_b1': _L0_ffn_in['b1'], 'L0_ffn_w_fast2': _L0_ffn_in['w_fast2'], 'L0_ffn_w_slow2': _L0_ffn_in['w_slow2'], 'L0_ffn_h_fast2': _L0_ffn_in['h_fast2'], 'L0_ffn_m_gate2': _L0_ffn_in['m_gate2'], 'L0_ffn_b2': _L0_ffn_in['b2']}

def reference(x, txt, L0_tok_W, L0_tok_b, L0_attn_w_qkv, L0_attn_b_qkv, L0_attn_w_out, L0_attn_b_out, L0_ffn_router_w, L0_ffn_probe_w, L0_ffn_router_emb, L0_ffn_fatigue, L0_ffn_energy, L0_ffn_w_fast1, L0_ffn_w_slow1, L0_ffn_h_fast1, L0_ffn_m_gate1, L0_ffn_b1, L0_ffn_w_fast2, L0_ffn_w_slow2, L0_ffn_h_fast2, L0_ffn_m_gate2, L0_ffn_b2):
    import jax
    import jax.numpy as jnp

    def _L0_tok_ref(images, W, b):
        import jax, jax.numpy as jnp
        import numpy as np
        N_PATCHES = 14

        def _patchify(images, n_patches):
            n, c, h, w = images.shape
            ps = h // n_patches
            x = images.reshape(n, c, n_patches, ps, n_patches, ps)
            x = x.transpose(0, 2, 4, 1, 3, 5)
            return x.reshape(n, n_patches * n_patches, c * ps * ps)
        patches = _patchify(images, N_PATCHES)
        tokens = jnp.einsum('npd,hd->nph', patches, W) + b
        return tokens

    def _L0_attn_ref(x_q, w_qkv, b_qkv, w_out, b_out):
        import jax, jax.numpy as jnp
        import numpy as np
        EMBED_DIM = 192
        NUM_HEADS = 12
        HEAD_DIM = EMBED_DIM // NUM_HEADS
        SCALING = HEAD_DIM ** (-0.5)
        B, S = (2, 512)
        b_sz, s_len, _ = x_q.shape
        qkv = x_q @ w_qkv.T + b_qkv
        qkv = qkv.reshape(b_sz, s_len, 3, NUM_HEADS, HEAD_DIM)
        q = qkv[:, :, 0].transpose(0, 2, 1, 3) * SCALING
        k = qkv[:, :, 1].transpose(0, 2, 1, 3)
        v = qkv[:, :, 2].transpose(0, 2, 1, 3)
        attn = jnp.einsum('bhsd,bhtd->bhst', q, k)
        attn = jax.nn.softmax(attn.astype(jnp.float32), axis=-1).astype(attn.dtype)
        out = jnp.einsum('bhst,bhtd->bhsd', attn, v)
        out = out.transpose(0, 2, 1, 3).reshape(b_sz, s_len, EMBED_DIM)
        return out @ w_out.T + b_out

    def _L0_ffn_ref(x, router_w, probe_w, router_emb, fatigue, energy, w_fast1, w_slow1, h_fast1, m_gate1, b1, w_fast2, w_slow2, h_fast2, m_gate2, b2):
        import jax, jax.numpy as jnp
        import numpy as np
        B, T, C, H, E, TOPK, DR = (2, 512, 192, 768, 8, 2, 24)

        def _normalize(v, axis=-1, eps=1e-12):
            return v / jnp.maximum(jnp.linalg.norm(v, axis=axis, keepdims=True), eps)
        Bd, Td, Cd = x.shape
        logits = jnp.einsum('btc,ec->bte', x, router_w)
        tok_proxy = x.mean(axis=-1, keepdims=True)
        router_gain = jnp.linalg.norm(router_emb, axis=-1)
        base_bias = 0.02 * tok_proxy
        gain_bias = 0.02 * tok_proxy * router_gain
        tok_unit = _normalize(jnp.einsum('btc,dc->btd', x, probe_w))
        align_bias = 0.02 * jnp.einsum('btd,ed->bte', tok_unit, _normalize(router_emb))
        logits = logits + base_bias + gain_bias + align_bias + 0.1 * energy - 0.1 * fatigue
        g, idx = jax.lax.top_k(logits, TOPK)
        gates = jax.nn.softmax(g, axis=-1)
        N = Bd * Td
        gates_full = jnp.zeros((N, E), x.dtype).at[jnp.arange(N)[:, None], idx.reshape(N, TOPK)].set(gates.reshape(N, TOPK))
        flat_x = x.reshape(N, Cd)

        def body(acc, p):
            wf1, ws1, hf1, mg1, bb1, wf2, ws2, hf2, mg2, bb2, ge = p
            W1 = wf1 + mg1 * ws1 + hf1
            h = jnp.square(jnp.maximum(flat_x @ W1 + bb1, 0.0))
            W2 = wf2 + mg2 * ws2 + hf2
            y = h @ W2 + bb2
            return (acc + ge[:, None] * y, None)
        out, _ = jax.lax.scan(body, jnp.zeros((N, Cd), x.dtype), (w_fast1, w_slow1, h_fast1, m_gate1, b1, w_fast2, w_slow2, h_fast2, m_gate2, b2, gates_full.T))
        return out.reshape(Bd, Td, Cd)
    h = _L0_tok_ref(x, L0_tok_W, L0_tok_b)
    h = jnp.concatenate([h, txt], axis=1)
    h = h + _L0_attn_ref(_layernorm(h, axis=-1), L0_attn_w_qkv, L0_attn_b_qkv, L0_attn_w_out, L0_attn_b_out)
    h = h + _L0_ffn_ref(_layernorm(h, axis=-1), L0_ffn_router_w, L0_ffn_probe_w, L0_ffn_router_emb, L0_ffn_fatigue, L0_ffn_energy, L0_ffn_w_fast1, L0_ffn_w_slow1, L0_ffn_h_fast1, L0_ffn_m_gate1, L0_ffn_b1, L0_ffn_w_fast2, L0_ffn_w_slow2, L0_ffn_h_fast2, L0_ffn_m_gate2, L0_ffn_b2)
    return h

_drawn_inputs = setup_inputs


def setup_inputs(seed=0):
    import zlib

    import numpy as np

    out = dict(_drawn_inputs(seed))
    spreads = {'L0_attn_b_qkv': (0.0, 0.1),
     'L0_attn_b_out': (0.0, 0.1),
     'L0_ffn_fatigue': (0.0, 0.459),
     'L0_ffn_energy': (1.0, 0.6),
     'L0_ffn_b1': (0.0, 0.36),
     'L0_ffn_b2': (0.0, 0.1)}
    factors = {'L0_tok_b': 4.403,
     'L0_ffn_probe_w': 5.445,
     'L0_ffn_router_emb': 5.518,
     'L0_ffn_h_fast1': 3.736,
     'L0_ffn_m_gate1': 3.155,
     'L0_ffn_h_fast2': 4.391,
     'L0_ffn_m_gate2': 3.825}
    for name, (base, spread) in spreads.items():
        noise = np.random.default_rng([zlib.crc32(name.encode()), seed]).standard_normal(out[name].shape)
        drawn = base * np.exp(spread * noise) if base else spread * noise
        out[name] = jnp.asarray(drawn.astype(out[name].dtype))
    for name, factor in factors.items():
        out[name] = (out[name] * factor).astype(out[name].dtype)
    return out
```

```python
from contextlib import ExitStack

import concourse.bass as bass
from concourse import mybir

F32 = mybir.dt.float32
BF16 = mybir.dt.bfloat16
I32 = mybir.dt.int32
ALU = mybir.AluOpType
ACT = mybir.ActivationFunctionType
AX = mybir.AxisListType.X

IMAGES, PATCHES, TEXT, PIXELS = 32, 196, 77, 768
C, HEADS, D = 192, 12, 16
S = PATCHES + TEXT
GROUP = PATCHES // 2
GROUPS = 3
PAD = GROUP * GROUPS
HALF = C // 2
N = IMAGES * S
EXPERTS, HID, PROBE = 8, 768, 24
LN_EPS = 1e-5
TERMS = [(0, 0), (1, 1), (0, 1), (1, 0), (0, 2), (2, 0)]
SCORE_ROWS = D * len(TERMS)
SHIFT_ROWS = 3
ROUTE = EXPERTS + PROBE + EXPERTS + 1
TILE = 256
TOPK = 2
TILES = (TOPK * N - EXPERTS) // TILE + EXPERTS
CAP = N + TILE
ZERO_ROW = EXPERTS * CAP
ROW = C + 2
NO_TOKEN = float(N)
WCOLS = EXPERTS * C * HID // (128 * IMAGES)
HCH = HID // 128
MAXT = (N + TILE - 1) // TILE


class At:

    def __init__(self, loop, j, unroll):
        self.loop, self.j, self.unroll = loop, j, unroll

    def back(self, k):
        return At(self.loop, self.j - k, self.unroll)

    def ring(self, n):
        return self.j % n

    def exists(self, limit):
        return self.loop is not None or 0 <= self.j < limit

    def past(self, k):
        return self.loop is not None or self.j >= k

    def times(self, per, plus=0):
        if self.loop is None:
            return per * self.j + plus
        return self.loop * (per * self.unroll) + (per * self.j + plus)

    def done(self, per=1, n=None):
        return self.times(per, per if n is None else n)

    def uses(self, n, per):
        if self.loop is None:
            return (self.j // n + 1) * per
        return self.loop * (self.unroll // n * per) + (self.j // n + 1) * per


def positive(count):
    return not isinstance(count, int) or count > 0


def alone(eng, passed):
    eng.sem_inc(passed, 1)


class Counter:

    def __init__(self, per=0):
        self.per, self.at, self.k = per, At(None, 0, 1), 0

    def start(self, at, k=0):
        self.at, self.k = at, k

    def next(self):
        self.k += 1
        assert not self.per or self.k <= self.per
        return self.at.times(self.per, self.k)


STEPS = [
    (0, 0, "tok0", 0), (1, 0, "shift1", 2), (1, 1, "tok1", 0), (2, 0, "rank", 4),
    (4, 0, "xt0", 0), (4, 1, "xt1", 0), (5, 0, "qk0", 0), (5, 1, "qk1", 0), (6, 0, "qk2", 0),
    (6, 1, "shift0", 1), (7, 0, "v01", 0), (7, 1, "out01", 3), (8, 0, "v2", 0), (8, 1, "out2", 3),
    (10, 0, "x2t0", 3), (10, 1, "x2t1", 3), (11, 1, "route", 3),
]
LAST_LAG = 4
ITERATIONS = IMAGES + LAST_LAG
UNROLL = 4
LOOP_FROM, LOOP_TIMES = 5, 6
TILES_FROM = 5
TILES_TIMES = (TILES - TILES_FROM) // UNROLL


def iterations(eng, body):
    for i in range(LOOP_FROM):
        body(At(None, i, UNROLL))
    with eng.Fori(0, LOOP_TIMES, 1) as loop:
        for j in range(UNROLL):
            body(At(loop, LOOP_FROM + j, UNROLL))
    for i in range(LOOP_FROM + UNROLL * LOOP_TIMES, ITERATIONS):
        body(At(None, i, UNROLL))


def tiles(eng, body):
    for k in range(TILES_FROM):
        body(At(None, k, UNROLL))
    with eng.Fori(0, TILES_TIMES, 1) as loop:
        for j in range(UNROLL):
            body(At(loop, TILES_FROM + j, UNROLL))
    for k in range(TILES_FROM + UNROLL * TILES_TIMES, TILES + 1):
        body(At(None, k, UNROLL))


def build(nc, a, out):
    ctx = ExitStack()
    with ctx:
        phase1 = ExitStack()

        def kept(name, shape, dt=F32):
            return ctx.enter_context(nc.sbuf_tensor(name, shape, dt))

        def sb(name, shape, dt=F32):
            return phase1.enter_context(nc.sbuf_tensor(name, shape, dt))

        def sem(name):
            return ctx.enter_context(nc.semaphore(name))

        def sems(name, n):
            return [sem(f"{name}{i}") for i in range(n)]

        qk_dram = nc.dram_tensor("qk_parts", (2, 3, 2 * C, S), BF16).ap()
        den_dram = nc.dram_tensor("denominators", (2, 4, GROUPS, S), F32).ap()
        rden_dram = nc.dram_tensor("inverse_denominators", (2, 4, GROUPS, S), F32).ap()
        rows_dram = nc.dram_tensor("expert_rows", (ZERO_ROW + TILE, ROW), F32).ap()
        w1_dram = nc.dram_tensor("w1", (EXPERTS, C, HID), F32).ap()
        w2_dram = nc.dram_tensor("w2", (EXPERTS, HID, C), F32).ap()
        table_dram = nc.dram_tensor("tile_table", (TILES, 2), I32).ap()
        out_rows = out.rearrange("b s c -> (b s) c")

        ident = kept("ident", [128, 128])
        ramp = kept("ramp", [GROUP, EXPERTS])
        region = kept("region", [GROUP, EXPERTS])
        steps256 = kept("steps256", [GROUP, MAXT])
        tile_no = kept("tile_no", [GROUP, 2])
        base = kept("base", [GROUP, EXPERTS])
        empty = kept("empty", [128, 2, ROW])

        identb = sb("identb", [128, 128], BF16)
        before = sb("before", [GROUP, GROUP], BF16)
        ones = sb("ones", [GROUP, GROUP], BF16)
        place0 = sb("place0", [GROUP, GROUPS])
        half_neg = sb("half_neg", [GROUP, GROUPS])
        half_pos = sb("half_pos", [GROUP, EXPERTS])
        w_tok = sb("w_tok", [128, PIXELS // 128, C])
        b_tok = sb("b_tok", [GROUP, C])
        w_qkv = sb("w_qkv", [HALF + 1, 2, 3 * C])
        w_out = sb("w_out", [128, GROUPS, C])
        b_out = sb("b_out", [GROUP, C])
        w_route = sb("w_route", [HALF, 2, ROUTE])
        probe_w = sb("probe_w", [PROBE, C])
        emb_t = sb("emb_t", [PROBE, EXPERTS])
        emb_all = sb("emb_all", [GROUP, EXPERTS, PROBE])
        emb_sq = sb("emb_sq", [GROUP, EXPERTS, PROBE])
        gain = sb("gain", [GROUP, 4, EXPERTS])
        fatigue = sb("fatigue", [GROUP, EXPERTS])
        energy = sb("energy", [GROUP, EXPERTS])
        bias8 = sb("bias8", [GROUP, EXPERTS])
        m_gate = sb("m_gate", [128, 2])

        patches = [sb(f"patches{r}", [128, PIXELS // 128, PATCHES]) for r in range(2)]
        resid = [sb(f"resid{r}", [GROUP, GROUPS, C]) for r in range(4)]
        stats = [sb(f"stats{r}", [GROUP, GROUPS, 6]) for r in range(2)]
        mean_var = [sb(f"mean_var{r}", [GROUP, GROUPS, 2]) for r in range(2)]
        var_eps = [sb(f"var_eps{r}", [GROUP, GROUPS]) for r in range(2)]
        rstd = [sb(f"rstd{r}", [GROUP, GROUPS]) for r in range(2)]
        xn = sb("xn", [GROUP, GROUPS, C])
        xn_t = [sb(f"xn_t{r}", [HALF + 1, 2, PAD]) for r in range(2)]
        parts = [sb(f"parts{r}", [128, 9, S], BF16) for r in range(2)]
        rest = sb("rest", [128, 3, S])
        stack = [sb(f"stack{r}", [SCORE_ROWS + SHIFT_ROWS, 2 * HEADS, PAD], BF16) for r in range(4)]
        values = [sb(f"values{r}", [GROUP, GROUPS, HEADS, 32]) for r in range(4)]
        maxima = sb("maxima", [GROUP, GROUPS, HEADS])
        shift = [sb(f"shift{r}", [GROUP, GROUPS, 128], BF16) for r in range(2)]
        shift_rest = [sb(f"shift_rest{r}", [GROUP, GROUPS, 6]) for r in range(2)]
        shift_t = [sb(f"shift_t{r}", [18, S], BF16) for r in range(2)]
        probs = [sb(f"probs{r}", [GROUP, GROUPS, S]) for r in range(8)]
        heads_t = [sb(f"heads_t{r}", [128, GROUPS, S]) for r in range(2)]
        den = sb("den", [126, 26])
        rden = sb("rden", [126, 26])
        rden_all = [sb(f"rden_all{r}", [128, GROUPS, S]) for r in range(2)]
        attn_t = [sb(f"attn_t{r}", [128, GROUPS, PAD]) for r in range(2)]
        h2 = [sb(f"h2{r}", [GROUP, GROUPS, C]) for r in range(2)]
        rows = [[sb(f"rows{r}{k}", [GROUP, GROUPS, ROW]) for k in range(2)] for r in range(2)]
        xn2_t = sb("xn2_t", [HALF, 2, PAD])
        routed = sb("routed", [GROUP, GROUPS, ROUTE])
        sq = sb("sq", [GROUP, GROUPS, PROBE])
        nrm = sb("nrm", [GROUP, 4, GROUPS])
        logit = sb("logit", [GROUP, GROUPS, EXPERTS])
        align = sb("align", [GROUP, GROUPS, EXPERTS])
        tmp8 = sb("tmp8", [GROUP, GROUPS, EXPERTS])
        masked = sb("masked", [GROUP, GROUPS, EXPERTS])
        top = sb("top", [GROUP, 2, GROUPS])
        pick = sb("pick", [GROUP, 2, GROUPS])
        hot = sb("hot", [GROUP, 2, GROUPS * EXPERTS])
        chosen = sb("chosen", [GROUP, GROUPS, EXPERTS], BF16)
        gates = [sb(f"gates{r}", [GROUP, 5, GROUPS]) for r in range(2)]
        token = sb("token", [GROUP, GROUPS])
        pos = sb("pos", [GROUP, GROUPS * EXPERTS])
        pos2 = sb("pos2", [GROUP, 2, GROUPS * EXPERTS])
        posf = sb("posf", [GROUP, 2 * GROUPS])
        posi = [sb(f"posi{r}", [GROUP, 2 * GROUPS], I32) for r in range(2)]
        w_in = [[sb(f"w_in{r}{k}", [128, WCOLS]) for k in range(6)] for r in range(1)]
        w_sum = [[sb(f"w_sum{r}{k}", [128, WCOLS]) for k in range(2)] for r in range(1)]

        ps = ctx.enter_context(nc.psum_tensor("ps", [128, 8, 512], F32))
        ps_max = ps[:, 0:3, :]
        ps_key = ps[:, 3:6, :]
        ps_head = ps[:, 6, :]
        ps_mix = ps[:, 7, :]
        ps_mix_b = ps_mix.bitcast(BF16)

        made = {name: sem(f"made_{name}") for _, _, name, _ in STEPS}
        taken = {name: sem(f"taken_{name}") for _, _, name, _ in STEPS}
        LAG = {name: lag for _, _, name, lag in STEPS}
        const_in = sem("const_in")
        sp_passed, pool_passed, dve_passed = sem("sp_passed"), sem("pool_passed"), sem("dve_passed")
        weights_zeroed = sem("weights_zeroed")
        route_w_in = sem("route_w_in")
        setup_chain = sem("setup_chain")
        gain_sq = sem("gain_sq")
        gain_root = sem("gain_root")
        emb_ready = sem("emb_ready")
        align_made = sem("align_made")
        setup_done = sem("setup_done")
        pool_setup = sem("pool_setup")
        pads_zeroed = sem("pads_zeroed")
        patches_in = sems("patches_in", 2)
        text_in = sems("text_in", 2)
        stats_chain = sem("stats_chain")
        stats_ready = sem("stats_ready")
        rstd_chain = sem("rstd_chain")
        rstd_ready = sem("rstd_ready")
        xn_ready = sem("xn_ready")
        resid_biased = sem("resid_biased")
        part1_ready = sem("part1_ready")
        part2_ready = sem("part2_ready")
        part3_ready = sem("part3_ready")
        parts_out = sems("parts_out", 2)
        stack_in = sems("stack_in", 4)
        max_made = sem("max_made")
        max_taken = sem("max_taken")
        shift_chain = sems("shift_chain", 2)
        shift_ready = sems("shift_ready", 2)
        shift_in = sems("shift_in", 2)
        key_made = sem("key_made")
        exp_done = sem("exp_done")
        head_made = sem("head_made")
        head_taken = sem("head_taken")
        den_out = sem("den_out")
        den_in = sem("den_in")
        den_inverse = sem("den_inverse")
        rden_out = sem("rden_out")
        rden_in = sems("rden_in", 2)
        attn_ready = sem("attn_ready")
        h2_out = sems("h2_out", 2)
        stats2_chain = sem("stats2_chain")
        stats2_ready = sem("stats2_ready")
        rstd2_chain = sem("rstd2_chain")
        rstd2_ready = sem("rstd2_ready")
        xn2_ready = sem("xn2_ready")
        row_copied = sem("row_copied")
        norm2_ready = sem("norm2_ready")
        norm_ready = sem("norm_ready")
        route_chain = sem("route_chain")
        chosen_ready = sem("chosen_ready")
        top_gap = sem("top_gap")
        gate_exp = sem("gate_exp")
        gate_sum = sem("gate_sum")
        gate_inv = sem("gate_inv")
        gate_chain = sem("gate_chain")
        place_chain = sem("place_chain")
        pos_ready = sem("pos_ready")
        rows_out = sems("rows_out", 2)
        w_loaded = sem("w_loaded")
        w_chain = sem("w_chain")
        w_summed = sem("w_summed")
        w_stored = sem("w_stored")
        empty_ready = sem("empty_ready")
        empty_out = sem("empty_out")
        plan_chain = sem("plan_chain")
        ends_ready = sem("ends_ready")
        table_ready = sem("table_ready")
        table_out = sem("table_out")
        table_in = sem("table_in")
        ends_out = sem("ends_out")

        CONSTS = 30
        FILLS = 8
        flat_w = {}
        for k, n in enumerate(("w_fast", "w_slow", "h_fast")):
            for layer in range(2):
                flat_w[layer, k] = a[f"L0_ffn_{n}{layer + 1}"].rearrange("e a b -> (e a b)").rearrange(
                    "(p f) -> p f", p=128)
        w1_flat = w1_dram.rearrange("e a b -> (e a b)").rearrange("(p f) -> p f", p=128)
        w2_flat = w2_dram.rearrange("e a b -> (e a b)").rearrange("(p f) -> p f", p=128)
        image_in = a["patches"].rearrange("b (k p) t -> b p k t", p=128)

        block = phase1.enter_context(nc.Block())

        @block.sync
        def _(sp):
            loads = [0]

            def load(dst, src, signal=const_in):
                if signal is const_in:
                    loads[0] += 1
                sp.dma_start(dst, src).then_inc(signal, 16)

            def image_loads(at):
                if at.past(2):
                    sp.wait_ge(made["tok1"], at.back(2).done())
                src = image_in[at.j] if at.loop is None else image_in[bass.ds(at.times(1), 1)].rearrange(
                    "b p k t -> (b p) k t")
                sp.dma_start(patches[at.ring(2)][:], src).then_inc(patches_in[at.ring(2)], 16)

            def text_load(at):
                if at.past(4):
                    sp.wait_ge(taken["out2"], at.back(4).done())
                src = a["txt"][at.j] if at.loop is None else a["txt"][bass.ds(at.times(1), 1)].rearrange(
                    "b t c -> (b t) c")
                sp.dma_start(resid[at.ring(4)][0:TEXT, 2, :], src).then_inc(text_in[at.ring(2)], 16)

            def weight_loads(at):
                if at.past(1):
                    sp.wait_ge(w_summed, at.back(1).done(2))
                for layer in range(2):
                    for k in range(3):
                        sp.dma_start(w_in[0][3 * layer + k][:],
                                     flat_w[layer, k][:, bass.ds(at.times(WCOLS), WCOLS)]).then_inc(w_loaded, 16)

            load(w_tok[:], a["w_tok_t"].rearrange("(k p) h -> p k h", p=128))
            sp.wait_ge(pads_zeroed, 4)
            image_loads(At(None, 0, UNROLL))
            text_load(At(None, 0, UNROLL))
            load(b_tok[:], a["L0_tok_b"].partition_broadcast(GROUP))
            load(ident[:], a["ident"])
            load(identb[:], a["identb"])
            load(before[:], a["before"])
            load(w_qkv[0:HALF, :, :], a["w_qkv_t"].rearrange("(k p) n -> p k n", p=HALF))
            load(w_qkv[HALF:HALF + 1, 1, :], a["L0_attn_b_qkv"][None, :])
            load(ramp[:], a["ramp"].partition_broadcast(GROUP))
            load(region[:], a["region"].partition_broadcast(GROUP))
            load(steps256[:], a["steps256"].partition_broadcast(GROUP))
            load(place0[:], a["place0"])
            load(tile_no[:], a["tile_no"])
            load(base[:], a["region"].partition_broadcast(GROUP))
            load(emb_all[:].rearrange("p e d -> p (e d)"),
                 a["L0_ffn_router_emb"].rearrange("e d -> (e d)").partition_broadcast(GROUP))
            load(emb_t[:], a["emb_t"])
            load(probe_w[:], a["L0_ffn_probe_w"])
            load(fatigue[:], a["L0_ffn_fatigue"].partition_broadcast(GROUP))
            load(energy[:], a["L0_ffn_energy"].partition_broadcast(GROUP))
            load(b_out[:], a["L0_attn_b_out"].partition_broadcast(GROUP))
            sp.wait_ge(weights_zeroed, 1)
            for j in range(4):
                load(w_out[32 * j:32 * j + D, :, :],
                     a["w_out_t"].rearrange("(g j r) n -> j r g n", j=4, r=D)[j])
            for layer in range(2):
                load(m_gate[:, layer:layer + 1], a[f"m_gate{layer + 1}_rows"])
            for k in range(2):
                load(w_route[:, k, 0:EXPERTS], a["router_t"][k * HALF:(k + 1) * HALF, :])
                load(w_route[:, k, EXPERTS:EXPERTS + PROBE], a["probe_t"][k * HALF:(k + 1) * HALF, :])
            assert loads[0] == CONSTS - 1, loads
            image_loads(At(None, 1, UNROLL))
            text_load(At(None, 1, UNROLL))
            weight_loads(At(None, 0, UNROLL))

            def shift_rows(at, half):
                sp.wait_ge(taken[f"shift{half}"], at.done())
                for k in range(SHIFT_ROWS):
                    row = SCORE_ROWS + k
                    sp.dma_start(stack[at.ring(4)][row:row + 1, 6 * half:6 * half + 6, 0:S],
                                 shift_t[half][6 * k:6 * k + 6, :]).then_inc(shift_in[half], 16)

            def denominators(at):
                r = at.ring(2)
                sp.wait_ge(head_taken, at.done(GROUPS))
                sp.dma_start(den_dram[r], heads_t[r][D:128:32, :, :]).then_inc(den_out, 16)
                sp.wait_ge(den_out, at.done(16))
                sp.dma_start(den[:], den_dram[r].rearrange("j g t -> (j g t)").rearrange(
                    "(p f) -> p f", p=126)).then_inc(den_in, 16)
                sp.wait_ge(den_inverse, at.done())
                sp.dma_start(rden_dram[r].rearrange("j g t -> (j g t)").rearrange("(p f) -> p f", p=126),
                             rden[:]).then_inc(rden_out, 16)
                sp.wait_ge(rden_out, at.done(16))
                for j in range(4):
                    sp.dma_start(rden_all[r][32 * j:32 * j + D, :, :].rearrange("p g t -> p (g t)"),
                                 rden_dram[r, j].rearrange("g t -> (g t)").partition_broadcast(D)
                                 ).then_inc(rden_in[r], 16)

            def stack_loads(at):
                r = at.ring(2)
                sp.wait_ge(part3_ready, at.done())
                alone(sp, sp_passed)
                if at.past(2):
                    sp.wait_ge(stack_in[at.back(2).ring(4)], at.back(2).uses(4, 160))
                alone(sp, sp_passed)
                sp.dma_start(qk_dram[r].rearrange("a (m p) t -> p (a m) t", p=128), parts[r][:]
                             ).then_inc(parts_out[r], 16)
                sp.wait_ge(parts_out[at.ring(2)], at.uses(2, 16))
                alone(sp, sp_passed)
                if at.past(4):
                    sp.wait_ge(key_made, at.back(4).done(HEADS))
                view = qk_dram[r].rearrange("a (h d) t -> a d h t", d=D)
                for t, (q_part, k_part) in enumerate(TERMS):
                    dst = stack[at.ring(4)][D * t:D * t + D, :, 0:S]
                    if q_part == k_part:
                        sp.dma_start(dst, view[q_part]).then_inc(stack_in[at.ring(4)], 16)
                    else:
                        sp.dma_start(dst[:, 0:HEADS, :], view[q_part][:, 0:HEADS, :]
                                     ).then_inc(stack_in[at.ring(4)], 16)
                        sp.dma_start(dst[:, HEADS:, :], view[k_part][:, HEADS:, :]
                                     ).then_inc(stack_in[at.ring(4)], 16)

            def h2_store(at):
                sp.wait_ge(taken["out2"], at.done())
                sp.wait_ge(taken["out01"], at.done())
                r = at.ring(2)
                dst = out[at.j] if at.loop is None else out[bass.ds(at.times(1), 1)].rearrange("b s c -> (b s) c")
                sp.dma_start(dst[0:PATCHES, :].rearrange("(g p) c -> p g c", p=GROUP), h2[r][:, 0:2, :]
                             ).then_inc(h2_out[r], 16)
                sp.dma_start(dst[PATCHES:S, :], h2[r][0:TEXT, 2, :]).then_inc(h2_out[r], 16)

            def weight_stores(at):
                sp.wait_ge(w_summed, at.done(2))
                for layer, flat in enumerate((w1_flat, w2_flat)):
                    sp.dma_start(flat[:, bass.ds(at.times(WCOLS), WCOLS)], w_sum[0][layer][:]
                                 ).then_inc(w_stored, 16)

            def body(i):
                if i.back(2).exists(IMAGES):
                    shift_rows(i.back(2), 1)
                if i.back(3).exists(IMAGES):
                    denominators(i.back(3))
                if i.loop is not None or 2 <= i.j + 1 < IMAGES:
                    image_loads(i.back(-1))
                if i.back(1).exists(IMAGES):
                    shift_rows(i.back(1), 0)
                if i.exists(IMAGES):
                    weight_stores(i)
                    if i.loop is not None or i.j + 1 < IMAGES:
                        weight_loads(i.back(-1))
                    stack_loads(i)
                if i.back(3).exists(IMAGES):
                    h2_store(i.back(3))
                if i.loop is not None or 2 <= i.j + 1 < IMAGES:
                    text_load(i.back(-1))

            iterations(sp, body)
            for r in range(2):
                sp.wait_ge(h2_out[r], 32 * IMAGES // 2)
                sp.wait_ge(rows_out[r], 96 * IMAGES // 2)
            sp.wait_ge(w_stored, 32 * IMAGES)

        @block.gpsimd
        def _(pool):
            filled = [0]

            def fill(dst, value):
                nc.gpsimd.memset(dst, value).then_inc(pool_setup, 1)
                filled[0] += 1
                pool.wait_ge(pool_setup, filled[0])

            fill(w_out[:], 0.0)
            nc.gpsimd.memset(half_neg[:], -0.5).then_inc(weights_zeroed, 1)
            pool.wait_ge(weights_zeroed, 1)
            fill(half_pos[:], 0.5)
            for r in range(2):
                fill(rden_all[r][:], 0.0)
                fill(shift[r][:], 0.0)
            fill(empty[:], 0.0)
            fill(empty[:, :, C:C + 1], NO_TOKEN)
            assert filled[0] == FILLS
            pool.wait_ge(const_in, 16 * (CONSTS - 1))
            nc.gpsimd.tensor_scalar(token[:], place0[:], -float(S), None, ALU.add).then_inc(pool_setup, 1)
            pool.wait_ge(pool_setup, FILLS + 1)
            pool.wait_ge(gain_sq, 1)
            nc.gpsimd.tensor_tensor(gain[:, 1, :], gain[:, 0, :], half_pos[:], ALU.pow).then_inc(gain_root, 1)
            w_c = Counter(4)

            def weights(at):
                if at.past(1):
                    pool.wait_ge(w_stored, at.back(1).done(32))
                pool.wait_ge(w_loaded, at.done(96))
                alone(pool, pool_passed)
                w_c.start(at)
                for layer in range(2):
                    fast, slow, h_fast = w_in[0][3 * layer:3 * layer + 3]
                    total = w_sum[0][layer]
                    if layer == 1:
                        alone(pool, pool_passed)
                    nc.gpsimd.tensor_scalar(slow[:], slow[:], m_gate[:, layer:layer + 1], None, ALU.mult
                                            ).then_inc(w_chain, 1)
                    pool.wait_ge(w_chain, w_c.next())
                    nc.gpsimd.tensor_tensor(slow[:], slow[:], fast[:], ALU.add).then_inc(w_chain, 1)
                    pool.wait_ge(w_chain, w_c.next())
                    nc.gpsimd.tensor_tensor(total[:], slow[:], h_fast[:], ALU.add).then_inc(w_summed, 1)

            def power(at, chain, mv, ve, rs, ready, done):
                pool.wait_ge(ready, at.done())
                alone(pool, pool_passed)
                nc.gpsimd.tensor_scalar(ve[:], mv[:, :, 1], LN_EPS, None, ALU.add).then_inc(chain, 1)
                pool.wait_ge(chain, at.done())
                nc.gpsimd.tensor_tensor(rs[:], ve[:], half_neg[:], ALU.pow).then_inc(done, 1)

            def gate(at):
                g = gates[at.ring(2)]
                pool.wait_ge(gate_exp, at.done())
                alone(pool, pool_passed)
                nc.gpsimd.tensor_scalar(g[:, 2, :], g[:, 1, :], 1.0, None, ALU.add).then_inc(gate_sum, 1)
                pool.wait_ge(gate_inv, at.done())
                nc.gpsimd.tensor_tensor(g[:, 4, :], g[:, 1, :], g[:, 3, :], ALU.mult)
                nc.gpsimd.tensor_scalar(token[:], token[:], float(S), None, ALU.add).then_inc(gate_chain, 1)
                pool.wait_ge(gate_chain, at.done())
                pair = rows[at.ring(2)]
                alone(pool, pool_passed)
                nc.gpsimd.tensor_copy(pair[0][:, :, C], token[:])
                nc.gpsimd.tensor_copy(pair[1][:, :, C], token[:])
                nc.gpsimd.tensor_copy(pair[0][:, :, C + 1], g[:, 3, :])
                nc.gpsimd.tensor_copy(pair[1][:, :, C + 1], g[:, 4, :]).then_inc(row_copied, 1)

            def place(at):
                pool.wait_ge(row_copied, at.done(2))
                pool.wait_ge(pos_ready, at.done())
                alone(pool, pool_passed)
                for k in range(TOPK):
                    for g in range(GROUPS):
                        n = TEXT if g == 2 else GROUP
                        pool.indirect_dma_start(
                            rows_dram, bass.IndirectOffsetOnAxis(
                                ap=posi[at.ring(2)][0:n, k * GROUPS + g:k * GROUPS + g + 1], axis=0),
                            rows[at.ring(2)][k][0:n, g, :], None).then_inc(rows_out[at.ring(2)], 16)

            def body(i):
                four, three = i.back(4), i.back(3)
                if four.exists(IMAGES):
                    pool.wait_ge(norm2_ready, four.done())
                    nc.gpsimd.tensor_tensor(nrm[:, 1, :], nrm[:, 0, :], half_pos[:, 0:GROUPS], ALU.pow
                                            ).then_inc(norm_ready, 1)
                if i.exists(IMAGES):
                    weights(i)
                    power(i, rstd_chain, mean_var[0], var_eps[0], rstd[0], stats_ready, rstd_ready)
                if four.exists(IMAGES):
                    gate(four)
                if three.exists(IMAGES):
                    r = three.ring(2)
                    pool.wait_ge(rden_in[three.ring(2)], three.uses(2, 64))
                    if three.past(2):
                        pool.wait_ge(made["out2"], three.back(2).done())
                    nc.gpsimd.tensor_tensor(attn_t[r][:, :, 0:S], heads_t[r][:], rden_all[r][:], ALU.mult
                                            ).then_inc(attn_ready, 1)
                if i.exists(IMAGES):
                    pool.wait_ge(xn_ready, i.done())
                    h = resid[i.ring(4)]
                    for g in range(2):
                        nc.gpsimd.tensor_tensor(h[:, g, :], h[:, g, :], b_out[:], ALU.add)
                    nc.gpsimd.tensor_tensor(h[0:TEXT, 2, :], h[0:TEXT, 2, :], b_out[0:TEXT, :], ALU.add
                                            ).then_inc(resid_biased, 1)
                if four.exists(IMAGES):
                    place(four)
                if three.exists(IMAGES):
                    power(three, rstd2_chain, mean_var[1], var_eps[1], rstd[1], stats2_ready, rstd2_ready)
                    pool.wait_ge(xn2_ready, three.done())
                    alone(pool, pool_passed)
                    pair = rows[three.ring(2)]
                    nc.gpsimd.tensor_copy(pair[1][:, :, 0:C], pair[0][:, :, 0:C]).then_inc(row_copied, 1)

            iterations(pool, body)

        @block.vector
        def _(dve):
            step = Counter()

            for r in range(4):
                nc.vector.memset(resid[r][64:GROUP, 2, :], 0.0).then_inc(pads_zeroed, 1)
            for r in range(4):
                nc.vector.memset(stack[r][:, :, S:PAD], 0.0)
                nc.vector.memset(stack[r][SCORE_ROWS:, HEADS:, 0:S], 1.0)
                nc.vector.memset(values[r][:, :, :, D:2 * D], 1.0)
            for r in range(2):
                nc.vector.memset(attn_t[r][:, :, S:PAD], 0.0)
                nc.vector.memset(xn_t[r][HALF:HALF + 1, 1, :], 1.0)
            nc.vector.memset(ones[:], 1.0)
            nc.vector.memset(w_route[:, :, ROUTE - 1:ROUTE], 1.0 / C).then_inc(setup_chain, 1)
            dve.wait_ge(setup_chain, step.next())
            dve.wait_ge(const_in, 16 * (CONSTS - 1))
            nc.vector.tensor_tensor(emb_sq[:], emb_all[:], emb_all[:], ALU.mult).then_inc(setup_chain, 1)
            dve.wait_ge(setup_chain, step.next())
            nc.vector.tensor_reduce(gain[:, 0, :], emb_sq[:], AX, ALU.add).then_inc(gain_sq, 1)
            dve.wait_ge(gain_root, 1)
            nc.vector.tensor_scalar(gain[:, 2, :], gain[:, 1, :], 0.02, 0.02, ALU.mult, ALU.add
                                    ).then_inc(setup_chain, 1)
            dve.wait_ge(setup_chain, step.next())
            nc.vector.tensor_scalar(gain[:, 3, :], gain[:, 1, :], 1e-12, None, ALU.max).then_inc(setup_chain, 1)
            dve.wait_ge(setup_chain, step.next())
            nc.vector.reciprocal(gain[:, 3, :], gain[:, 3, :]).then_inc(setup_chain, 1)
            dve.wait_ge(setup_chain, step.next())
            nc.vector.tensor_tensor(emb_t[:], emb_t[:], gain[0:PROBE, 3, :], ALU.mult).then_inc(emb_ready, 1)
            nc.vector.tensor_tensor(bias8[:], energy[:], fatigue[:], ALU.subtract).then_inc(setup_chain, 1)
            dve.wait_ge(setup_chain, step.next())
            nc.vector.tensor_scalar(bias8[:], bias8[:], 0.1, None, ALU.mult).then_inc(setup_chain, 1)
            dve.wait_ge(setup_chain, step.next())
            dve.wait_ge(align_made, 1)
            lo = EXPERTS + PROBE
            nc.vector.tensor_copy(w_route[:, 0, lo:lo + EXPERTS], ps_mix[0:HALF, 0:EXPERTS])
            nc.vector.tensor_copy(w_route[:, 1, lo:lo + EXPERTS], ps_mix[0:HALF, EXPERTS:2 * EXPERTS]
                                  ).then_inc(setup_done, 1)

            shift_c = [Counter(3) for _ in range(2)]
            route_c = Counter(19)
            place_c = Counter(3)

            def tok(at, g):
                dve.wait_ge(made[f"tok{g}"], at.done())
                if g == 0:
                    if at.past(4):
                        dve.wait_ge(taken["out2"], at.back(4).done())
                nc.vector.tensor_tensor(resid[at.ring(4)][:, g, :], ps_mix[0:GROUP, 0:C], b_tok[:], ALU.add
                                        ).then_inc(taken[f"tok{g}"], 1)

            def layer_stats(at, h, k, chain, ready, groups, finish):
                for g in groups:
                    nc.vector.bn_stats(stats[k][:, g, :], h[:, g, :]).then_inc(chain, 1)
                if finish:
                    dve.wait_ge(chain, at.done(3))
                    alone(dve, dve_passed)
                    for g in range(GROUPS):
                        last = nc.vector.bn_aggr(mean_var[k][:, g, :], stats[k][:, g, :])
                    last.then_inc(ready, 1)

            def normalise(at, h, k, dst, rstd_done, done):
                dve.wait_ge(rstd_done, at.done())
                for g in range(GROUPS):
                    last = nc.vector.tensor_scalar(dst[:, g, 0:C], h[:, g, :], mean_var[k][:, g, 0:1],
                                                   rstd[k][:, g:g + 1], ALU.subtract, ALU.mult)
                last.then_inc(done, 1)

            def remainder(at, m):
                dve.wait_ge(part1_ready, at.done(3, m + 1))
                if m == 0:
                    if at.past(1):
                        dve.wait_ge(part3_ready, at.back(1).done())
                nc.vector.tensor_tensor(rest[:, m, :], ps_mix[:, 0:S], parts[at.ring(2)][:, m, :], ALU.subtract
                                        ).then_inc(taken[f"qk{m}"], 1)

            def third_part(at):
                dve.wait_ge(part2_ready, at.done())
                p = parts[at.ring(2)]
                nc.vector.tensor_tensor(p[:, 6:9, :], rest[:], p[:, 3:6, :], ALU.subtract).then_inc(part3_ready, 1)

            def maximum(at, h):
                dve.wait_ge(max_made, at.done(HEADS, h + 1))
                nc.vector.tensor_reduce(maxima[:, :, h], ps_max[0:GROUP, :, 0:S], AX, ALU.max).then_inc(max_taken, 1)

            def shifts(at, half):
                dve.wait_ge(max_taken, at.done(HEADS, 6 * (half + 1)))
                if at.past(1):
                    dve.wait_ge(made[f"shift{half}"], at.back(1).done())
                c, m = shift_c[half], maxima[:, :, 6 * half:6 * half + 6]
                s, r = shift[half], shift_rest[half]
                c.start(at)
                nc.vector.tensor_scalar(s[:, :, 0:6], m, -1.0, None, ALU.mult).then_inc(shift_chain[half], 1)
                dve.wait_ge(shift_chain[half], c.next())
                nc.vector.scalar_tensor_tensor(r[:], m, -1.0, s[:, :, 0:6], ALU.mult, ALU.subtract
                                               ).then_inc(shift_chain[half], 1)
                dve.wait_ge(shift_chain[half], c.next())
                nc.vector.tensor_copy(s[:, :, 6:12], r[:]).then_inc(shift_chain[half], 1)
                dve.wait_ge(shift_chain[half], c.next())
                nc.vector.tensor_tensor(s[:, :, 12:18], r[:], s[:, :, 6:12], ALU.subtract
                                        ).then_inc(shift_ready[half], 1)

            def invert(at):
                dve.wait_ge(den_in, at.done(16))
                if at.past(1):
                    dve.wait_ge(rden_out, at.back(1).done(16))
                nc.vector.reciprocal(rden[:], den[:]).then_inc(den_inverse, 1)

            def attention_out(at, name, groups):
                dve.wait_ge(made[name], at.done())
                if name == "out01":
                    dve.wait_ge(resid_biased, at.done())
                    if at.past(2):
                        dve.wait_ge(h2_out[at.back(2).ring(2)], at.back(2).uses(2, 32))
                n = len(groups)
                lo, hi = groups[0], groups[-1] + 1
                nc.vector.tensor_tensor(h2[at.ring(2)][:, lo:hi, :],
                                        ps_mix[0:GROUP, 0:n * C].rearrange("p (g c) -> p g c", g=n),
                                        resid[at.ring(4)][:, lo:hi, :], ALU.add).then_inc(taken[name], 1)

            b3 = [GROUP, GROUPS, EXPERTS]

            def over_experts(v):
                return v[:, :, None].broadcast_to(b3)

            def over_groups(v):
                return v[:, None, :].broadcast_to(b3)

            def route_a(at):
                dve.wait_ge(made["route"], at.done())
                nc.vector.tensor_copy(routed[:], ps_mix[0:GROUP, 0:GROUPS * ROUTE].rearrange(
                    "p (g n) -> p g n", g=GROUPS)).then_inc(taken["route"], 1)
                dve.wait_ge(taken["route"], at.done())
                c = route_c
                c.start(at)
                probe = routed[:, :, EXPERTS:lo]
                nc.vector.tensor_tensor(sq[:], probe, probe, ALU.mult).then_inc(route_chain, 1)
                dve.wait_ge(route_chain, c.next())
                nc.vector.tensor_reduce(nrm[:, 0, :], sq[:], AX, ALU.add).then_inc(norm2_ready, 1)

            def route_b(at):
                c = route_c
                c.start(at, 1)
                dve.wait_ge(norm_ready, at.done())
                nc.vector.tensor_scalar(nrm[:, 2, :], nrm[:, 1, :], 1e-12, None, ALU.max).then_inc(route_chain, 1)
                dve.wait_ge(route_chain, c.next())
                nc.vector.reciprocal(nrm[:, 3, :], nrm[:, 2, :]).then_inc(route_chain, 1)
                dve.wait_ge(route_chain, c.next())
                nc.vector.tensor_tensor(align[:], routed[:, :, lo:lo + EXPERTS], over_experts(nrm[:, 3, :]),
                                        ALU.mult).then_inc(route_chain, 1)
                dve.wait_ge(route_chain, c.next())
                nc.vector.tensor_tensor(tmp8[:], over_experts(routed[:, :, ROUTE - 1]),
                                        over_groups(gain[:, 2, :]), ALU.mult).then_inc(route_chain, 1)
                dve.wait_ge(route_chain, c.next())
                nc.vector.tensor_tensor(logit[:], routed[:, :, 0:EXPERTS], tmp8[:], ALU.add).then_inc(route_chain, 1)
                dve.wait_ge(route_chain, c.next())
                nc.vector.scalar_tensor_tensor(logit[:], align[:], 0.02, logit[:], ALU.mult, ALU.add
                                               ).then_inc(route_chain, 1)
                dve.wait_ge(route_chain, c.next())
                nc.vector.tensor_tensor(logit[:], logit[:], over_groups(bias8[:]), ALU.add).then_inc(route_chain, 1)
                dve.wait_ge(route_chain, c.next())
                choose(c, logit, 0)

            def choose(c, scores, k):
                nc.vector.tensor_reduce(top[:, k, :], scores[:], AX, ALU.max).then_inc(route_chain, 1)
                dve.wait_ge(route_chain, c.next())
                nc.vector.tensor_tensor(tmp8[:], scores[:], over_experts(top[:, k, :]), ALU.is_equal
                                        ).then_inc(route_chain, 1)
                dve.wait_ge(route_chain, c.next())
                nc.vector.tensor_tensor(tmp8[:], tmp8[:], over_groups(ramp[:]), ALU.mult).then_inc(route_chain, 1)
                dve.wait_ge(route_chain, c.next())
                nc.vector.tensor_reduce(pick[:, k, :], tmp8[:], AX, ALU.min).then_inc(route_chain, 1)
                dve.wait_ge(route_chain, c.next())
                nc.vector.tensor_tensor(hot[:, k, :].rearrange("p (g e) -> p g e", g=GROUPS),
                                        over_groups(ramp[:]), over_experts(pick[:, k, :]), ALU.is_equal
                                                 ).then_inc(route_chain, 1)
                dve.wait_ge(route_chain, c.next())

            def route_c2(at):
                c = route_c
                c.start(at, 13)
                hot0 = hot[:, 0, :].rearrange("p (g e) -> p g e", g=GROUPS)
                hot1 = hot[:, 1, :].rearrange("p (g e) -> p g e", g=GROUPS)
                nc.vector.scalar_tensor_tensor(masked[:], hot0, -3e38, logit[:], ALU.mult, ALU.add
                                               ).then_inc(route_chain, 1)
                dve.wait_ge(route_chain, c.next())
                choose(c, masked, 1)
                if at.past(1):
                    dve.wait_ge(made["rank"], at.back(1).done())
                nc.vector.tensor_tensor(chosen[:], hot0, hot1, ALU.add).then_inc(chosen_ready, 1)
                if at.past(2):
                    dve.wait_ge(rows_out[at.back(2).ring(2)], at.back(2).uses(2, 96))
                nc.vector.tensor_tensor(gates[at.ring(2)][:, 0, :], top[:, 1, :], top[:, 0, :], ALU.subtract
                                        ).then_inc(top_gap, 1)

            def place(at):
                c = place_c
                c.start(at)
                dve.wait_ge(made["rank"], at.done())
                ge = GROUPS * EXPERTS
                nc.vector.tensor_tensor(pos[:].rearrange("p (g e) -> p g e", g=GROUPS),
                                        ps_mix[0:GROUP, 0:ge].rearrange("p (g e) -> p g e", g=GROUPS),
                                        over_groups(base[:]), ALU.add).then_inc(place_chain, 1)
                dve.wait_ge(place_chain, c.next())
                nc.vector.tensor_tensor(base[:], base[:], ps_mix[0:GROUP, ge:ge + EXPERTS], ALU.add
                                        ).then_inc(taken["rank"], 1)
                nc.vector.tensor_tensor(pos2[:], hot[:], pos[:, None, :].broadcast_to([GROUP, 2, ge]), ALU.mult
                                        ).then_inc(place_chain, 1)
                dve.wait_ge(place_chain, c.next())
                nc.vector.tensor_reduce(posf[:], pos2[:].rearrange("p k (g e) -> p (k g) e", g=GROUPS),
                                        AX, ALU.add).then_inc(place_chain, 1)
                dve.wait_ge(place_chain, c.next())
                nc.vector.tensor_copy(posi[at.ring(2)][:], posf[:]).then_inc(pos_ready, 1)

            def gate_inverse(at):
                dve.wait_ge(gate_sum, at.done())
                g = gates[at.ring(2)]
                nc.vector.reciprocal(g[:, 3, :], g[:, 2, :]).then_inc(gate_inv, 1)

            def body(i):
                one, two, three, four = (i.back(k) for k in (1, 2, 3, 4))
                here = i.exists(IMAGES)
                for slot in range(HEADS):
                    if slot == 0:
                        if two.exists(IMAGES):
                            shifts(two, 1)
                        if here:
                            tok(i, 0)
                        if four.exists(IMAGES):
                            route_b(four)
                    if slot == 1:
                        if here:
                            tok(i, 1)
                        if four.exists(IMAGES):
                            route_c2(four)
                        if here:
                            dve.wait_ge(taken["tok1"], i.done())
                            dve.wait_ge(text_in[i.ring(2)], i.uses(2, 16))
                            if i.past(1):
                                dve.wait_ge(rstd_ready, i.back(1).done())
                            layer_stats(i, resid[i.ring(4)], 0, stats_chain, stats_ready, range(GROUPS), False)
                    if slot == 2:
                        if four.exists(IMAGES):
                            place(four)
                        if here:
                            layer_stats(i, None, 0, stats_chain, stats_ready, (), True)
                    if slot == 3:
                        if four.exists(IMAGES):
                            gate_inverse(four)
                        if here:
                            if i.past(1):
                                dve.wait_ge(made["xt1"], i.back(1).done())
                            normalise(i, resid[i.ring(4)], 0, xn, rstd_ready, xn_ready)
                    if slot == 4 and three.exists(IMAGES):
                        invert(three)
                    if slot == 5 and here:
                        remainder(i, 0)
                        remainder(i, 1)
                    if slot == 6:
                        if here:
                            remainder(i, 2)
                        if one.exists(IMAGES):
                            shifts(one, 0)
                    if slot == 7:
                        if here:
                            third_part(i)
                        if three.exists(IMAGES):
                            attention_out(three, "out01", (0, 1))
                    if slot == 8 and three.exists(IMAGES):
                        attention_out(three, "out2", (2,))
                        dve.wait_ge(taken["out2"], three.done())
                        if three.past(1):
                            dve.wait_ge(rstd2_ready, three.back(1).done())
                        layer_stats(three, h2[three.ring(2)], 1, stats2_chain, stats2_ready, range(GROUPS), True)
                    if slot == 9 and three.exists(IMAGES):
                        if three.past(2):
                            dve.wait_ge(rows_out[three.back(2).ring(2)], three.back(2).uses(2, 96))
                        normalise(three, h2[three.ring(2)], 1, rows[three.ring(2)][0], rstd2_ready, xn2_ready)
                    if slot == 11 and three.exists(IMAGES):
                        route_a(three)
                    if one.exists(IMAGES):
                        maximum(one, slot)

            iterations(dve, body)

        @block.scalar
        def _(act):
            def take(at, name, dst, src, sem_done=None):
                act.wait_ge(made[name], at.done())
                nc.scalar.activation(dst, src, ACT.Copy).then_inc(taken[name] if sem_done is None else sem_done, 1)

            def body(i):
                one, two, three, four = (i.back(k) for k in (1, 2, 3, 4))
                here = i.exists(IMAGES)
                r = i.ring(2)

                def shift_take(at, half):
                    if at.past(1):
                        act.wait_ge(shift_in[half], at.back(1).done(48))
                    take(at, f"shift{half}", shift_t[half][:], ps_mix_b[0:18, 0:S])

                def heads_take(at, g):
                    act.wait_ge(head_made, at.done(GROUPS, g + 1))
                    if g == 0:
                        if at.past(2):
                            act.wait_ge(attn_ready, at.back(2).done())
                    nc.scalar.activation(heads_t[at.ring(2)][:, g, :], ps_head[:, 0:S], ACT.Copy
                                         ).then_inc(head_taken, 1)

                for slot in range(HEADS):
                    if slot == 1 and two.exists(IMAGES):
                        shift_take(two, 1)
                    if slot == 2 and four.exists(IMAGES):
                        act.wait_ge(top_gap, four.done())
                        g = gates[four.ring(2)]
                        nc.scalar.activation(g[:, 1, :], g[:, 0, :], ACT.Exp).then_inc(gate_exp, 1)
                    if slot == 4 and here:
                        if i.past(2):
                            act.wait_ge(made["v2"], i.back(2).done())
                        for k in range(2):
                            take(i, f"xt{k}", xn_t[r][0:HALF, k, :], ps_mix[0:HALF, 0:PAD])
                    if slot in (5, 6) and here:
                        if slot == 5:
                            if i.past(2):
                                act.wait_ge(parts_out[i.back(2).ring(2)], i.back(2).uses(2, 16))
                        for m in (0, 1) if slot == 5 else (2,):
                            take(i, f"qk{m}", parts[r][:, m, :], ps_mix[:, 0:S], part1_ready)
                    if slot == 6 and one.exists(IMAGES):
                        shift_take(one, 0)
                    if slot == 7 and here:
                        act.wait_ge(taken["qk2"], i.done())
                        nc.scalar.activation(parts[r][:, 3:6, :], rest[:], ACT.Copy).then_inc(part2_ready, 1)
                        if i.past(4):
                            act.wait_ge(head_made, i.back(4).done(GROUPS))
                        take(i, "v01", values[i.ring(4)][:, 0:2, :, 0:D],
                             ps_mix[0:GROUP, 0:2 * C].rearrange("p (g h d) -> p g h d", g=2, h=HEADS))
                    if slot == 8 and here:
                        take(i, "v2", values[i.ring(4)][:, 2, :, 0:D],
                             ps_mix[0:GROUP, 0:C].rearrange("p (h d) -> p h d", h=HEADS))
                    if slot == 10 and three.exists(IMAGES):
                        act.wait_ge(made["route"], four.done())
                        for k in range(2):
                            take(three, f"x2t{k}", xn2_t[:, k, :], ps_mix[0:HALF, 0:PAD])
                    if two.exists(IMAGES):
                        act.wait_ge(key_made, two.done(HEADS, slot + 1))
                        group = slot // 4
                        if positive(count := two.done(GROUPS, group - 1)):
                            act.wait_ge(head_made, count)
                        buf = probs[(4 * two.ring(2) + slot) % 8]
                        nc.scalar.activation(buf[:], ps_key[0:GROUP, :, 0:S], ACT.Exp, scale=D ** -0.5
                                             ).then_inc(exp_done, 1)
                        if slot == 5:
                            heads_take(two, 0)
                        if slot == 9:
                            heads_take(two, 1)
                    if slot == 1 and three.exists(IMAGES):
                        heads_take(three, 2)

            iterations(act, body)

        @block.tensor
        def _(pe):
            pe.wait_ge(emb_ready, 1)
            for k in range(2):
                last = nc.tensor.matmul(ps_mix[0:HALF, k * EXPERTS:(k + 1) * EXPERTS],
                                        probe_w[:, k * HALF:(k + 1) * HALF], emb_t[:], start=True, stop=True)
            last.then_inc(align_made, 1)
            pe.wait_ge(setup_done, 1)

            def transposes(src, at, name):
                for g in range(GROUPS):
                    last = nc.tensor.transpose(ps_mix[0:HALF, g * GROUP:(g + 1) * GROUP], src(g),
                                               ident[0:GROUP, 0:GROUP])
                last.then_inc(made[name], 1)

            def product(at, name):
                r = at.ring(2)
                if name in ("tok0", "tok1"):
                    g = int(name[3])
                    if g == 0:
                        pe.wait_ge(patches_in[at.ring(2)], at.uses(2, 16))
                    n = PIXELS // 128
                    for k in range(n):
                        last = nc.tensor.matmul(ps_mix[0:GROUP, 0:C], patches[r][:, k, g * GROUP:(g + 1) * GROUP],
                                                w_tok[:, k, :], start=(k == 0), stop=(k == n - 1))
                elif name in ("xt0", "xt1"):
                    k = int(name[2])
                    pe.wait_ge(xn_ready, at.done())
                    return transposes(lambda g: xn[:, g, k * HALF:(k + 1) * HALF], at, name)
                elif name in ("x2t0", "x2t1"):
                    k = int(name[3])
                    pe.wait_ge(xn2_ready, at.done())
                    return transposes(lambda g: rows[r][0][:, g, k * HALF:(k + 1) * HALF], at, name)
                elif name in ("qk0", "qk1", "qk2"):
                    m = int(name[2])
                    pe.wait_ge(taken["xt1"], at.done())
                    for k in range(2):
                        last = nc.tensor.matmul(ps_mix[:, 0:S], w_qkv[0:HALF + k, k, m * 128:(m + 1) * 128],
                                                xn_t[r][0:HALF + k, k, 0:S], start=(k == 0), stop=(k == 1))
                elif name in ("v01", "v2"):
                    groups = (0, 1) if name == "v01" else (2,)
                    for n, g in enumerate(groups):
                        for k in range(2):
                            last = nc.tensor.matmul(ps_mix[0:GROUP, n * C:(n + 1) * C],
                                                    xn_t[r][0:HALF + k, k, g * GROUP:(g + 1) * GROUP],
                                                    w_qkv[0:HALF + k, k, 2 * C:3 * C], start=(k == 0), stop=(k == 1))
                elif name in ("shift0", "shift1"):
                    half = int(name[5])
                    pe.wait_ge(shift_ready[half], at.done())
                    for g in range(GROUPS):
                        last = nc.tensor.transpose(ps_mix_b[:, g * GROUP:(g + 1) * GROUP], shift[half][:, g, :],
                                                   identb[0:GROUP, 0:GROUP])
                elif name in ("out01", "out2"):
                    groups = (0, 1) if name == "out01" else (2,)
                    pe.wait_ge(attn_ready, at.done())
                    for n, g in enumerate(groups):
                        for k in range(GROUPS):
                            last = nc.tensor.matmul(ps_mix[0:GROUP, n * C:(n + 1) * C],
                                                    attn_t[r][:, k, g * GROUP:(g + 1) * GROUP], w_out[:, k, :],
                                                    start=(k == 0), stop=(k == GROUPS - 1))
                elif name == "route":
                    pe.wait_ge(taken["x2t1"], at.done())
                    for g in range(GROUPS):
                        for k in range(2):
                            last = nc.tensor.matmul(ps_mix[0:GROUP, g * ROUTE:(g + 1) * ROUTE],
                                                    xn2_t[:, k, g * GROUP:(g + 1) * GROUP], w_route[:, k, :],
                                                    start=(k == 0), stop=(k == 1))
                elif name == "rank":
                    pe.wait_ge(chosen_ready, at.done())
                    rows_of = (GROUP, GROUP, TEXT)
                    for g in range(GROUPS):
                        dst = ps_mix[0:GROUP, g * EXPERTS:(g + 1) * EXPERTS]
                        n = rows_of[g]
                        nc.tensor.matmul(dst, before[0:n, :], chosen[0:n, g, :], start=True, stop=(g == 0))
                        for e in range(g):
                            nc.tensor.matmul(dst, ones[:], chosen[:, e, :], start=False, stop=(e == g - 1))
                    for g in range(GROUPS):
                        last = nc.tensor.matmul(ps_mix[0:GROUP, GROUPS * EXPERTS:(GROUPS + 1) * EXPERTS],
                                                ones[0:rows_of[g], :], chosen[0:rows_of[g], g, :],
                                                start=(g == 0), stop=(g == GROUPS - 1))
                last.then_inc(made[name], 1)

            def product_before(i, n):
                while True:
                    n -= 1
                    if n < 0:
                        n, i = len(STEPS) - 1, i.back(1)
                        if i.loop is None and i.j < 0:
                            return None, None
                    name, at = STEPS[n][2], i.back(STEPS[n][3])
                    if at.exists(IMAGES):
                        return name, at

            def heads(at, g):
                pe.wait_ge(exp_done, at.done(HEADS, 4 * g + 4))
                if g == 0:
                    pe.wait_ge(taken["v2"], at.done())
                if positive(count := at.done(GROUPS, g)):
                    pe.wait_ge(head_taken, count)
                for k in range(GROUPS):
                    n = TEXT if k == 2 else GROUP
                    for j in range(4):
                        h = 4 * g + j
                        last = nc.tensor.matmul(ps_head[32 * j:32 * j + 32, 0:S], values[at.ring(4)][0:n, k, h, :],
                                                probs[(4 * at.ring(2) + h) % 8][0:n, k, :],
                                                start=(k == 0), stop=(k == GROUPS - 1), skip_group_check=True)
                last.then_inc(head_made, 1)

            def body(i):
                one, two, three = i.back(1), i.back(2), i.back(3)
                for slot in range(HEADS):
                    for part in range(2):
                        for n, (s, p, name, lag) in enumerate(STEPS):
                            if (s, p) == (slot, part) and i.back(lag).exists(IMAGES):
                                previous, image = product_before(i, n)
                                if previous:
                                    pe.wait_ge(taken[previous], image.done())
                                product(i.back(lag), name)
                        if part == 0 and one.exists(IMAGES):
                            if slot == 0:
                                pe.wait_ge(stack_in[one.ring(4)], one.uses(4, 160))
                            if positive(count := one.done(HEADS, slot)):
                                pe.wait_ge(max_taken, count)
                            st = stack[one.ring(4)]
                            for g in range(GROUPS):
                                last = nc.tensor.matmul(ps_max[0:GROUP, g, 0:S],
                                                        st[0:SCORE_ROWS, slot, g * GROUP:(g + 1) * GROUP],
                                                        st[0:SCORE_ROWS, HEADS + slot, 0:S], start=True, stop=True)
                            last.then_inc(max_made, 1)
                        if part == 1 and two.exists(IMAGES):
                            if slot in (0, 6):
                                pe.wait_ge(shift_in[slot // 6], two.done(48))
                            if positive(count := two.done(HEADS, slot)):
                                pe.wait_ge(exp_done, count)
                            st = stack[two.ring(4)]
                            for g in range(GROUPS):
                                last = nc.tensor.matmul(ps_key[0:GROUP, g, 0:S],
                                                        st[:, HEADS + slot, g * GROUP:(g + 1) * GROUP],
                                                        st[:, slot, 0:S], start=True, stop=True)
                            last.then_inc(key_made, 1)
                    if slot == 5 and two.exists(IMAGES):
                        heads(two, 0)
                    if slot == 9 and two.exists(IMAGES):
                        heads(two, 1)
                    if slot == 1 and three.exists(IMAGES):
                        heads(three, 2)

            iterations(pe, body)
        phase1.close()

        ends = kept("ends", [GROUP, EXPERTS], I32)
        many = kept("many", [GROUP, EXPERTS, MAXT])
        plan = kept("plan", [GROUP, 8, EXPERTS])
        cell = kept("cell", [GROUP, 6])
        table = kept("table", [GROUP, 2], I32)
        table_row = kept("table_row", [1, 2 * TILES], I32)
        w1 = [kept(f"w1_{r}", [HALF, 2, HID]) for r in range(2)]
        w2 = [kept(f"w2_{r}", [128, HCH, C]) for r in range(2)]
        b1 = [kept(f"b1_{r}", [128, HCH]) for r in range(2)]
        b2 = [kept(f"b2_{r}", [128, C]) for r in range(2)]
        x_row = [kept(f"x_row{r}", [128, 2, ROW]) for r in range(4)]
        x_t = [kept(f"x_t{r}", [HALF, 2, TILE]) for r in range(2)]
        relu = [kept(f"relu{r}", [128, TILE]) for r in range(4)]
        hidden = [kept(f"hidden{r}", [128, HCH, TILE]) for r in range(2)]
        y_bias = kept("y_bias", [128, 2, C])
        y_gated = [kept(f"y_gated{r}", [128, 2, C]) for r in range(2)]
        token_no = [kept(f"token_no{r}", [128, 2], I32) for r in range(2)]
        ps_xt = ps[0:HALF, 0, :].rearrange("p (k t) -> p k t", k=2)
        ps_hid = [ps[:, 1 + n, 0:TILE] for n in range(4)]
        ps_y = ps[:, 5:7, 0:C]

        w1_in, w2_in, b1_in, b2_in = (sems(n, 2) for n in ("w1_in", "w2_in", "b1_in", "b2_in"))
        x_in = sems("x_in", 4)
        xt_made, xt_taken = sem("xt_made"), sem("xt_taken")
        hid_made, relu_done, hid_ready = sem("hid_made"), sem("relu_done"), sem("hid_ready")
        y_made, y_taken, y_ready = sem("y_made"), sem("y_taken"), sem("y_ready")
        scattered = sem("scattered")

        block2 = ctx.enter_context(nc.Block())

        @block2.sync
        def _(sp):
            sp.wait_ge(ends_ready, 1)
            for e in range(EXPERTS):
                row = sp.value_load(ends[0:1, e:e + 1], min_val=e * CAP, max_val=e * CAP + N)
                sp.dma_start(rows_dram[bass.ds(row, TILE), :].rearrange("(p a) f -> p a f", a=2), empty[:]
                             ).then_inc(ends_out, 16)
            sp.dma_start(rows_dram[ZERO_ROW:ZERO_ROW + TILE, :].rearrange("(p a) f -> p a f", a=2), empty[:]
                         ).then_inc(ends_out, 16)
            sp.wait_ge(table_ready, 1)
            sp.dma_start(table_dram, table[0:TILES, :]).then_inc(table_out, 16)
            sp.wait_ge(table_out, 16)
            sp.dma_start(table_row[:], table_dram.rearrange("k n -> (k n)")[None, :]).then_inc(table_in, 16)
            sp.wait_ge(table_in, 16)
            sp.wait_ge(ends_out, 16 * (EXPERTS + 1))

            def body(at):
                if not at.exists(TILES):
                    return
                r, two = at.ring(2), at.back(2)
                e = sp.value_load(table_row[0:1, bass.ds(at.times(2), 1)], min_val=0, max_val=EXPERTS - 1)
                row = sp.value_load(table_row[0:1, bass.ds(at.times(2, 1), 1)], min_val=0, max_val=ZERO_ROW)
                if at.past(4):
                    sp.wait_ge(y_ready, at.back(4).done())
                alone(sp, sp_passed)
                sp.dma_start(x_row[at.ring(4)][:], rows_dram[bass.ds(row, TILE), :].rearrange("(p a) f -> p a f", a=2)
                             ).then_inc(x_in[at.ring(4)], 16)
                if at.past(2):
                    sp.wait_ge(relu_done, two.done(HCH))
                alone(sp, sp_passed)
                sp.dma_start(w1[r][:], w1_dram[bass.ds(e, 1)].rearrange("o (k p) h -> p (o k) h", p=HALF)
                             ).then_inc(w1_in[r], 16)
                sp.dma_start(b1[r][:], a["b1_t"][bass.ds(e, 1)].rearrange("o p j -> (o p) j")).then_inc(b1_in[r], 16)
                if at.past(2):
                    sp.wait_ge(y_taken, two.done())
                alone(sp, sp_passed)
                sp.dma_start(w2[r][:], w2_dram[bass.ds(e, 1)].rearrange("o (j p) c -> p (o j) c", p=128)
                             ).then_inc(w2_in[r], 16)
                sp.dma_start(b2[r][:], a["L0_ffn_b2"][bass.ds(e, 1)].rearrange("o c -> (o c)").partition_broadcast(128)
                             ).then_inc(b2_in[r], 16)

            tiles(sp, body)

        @block2.vector
        def _(dve):
            step = Counter()

            nc.vector.tensor_copy(ends[:], base[:]).then_inc(ends_ready, 1)
            t = slice(0, TILES)
            count, tiles_of, upto, behind, mine, first, part, ones8 = (plan[t, n, :] for n in range(8))
            nc.vector.memset(ones8, 1.0).then_inc(plan_chain, 1)
            dve.wait_ge(plan_chain, step.next())
            nc.vector.tensor_tensor(count, base[t, :], region[t, :], ALU.subtract).then_inc(plan_chain, 1)
            dve.wait_ge(plan_chain, step.next())
            shape = [TILES, EXPERTS, MAXT]
            nc.vector.tensor_tensor(many[t], count[:, :, None].broadcast_to(shape),
                                         steps256[t, None, :].broadcast_to(shape), ALU.is_gt).then_inc(plan_chain, 1)
            dve.wait_ge(plan_chain, step.next())
            nc.vector.tensor_reduce(tiles_of, many[t], AX, ALU.add).then_inc(plan_chain, 1)
            dve.wait_ge(plan_chain, step.next())
            nc.vector.tensor_tensor_scan(upto, ones8, tiles_of, 0.0, ALU.mult, ALU.add).then_inc(plan_chain, 1)
            dve.wait_ge(plan_chain, step.next())
            nc.vector.tensor_scalar(behind, upto, tile_no[t, 0:1], None, ALU.is_le).then_inc(plan_chain, 1)
            dve.wait_ge(plan_chain, step.next())
            nc.vector.tensor_reduce(cell[t, 0:1], behind, AX, ALU.add).then_inc(plan_chain, 1)
            dve.wait_ge(plan_chain, step.next())
            nc.vector.tensor_scalar(mine, ramp[t, :], float(EXPERTS), cell[t, 0:1], ALU.add, ALU.is_equal
                                    ).then_inc(plan_chain, 1)
            dve.wait_ge(plan_chain, step.next())
            nc.vector.tensor_tensor(first, tiles_of, upto, ALU.subtract).then_inc(plan_chain, 1)
            dve.wait_ge(plan_chain, step.next())
            nc.vector.scalar_tensor_tensor(first, first, float(TILE), region[t, :], ALU.mult, ALU.add
                                           ).then_inc(plan_chain, 1)
            dve.wait_ge(plan_chain, step.next())
            nc.vector.tensor_tensor(part, mine, first, ALU.mult).then_inc(plan_chain, 1)
            dve.wait_ge(plan_chain, step.next())
            nc.vector.tensor_reduce(cell[t, 1:2], part, AX, ALU.add).then_inc(plan_chain, 1)
            dve.wait_ge(plan_chain, step.next())
            nc.vector.tensor_reduce(cell[t, 2:3], mine, AX, ALU.add).then_inc(plan_chain, 1)
            dve.wait_ge(plan_chain, step.next())
            nc.vector.tensor_tensor(part, mine, ramp[t, :], ALU.mult).then_inc(plan_chain, 1)
            dve.wait_ge(plan_chain, step.next())
            nc.vector.tensor_reduce(cell[t, 3:4], part, AX, ALU.add).then_inc(plan_chain, 1)
            dve.wait_ge(plan_chain, step.next())
            nc.vector.scalar_tensor_tensor(cell[t, 4:5], cell[t, 2:3], tile_no[t, 1:2], cell[t, 1:2],
                                                ALU.mult, ALU.add).then_inc(plan_chain, 1)
            dve.wait_ge(plan_chain, step.next())
            nc.vector.tensor_scalar(table[t, 1:2], cell[t, 4:5], float(ZERO_ROW), None, ALU.add
                                    ).then_inc(plan_chain, 1)
            dve.wait_ge(plan_chain, step.next())
            nc.vector.scalar_tensor_tensor(table[t, 0:1], cell[t, 2:3], float(EXPERTS), cell[t, 3:4],
                                           ALU.mult, ALU.add).then_inc(table_ready, 1)

            def square(at):
                for j in range(HCH):
                    dve.wait_ge(relu_done, at.done(HCH, j + 1))
                    if j == 0:
                        if at.past(2):
                            dve.wait_ge(y_made, at.back(2).done())
                    rl = relu[(2 * at.ring(2) + j) % 4]
                    nc.vector.tensor_tensor(hidden[at.ring(2)][:, j, :], rl[:], rl[:], ALU.mult
                                            ).then_inc(hid_ready, 1)

            def output(at):
                r = at.ring(2)
                dve.wait_ge(b2_in[at.ring(2)], at.uses(2, 16))
                dve.wait_ge(y_made, at.done())
                if at.past(1):
                    dve.wait_ge(y_ready, at.back(1).done())
                nc.vector.tensor_tensor(y_bias[:], ps_y, b2[r][:, None, :].broadcast_to([128, 2, C]), ALU.add
                                        ).then_inc(y_taken, 1)
                dve.wait_ge(y_taken, at.done())
                if at.past(2):
                    dve.wait_ge(scattered, at.back(2).done(32))
                nc.vector.tensor_copy(token_no[r][:], x_row[at.ring(4)][:, :, C])
                for half in range(2):
                    last = nc.vector.tensor_scalar(y_gated[r][:, half, :], y_bias[:, half, :],
                                                   x_row[at.ring(4)][:, half, C + 1:C + 2], None, ALU.mult)
                last.then_inc(y_ready, 1)

            def body(at):
                if at.exists(TILES):
                    square(at)
                if at.back(1).exists(TILES):
                    output(at.back(1))

            tiles(dve, body)

        @block2.scalar
        def _(act):
            def rows_t(at):
                if at.past(2):
                    act.wait_ge(hid_made, at.back(2).done(HCH))
                act.wait_ge(xt_made, at.done())
                nc.scalar.activation(x_t[at.ring(2)][:], ps_xt, ACT.Copy).then_inc(xt_taken, 1)

            def body(at):
                if at.loop is None and at.j == 0:
                    rows_t(at)
                if at.exists(TILES):
                    act.wait_ge(b1_in[at.ring(2)], at.uses(2, 16))
                    for j in range(HCH):
                        act.wait_ge(hid_made, at.done(HCH, j + 1))
                        if positive(count := at.done(HCH, j - 3)):
                            act.wait_ge(hid_ready, count)
                        nc.scalar.activation(relu[(2 * at.ring(2) + j) % 4][:], ps_hid[(2 * at.ring(2) + j) % 4],
                                             ACT.Relu, bias=b1[at.ring(2)][:, j:j + 1]).then_inc(relu_done, 1)
                if at.back(-1).exists(TILES):
                    rows_t(at.back(-1))

            tiles(act, body)

        @block2.tensor
        def _(pe):
            def rows_t(at):
                r = at.ring(2)
                pe.wait_ge(x_in[at.ring(4)], at.uses(4, 16))
                if at.past(1):
                    pe.wait_ge(xt_taken, at.back(1).done())
                for k in range(2):
                    for half in range(2):
                        last = nc.tensor.transpose(ps_xt[:, k, half * 128:(half + 1) * 128],
                                                   x_row[at.ring(4)][:, half, k * HALF:(k + 1) * HALF], ident[:])
                last.then_inc(xt_made, 1)

            def hidden_layer(at):
                r = at.ring(2)
                pe.wait_ge(w1_in[at.ring(2)], at.uses(2, 16))
                pe.wait_ge(xt_taken, at.done())
                for j in range(HCH):
                    if positive(count := at.done(HCH, j - 3)):
                        pe.wait_ge(relu_done, count)
                    for k in range(2):
                        last = nc.tensor.matmul(ps_hid[(2 * r + j) % 4], w1[r][:, k, j * 128:(j + 1) * 128],
                                                x_t[r][:, k, :], start=(k == 0), stop=(k == 1))
                    last.then_inc(hid_made, 1)

            def output(at):
                r = at.ring(2)
                pe.wait_ge(w2_in[at.ring(2)], at.uses(2, 16))
                pe.wait_ge(hid_ready, at.done(HCH))
                if at.past(1):
                    pe.wait_ge(y_taken, at.back(1).done())
                for half in range(2):
                    for j in range(HCH):
                        last = nc.tensor.matmul(ps_y[:, half, :], hidden[r][:, j, half * 128:(half + 1) * 128],
                                                w2[r][:, j, :], start=(j == 0), stop=(j == HCH - 1))
                last.then_inc(y_made, 1)

            def body(at):
                if at.loop is None and at.j == 0:
                    rows_t(at)
                if at.exists(TILES):
                    hidden_layer(at)
                if at.back(-1).exists(TILES):
                    rows_t(at.back(-1))
                if at.back(1).exists(TILES):
                    output(at.back(1))

            tiles(pe, body)

        @block2.gpsimd
        def _(pool):
            def body(at):
                if not at.back(1).exists(TILES):
                    return
                at = at.back(1)
                if at.past(1):
                    pool.wait_ge(scattered, at.back(1).done(32))
                pool.wait_ge(y_ready, at.done())
                alone(pool, pool_passed)
                for half in range(2):
                    pool.indirect_dma_start(
                        out_rows, bass.IndirectOffsetOnAxis(ap=token_no[at.ring(2)][:, half:half + 1], axis=0),
                        y_gated[at.ring(2)][:, half, :], None, bounds_check=N - 1, oob_is_err=False,
                        compute_op=ALU.add).then_inc(scattered, 16)

            tiles(pool, body)
            pool.wait_ge(scattered, 32 * TILES)


def kernel(**inputs):
    import numpy as np
    import concourse.bacc as bacc
    from concourse.bass_utils import run_bass_kernel_spmd
    import ml_dtypes

    x = {k: np.ascontiguousarray(v) for k, v in inputs.items()}
    images = x.pop("x")
    side = 14
    px = images.shape[2] // side
    arrays = {
        "patches": images.reshape(IMAGES, 3, side, px, side, px).transpose(0, 1, 3, 5, 2, 4).reshape(
            IMAGES, PIXELS, PATCHES),
        "txt": x["txt"],
        "w_tok_t": x["L0_tok_W"].T,
        "L0_tok_b": x["L0_tok_b"],
        "w_qkv_t": x["L0_attn_w_qkv"].T,
        "L0_attn_b_qkv": x["L0_attn_b_qkv"],
        "w_out_t": x["L0_attn_w_out"].T,
        "L0_attn_b_out": x["L0_attn_b_out"],
        "router_t": x["L0_ffn_router_w"].T,
        "probe_t": x["L0_ffn_probe_w"].T,
        "L0_ffn_probe_w": x["L0_ffn_probe_w"],
        "L0_ffn_router_emb": x["L0_ffn_router_emb"],
        "emb_t": x["L0_ffn_router_emb"].T,
        "b1_t": x["L0_ffn_b1"].reshape(EXPERTS, HCH, 128).transpose(0, 2, 1),
        "L0_ffn_b2": x["L0_ffn_b2"],
        "m_gate1_rows": np.repeat(x["L0_ffn_m_gate1"], 128 // EXPERTS)[:, None],
        "m_gate2_rows": np.repeat(x["L0_ffn_m_gate2"], 128 // EXPERTS)[:, None],
        "ident": np.eye(128, dtype=np.float32),
        "identb": np.eye(128, dtype=ml_dtypes.bfloat16),
        "before": np.triu(np.ones((GROUP, GROUP)), 1).astype(ml_dtypes.bfloat16),
        "ramp": np.arange(EXPERTS, dtype=np.float32) - EXPERTS,
        "region": np.arange(EXPERTS, dtype=np.float32) * CAP,
        "steps256": np.arange(MAXT, dtype=np.float32) * TILE,
        "place0": (np.arange(GROUPS)[None, :] * GROUP + np.arange(GROUP)[:, None]).astype(np.float32),
        "tile_no": np.stack([np.arange(GROUP), np.arange(GROUP) * TILE - ZERO_ROW], 1).astype(np.float32),
    }
    for n in ("fatigue", "energy", "w_fast1", "w_slow1", "h_fast1", "w_fast2", "w_slow2", "h_fast2"):
        arrays[f"L0_ffn_{n}"] = x[f"L0_ffn_{n}"]
    arrays = {k: np.ascontiguousarray(v) for k, v in arrays.items()}
    nc = bacc.Bacc("TRN2", target_bir_lowering=False, num_devices=1)
    aps = {k: nc.dram_tensor(f"in_{k}", v.shape, mybir.dt.from_np(v.dtype), kind="ExternalInput").ap()
           for k, v in arrays.items()}
    out = nc.dram_tensor("out", (IMAGES, S, C), F32, kind="ExternalOutput").ap()
    build(nc, aps, out)
    r = run_bass_kernel_spmd(nc, [{f"in_{k}": v for k, v in arrays.items()}], core_ids=[0])
    return r.results[0]["out"]
```

```python
from contextlib import ExitStack

import concourse.bass as bass
from concourse import mybir

F32 = mybir.dt.float32
BF16 = mybir.dt.bfloat16
I32 = mybir.dt.int32
ALU = mybir.AluOpType
ACT = mybir.ActivationFunctionType
AX = mybir.AxisListType.X

IMAGES, PATCHES, TEXT, PIXELS = 32, 196, 77, 768
C, HEADS, D = 192, 12, 16
S = PATCHES + TEXT
GROUP = PATCHES // 2
GROUPS = 3
PAD = GROUP * GROUPS
HALF = C // 2
N = IMAGES * S
EXPERTS, HID, PROBE = 8, 768, 24
LN_EPS = 1e-5
TERMS = [(0, 0), (1, 1), (0, 1), (1, 0), (0, 2), (2, 0)]
SCORE_ROWS = D * len(TERMS)
SHIFT_ROWS = 3
ROUTE = EXPERTS + PROBE + EXPERTS + 1
TILE = 256
TOPK = 2
TILES = (TOPK * N - EXPERTS) // TILE + EXPERTS
CAP = N + TILE
ZERO_ROW = EXPERTS * CAP
ROW = C + 2
NO_TOKEN = float(N)
WCOLS = EXPERTS * C * HID // (128 * IMAGES)
HCH = HID // 128
MAXT = (N + TILE - 1) // TILE


class At:

    def __init__(self, loop, j, unroll):
        self.loop, self.j, self.unroll = loop, j, unroll

    def back(self, k):
        return At(self.loop, self.j - k, self.unroll)

    def ring(self, n):
        return self.j % n

    def exists(self, limit):
        return self.loop is not None or 0 <= self.j < limit

    def past(self, k):
        return self.loop is not None or self.j >= k

    def times(self, per, plus=0):
        if self.loop is None:
            return per * self.j + plus
        return self.loop * (per * self.unroll) + (per * self.j + plus)

    def done(self, per=1, n=None):
        return self.times(per, per if n is None else n)

    def uses(self, n, per):
        if self.loop is None:
            return (self.j // n + 1) * per
        return self.loop * (self.unroll // n * per) + (self.j // n + 1) * per


def positive(count):
    return not isinstance(count, int) or count > 0


def alone(eng, passed):
    eng.sem_inc(passed, 1)


class Counter:

    def __init__(self, per=0):
        self.per, self.at, self.k = per, At(None, 0, 1), 0

    def start(self, at, k=0):
        self.at, self.k = at, k

    def next(self):
        self.k += 1
        assert not self.per or self.k <= self.per
        return self.at.times(self.per, self.k)


CHUNKS = HEADS * GROUPS
STEPS = [
    (0, "tok0", 0), (1, "tok1", 0), (2, "pv2", 3), (3, "x2t0", 4), (4, "x2t1", 4), (6, "route", 4),
    (8, "shift1", 2), (12, "xt0", 0), (13, "xt1", 0), (14, "qk0", 0), (15, "qk1", 0), (16, "qk2", 0),
    (18, "pv0", 2), (19, "v01", 0), (21, "v2", 0), (24, "shift0", 1), (25, "out01", 3), (27, "out2", 3),
    (29, "pv1", 2), (31, "rank", 4),
]
MIX = 4
assert len(STEPS) % MIX == 0
NAMES = [name for _, name, _ in STEPS]
LAST_LAG = 5
ITERATIONS = IMAGES + LAST_LAG
UNROLL = 4
LOOP_FROM, LOOP_TIMES = 5, 6
TILES_FROM = 5
TILES_TIMES = (TILES - TILES_FROM) // UNROLL


def iterations(eng, body):
    for i in range(LOOP_FROM):
        body(At(None, i, UNROLL))
    with eng.Fori(0, LOOP_TIMES, 1) as loop:
        for j in range(UNROLL):
            body(At(loop, LOOP_FROM + j, UNROLL))
    for i in range(LOOP_FROM + UNROLL * LOOP_TIMES, ITERATIONS):
        body(At(None, i, UNROLL))


def tiles(eng, body):
    for k in range(TILES_FROM):
        body(At(None, k, UNROLL))
    with eng.Fori(0, TILES_TIMES, 1) as loop:
        for j in range(UNROLL):
            body(At(loop, TILES_FROM + j, UNROLL))
    for k in range(TILES_FROM + UNROLL * TILES_TIMES, TILES + 1):
        body(At(None, k, UNROLL))


def build(nc, a, out):
    ctx = ExitStack()
    with ctx:
        phase1 = ExitStack()

        def kept(name, shape, dt=F32):
            return ctx.enter_context(nc.sbuf_tensor(name, shape, dt))

        def sb(name, shape, dt=F32):
            return phase1.enter_context(nc.sbuf_tensor(name, shape, dt))

        def sem(name):
            return ctx.enter_context(nc.semaphore(name))

        def sems(name, n):
            return [sem(f"{name}{i}") for i in range(n)]

        qk_dram = nc.dram_tensor("qk_parts", (2, 3, 2 * C, S), BF16).ap()
        den_dram = nc.dram_tensor("denominators", (2, 4, GROUPS, S), F32).ap()
        rden_dram = nc.dram_tensor("inverse_denominators", (2, 4, GROUPS, S), F32).ap()
        rows_dram = nc.dram_tensor("expert_rows", (ZERO_ROW + TILE, ROW), F32).ap()
        w1_dram = nc.dram_tensor("w1", (EXPERTS, C, HID), F32).ap()
        w2_dram = nc.dram_tensor("w2", (EXPERTS, HID, C), F32).ap()
        table_dram = nc.dram_tensor("tile_table", (TILES, 2), I32).ap()
        out_rows = out.rearrange("b s c -> (b s) c")

        ident = kept("ident", [128, 128])
        ramp = kept("ramp", [GROUP, EXPERTS])
        region = kept("region", [GROUP, EXPERTS])
        steps256 = kept("steps256", [GROUP, MAXT])
        tile_no = kept("tile_no", [GROUP, 2])
        base = kept("base", [GROUP, EXPERTS])
        empty = kept("empty", [128, 2, ROW])

        identb = sb("identb", [128, 128], BF16)
        before = sb("before", [GROUP, GROUP], BF16)
        ones = sb("ones", [GROUP, GROUP], BF16)
        place0 = sb("place0", [GROUP, GROUPS])
        half_neg = sb("half_neg", [GROUP, GROUPS])
        half_pos = sb("half_pos", [GROUP, EXPERTS])
        w_tok = sb("w_tok", [128, PIXELS // 128, C])
        b_tok = sb("b_tok", [GROUP, C])
        w_qkv = sb("w_qkv", [HALF + 1, 2, 3 * C])
        w_out = sb("w_out", [128, GROUPS, C])
        b_out = sb("b_out", [GROUP, C])
        w_route = sb("w_route", [HALF, 2, ROUTE])
        probe_w = sb("probe_w", [PROBE, C])
        emb_t = sb("emb_t", [PROBE, EXPERTS])
        emb_all = sb("emb_all", [GROUP, EXPERTS, PROBE])
        emb_sq = sb("emb_sq", [GROUP, EXPERTS, PROBE])
        gain = sb("gain", [GROUP, 4, EXPERTS])
        fatigue = sb("fatigue", [GROUP, EXPERTS])
        energy = sb("energy", [GROUP, EXPERTS])
        bias8 = sb("bias8", [GROUP, EXPERTS])
        m_gate = sb("m_gate", [128, 2])

        patches = [sb(f"patches{r}", [128, PIXELS // 128, PATCHES]) for r in range(2)]
        resid = [sb(f"resid{r}", [GROUP, GROUPS, C]) for r in range(4)]
        stats = [sb(f"stats{r}", [GROUP, GROUPS, 6]) for r in range(2)]
        mean_var = [sb(f"mean_var{r}", [GROUP, GROUPS, 2]) for r in range(2)]
        var_eps = [sb(f"var_eps{r}", [GROUP, GROUPS]) for r in range(2)]
        rstd = [sb(f"rstd{r}", [GROUP, GROUPS]) for r in range(2)]
        xn = sb("xn", [GROUP, GROUPS, C])
        xn_t = [sb(f"xn_t{r}", [HALF + 1, 2, PAD]) for r in range(2)]
        parts = [sb(f"parts{r}", [128, 9, S], BF16) for r in range(2)]
        rest = sb("rest", [128, 3, S])
        stack = [sb(f"stack{r}", [SCORE_ROWS + SHIFT_ROWS, 2 * HEADS, PAD], BF16) for r in range(4)]
        values = [sb(f"values{r}", [GROUP, GROUPS, HEADS, 32]) for r in range(4)]
        maxima = sb("maxima", [GROUP, GROUPS, HEADS])
        shift = [sb(f"shift{r}", [GROUP, GROUPS, 128], BF16) for r in range(2)]
        shift_rest = [sb(f"shift_rest{r}", [GROUP, GROUPS, 6]) for r in range(2)]
        shift_t = [sb(f"shift_t{r}", [18, S], BF16) for r in range(2)]
        probs = [sb(f"probs{r}", [GROUP, GROUPS, S]) for r in range(8)]
        heads_t = [sb(f"heads_t{r}", [128, GROUPS, S]) for r in range(2)]
        den = sb("den", [126, 26])
        rden = sb("rden", [126, 26])
        rden_all = [sb(f"rden_all{r}", [128, GROUPS, S]) for r in range(2)]
        attn_t = [sb(f"attn_t{r}", [128, GROUPS, PAD]) for r in range(2)]
        h2 = [sb(f"h2{r}", [GROUP, GROUPS, C]) for r in range(2)]
        rows = [[sb(f"rows{r}{k}", [GROUP, GROUPS, ROW]) for k in range(2)] for r in range(2)]
        xn2_t = sb("xn2_t", [HALF, 2, PAD])
        routed = sb("routed", [GROUP, GROUPS, ROUTE])
        sq = sb("sq", [GROUP, GROUPS, PROBE])
        nrm = sb("nrm", [GROUP, 4, GROUPS])
        logit = sb("logit", [GROUP, GROUPS, EXPERTS])
        align = sb("align", [GROUP, GROUPS, EXPERTS])
        tmp8 = sb("tmp8", [GROUP, GROUPS, EXPERTS])
        masked = sb("masked", [GROUP, GROUPS, EXPERTS])
        top = sb("top", [GROUP, 2, GROUPS])
        pick = sb("pick", [GROUP, 2, GROUPS])
        hot = sb("hot", [GROUP, 2, GROUPS * EXPERTS])
        chosen = sb("chosen", [GROUP, GROUPS, EXPERTS], BF16)
        gates = [sb(f"gates{r}", [GROUP, 5, GROUPS]) for r in range(2)]
        token = sb("token", [GROUP, GROUPS])
        pos = sb("pos", [GROUP, GROUPS * EXPERTS])
        pos2 = sb("pos2", [GROUP, 2, GROUPS * EXPERTS])
        posf = sb("posf", [GROUP, 2 * GROUPS])
        posi = [sb(f"posi{r}", [GROUP, 2 * GROUPS], I32) for r in range(2)]
        w_in = [[sb(f"w_in{r}{k}", [128, WCOLS]) for k in range(6)] for r in range(1)]
        w_sum = [[sb(f"w_sum{r}{k}", [128, WCOLS]) for k in range(2)] for r in range(1)]

        ps = ctx.enter_context(nc.psum_tensor("ps", [128, 8, 512], F32))

        def bank(name):
            return ps[:, 4 + NAMES.index(name) % MIX, :]

        made = {name: sem(f"made_{name}") for name in NAMES}
        taken = {name: sem(f"taken_{name}") for name in NAMES}
        const_in = sem("const_in")
        sp_passed, pool_passed, dve_passed = sem("sp_passed"), sem("pool_passed"), sem("dve_passed")
        weights_zeroed = sem("weights_zeroed")
        route_w_in = sem("route_w_in")
        setup_chain = sem("setup_chain")
        gain_sq = sem("gain_sq")
        gain_root = sem("gain_root")
        emb_ready = sem("emb_ready")
        align_made = sem("align_made")
        setup_done = sem("setup_done")
        pool_setup = sem("pool_setup")
        pads_zeroed = sem("pads_zeroed")
        patches_in = sems("patches_in", 2)
        text_in = sems("text_in", 2)
        stats_chain = sem("stats_chain")
        stats_ready = sem("stats_ready")
        rstd_chain = sem("rstd_chain")
        rstd_ready = sem("rstd_ready")
        xn_ready = sem("xn_ready")
        resid_biased = sem("resid_biased")
        part1_ready = sem("part1_ready")
        part2_ready = sem("part2_ready")
        part3_ready = sem("part3_ready")
        parts_out = sems("parts_out", 2)
        stack_in = sems("stack_in", 4)
        max_made = sem("max_made")
        max_taken = sem("max_taken")
        shift_chain = sems("shift_chain", 2)
        shift_ready = sems("shift_ready", 2)
        shift_in = sems("shift_in", 2)
        key_made = sem("key_made")
        exp_done = sem("exp_done")
        den_out = sem("den_out")
        den_in = sem("den_in")
        den_inverse = sem("den_inverse")
        rden_out = sem("rden_out")
        rden_in = sems("rden_in", 2)
        attn_ready = sem("attn_ready")
        h2_out = sems("h2_out", 2)
        stats2_chain = sem("stats2_chain")
        stats2_ready = sem("stats2_ready")
        rstd2_chain = sem("rstd2_chain")
        rstd2_ready = sem("rstd2_ready")
        xn2_ready = sem("xn2_ready")
        row_copied = sem("row_copied")
        norm2_ready = sem("norm2_ready")
        norm_ready = sem("norm_ready")
        route_chain = sem("route_chain")
        chosen_ready = sem("chosen_ready")
        top_gap = sem("top_gap")
        gate_exp = sem("gate_exp")
        gate_sum = sem("gate_sum")
        gate_inv = sem("gate_inv")
        gate_chain = sem("gate_chain")
        place_chain = sem("place_chain")
        pos_ready = sem("pos_ready")
        rows_out = sems("rows_out", 2)
        w_loaded = sem("w_loaded")
        w_chain = sem("w_chain")
        w_summed = sem("w_summed")
        w_stored = sem("w_stored")
        empty_ready = sem("empty_ready")
        empty_out = sem("empty_out")
        plan_chain = sem("plan_chain")
        ends_ready = sem("ends_ready")
        table_ready = sem("table_ready")
        table_out = sem("table_out")
        table_in = sem("table_in")
        ends_out = sem("ends_out")

        CONSTS = 30
        FILLS = 8
        flat_w = {}
        for k, n in enumerate(("w_fast", "w_slow", "h_fast")):
            for layer in range(2):
                flat_w[layer, k] = a[f"L0_ffn_{n}{layer + 1}"].rearrange("e a b -> (e a b)").rearrange(
                    "(p f) -> p f", p=128)
        w1_flat = w1_dram.rearrange("e a b -> (e a b)").rearrange("(p f) -> p f", p=128)
        w2_flat = w2_dram.rearrange("e a b -> (e a b)").rearrange("(p f) -> p f", p=128)
        image_in = a["patches"].rearrange("b (k p) t -> b p k t", p=128)

        block = phase1.enter_context(nc.Block())

        @block.sync
        def _(sp):
            loads = [0]

            def load(dst, src, signal=const_in):
                if signal is const_in:
                    loads[0] += 1
                sp.dma_start(dst, src).then_inc(signal, 16)

            def image_loads(at):
                if at.past(2):
                    sp.wait_ge(made["tok1"], at.back(2).done())
                src = image_in[at.j] if at.loop is None else image_in[bass.ds(at.times(1), 1)].rearrange(
                    "b p k t -> (b p) k t")
                sp.dma_start(patches[at.ring(2)][:], src).then_inc(patches_in[at.ring(2)], 16)

            def text_load(at):
                if at.past(4):
                    sp.wait_ge(taken["out2"], at.back(4).done())
                src = a["txt"][at.j] if at.loop is None else a["txt"][bass.ds(at.times(1), 1)].rearrange(
                    "b t c -> (b t) c")
                sp.dma_start(resid[at.ring(4)][0:TEXT, 2, :], src).then_inc(text_in[at.ring(2)], 16)

            def weight_loads(at):
                if at.past(1):
                    sp.wait_ge(w_summed, at.back(1).done(2))
                for layer in range(2):
                    for k in range(3):
                        sp.dma_start(w_in[0][3 * layer + k][:],
                                     flat_w[layer, k][:, bass.ds(at.times(WCOLS), WCOLS)]).then_inc(w_loaded, 16)

            load(w_tok[:], a["w_tok_t"].rearrange("(k p) h -> p k h", p=128))
            sp.wait_ge(pads_zeroed, 4)
            image_loads(At(None, 0, UNROLL))
            text_load(At(None, 0, UNROLL))
            load(b_tok[:], a["L0_tok_b"].partition_broadcast(GROUP))
            load(ident[:], a["ident"])
            load(identb[:], a["identb"])
            load(before[:], a["before"])
            load(w_qkv[0:HALF, :, :], a["w_qkv_t"].rearrange("(k p) n -> p k n", p=HALF))
            load(w_qkv[HALF:HALF + 1, 1, :], a["L0_attn_b_qkv"][None, :])
            load(ramp[:], a["ramp"].partition_broadcast(GROUP))
            load(region[:], a["region"].partition_broadcast(GROUP))
            load(steps256[:], a["steps256"].partition_broadcast(GROUP))
            load(place0[:], a["place0"])
            load(tile_no[:], a["tile_no"])
            load(base[:], a["region"].partition_broadcast(GROUP))
            load(emb_all[:].rearrange("p e d -> p (e d)"),
                 a["L0_ffn_router_emb"].rearrange("e d -> (e d)").partition_broadcast(GROUP))
            load(emb_t[:], a["emb_t"])
            load(probe_w[:], a["L0_ffn_probe_w"])
            load(fatigue[:], a["L0_ffn_fatigue"].partition_broadcast(GROUP))
            load(energy[:], a["L0_ffn_energy"].partition_broadcast(GROUP))
            load(b_out[:], a["L0_attn_b_out"].partition_broadcast(GROUP))
            sp.wait_ge(weights_zeroed, 1)
            for j in range(4):
                load(w_out[32 * j:32 * j + D, :, :],
                     a["w_out_t"].rearrange("(g j r) n -> j r g n", j=4, r=D)[j])
            for layer in range(2):
                load(m_gate[:, layer:layer + 1], a[f"m_gate{layer + 1}_rows"])
            for k in range(2):
                load(w_route[:, k, 0:EXPERTS], a["router_t"][k * HALF:(k + 1) * HALF, :])
                load(w_route[:, k, EXPERTS:EXPERTS + PROBE], a["probe_t"][k * HALF:(k + 1) * HALF, :])
            assert loads[0] == CONSTS - 1, loads
            image_loads(At(None, 1, UNROLL))
            text_load(At(None, 1, UNROLL))
            weight_loads(At(None, 0, UNROLL))

            def shift_rows(at, half):
                sp.wait_ge(taken[f"shift{half}"], at.done())
                for k in range(SHIFT_ROWS):
                    row = SCORE_ROWS + k
                    sp.dma_start(stack[at.ring(4)][row:row + 1, 6 * half:6 * half + 6, 0:S],
                                 shift_t[half][6 * k:6 * k + 6, :]).then_inc(shift_in[half], 16)

            def denominators(at):
                r = at.ring(2)
                for g in range(GROUPS):
                    sp.wait_ge(taken[f"pv{g}"], at.done())
                sp.dma_start(den_dram[r], heads_t[r][D:128:32, :, :]).then_inc(den_out, 16)
                sp.wait_ge(den_out, at.done(16))
                sp.dma_start(den[:], den_dram[r].rearrange("j g t -> (j g t)").rearrange(
                    "(p f) -> p f", p=126)).then_inc(den_in, 16)

            def inverses(at):
                r = at.ring(2)
                sp.wait_ge(den_inverse, at.done())
                sp.dma_start(rden_dram[r].rearrange("j g t -> (j g t)").rearrange("(p f) -> p f", p=126),
                             rden[:]).then_inc(rden_out, 16)
                sp.wait_ge(rden_out, at.done(16))
                for j in range(4):
                    sp.dma_start(rden_all[r][32 * j:32 * j + D, :, :].rearrange("p g t -> p (g t)"),
                                 rden_dram[r, j].rearrange("g t -> (g t)").partition_broadcast(D)
                                 ).then_inc(rden_in[r], 16)

            def stack_loads(at):
                r = at.ring(2)
                sp.wait_ge(part3_ready, at.done())
                alone(sp, sp_passed)
                if at.past(2):
                    sp.wait_ge(stack_in[at.back(2).ring(4)], at.back(2).uses(4, 160))
                alone(sp, sp_passed)
                sp.dma_start(qk_dram[r].rearrange("a (m p) t -> p (a m) t", p=128), parts[r][:]
                             ).then_inc(parts_out[r], 16)
                sp.wait_ge(parts_out[at.ring(2)], at.uses(2, 16))
                alone(sp, sp_passed)
                if at.past(4):
                    sp.wait_ge(key_made, at.back(4).done(CHUNKS))
                view = qk_dram[r].rearrange("a (h d) t -> a d h t", d=D)
                for t, (q_part, k_part) in enumerate(TERMS):
                    dst = stack[at.ring(4)][D * t:D * t + D, :, 0:S]
                    if q_part == k_part:
                        sp.dma_start(dst, view[q_part]).then_inc(stack_in[at.ring(4)], 16)
                    else:
                        sp.dma_start(dst[:, 0:HEADS, :], view[q_part][:, 0:HEADS, :]
                                     ).then_inc(stack_in[at.ring(4)], 16)
                        sp.dma_start(dst[:, HEADS:, :], view[k_part][:, HEADS:, :]
                                     ).then_inc(stack_in[at.ring(4)], 16)

            def h2_store(at):
                sp.wait_ge(taken["out2"], at.done())
                sp.wait_ge(taken["out01"], at.done())
                r = at.ring(2)
                dst = out[at.j] if at.loop is None else out[bass.ds(at.times(1), 1)].rearrange("b s c -> (b s) c")
                sp.dma_start(dst[0:PATCHES, :].rearrange("(g p) c -> p g c", p=GROUP), h2[r][:, 0:2, :]
                             ).then_inc(h2_out[r], 16)
                sp.dma_start(dst[PATCHES:S, :], h2[r][0:TEXT, 2, :]).then_inc(h2_out[r], 16)

            def weight_stores(at):
                sp.wait_ge(w_summed, at.done(2))
                for layer, flat in enumerate((w1_flat, w2_flat)):
                    sp.dma_start(flat[:, bass.ds(at.times(WCOLS), WCOLS)], w_sum[0][layer][:]
                                 ).then_inc(w_stored, 16)

            def body(i):
                if i.back(3).exists(IMAGES):
                    denominators(i.back(3))
                if i.loop is not None or 2 <= i.j + 1 < IMAGES:
                    image_loads(i.back(-1))
                if i.back(2).exists(IMAGES):
                    shift_rows(i.back(2), 1)
                if i.back(3).exists(IMAGES):
                    inverses(i.back(3))
                if i.exists(IMAGES):
                    stack_loads(i)
                if i.back(1).exists(IMAGES):
                    shift_rows(i.back(1), 0)
                if i.back(3).exists(IMAGES):
                    h2_store(i.back(3))
                if i.loop is not None or 2 <= i.j + 1 < IMAGES:
                    text_load(i.back(-1))
                if i.exists(IMAGES):
                    weight_stores(i)
                    if i.loop is not None or i.j + 1 < IMAGES:
                        weight_loads(i.back(-1))

            iterations(sp, body)
            for r in range(2):
                sp.wait_ge(h2_out[r], 32 * IMAGES // 2)
                sp.wait_ge(rows_out[r], 96 * IMAGES // 2)
            sp.wait_ge(w_stored, 32 * IMAGES)

        @block.gpsimd
        def _(pool):
            filled = [0]

            def fill(dst, value):
                nc.gpsimd.memset(dst, value).then_inc(pool_setup, 1)
                filled[0] += 1
                pool.wait_ge(pool_setup, filled[0])

            fill(w_out[:], 0.0)
            nc.gpsimd.memset(half_neg[:], -0.5).then_inc(weights_zeroed, 1)
            pool.wait_ge(weights_zeroed, 1)
            fill(half_pos[:], 0.5)
            for r in range(2):
                fill(rden_all[r][:], 0.0)
                fill(shift[r][:], 0.0)
            fill(empty[:], 0.0)
            fill(empty[:, :, C:C + 1], NO_TOKEN)
            assert filled[0] == FILLS
            pool.wait_ge(const_in, 16 * (CONSTS - 1))
            nc.gpsimd.tensor_scalar(token[:], place0[:], -float(S), None, ALU.add).then_inc(pool_setup, 1)
            pool.wait_ge(pool_setup, FILLS + 1)
            pool.wait_ge(gain_sq, 1)
            nc.gpsimd.tensor_tensor(gain[:, 1, :], gain[:, 0, :], half_pos[:], ALU.pow).then_inc(gain_root, 1)
            w_c = Counter(4)

            def weights(at):
                if at.past(1):
                    pool.wait_ge(w_stored, at.back(1).done(32))
                pool.wait_ge(w_loaded, at.done(96))
                alone(pool, pool_passed)
                w_c.start(at)
                for layer in range(2):
                    fast, slow, h_fast = w_in[0][3 * layer:3 * layer + 3]
                    total = w_sum[0][layer]
                    if layer == 1:
                        alone(pool, pool_passed)
                    nc.gpsimd.tensor_scalar(slow[:], slow[:], m_gate[:, layer:layer + 1], None, ALU.mult
                                            ).then_inc(w_chain, 1)
                    pool.wait_ge(w_chain, w_c.next())
                    nc.gpsimd.tensor_tensor(slow[:], slow[:], fast[:], ALU.add).then_inc(w_chain, 1)
                    pool.wait_ge(w_chain, w_c.next())
                    nc.gpsimd.tensor_tensor(total[:], slow[:], h_fast[:], ALU.add).then_inc(w_summed, 1)

            def power(at, chain, mv, ve, rs, ready, done):
                pool.wait_ge(ready, at.done())
                alone(pool, pool_passed)
                nc.gpsimd.tensor_scalar(ve[:], mv[:, :, 1], LN_EPS, None, ALU.add).then_inc(chain, 1)
                pool.wait_ge(chain, at.done())
                nc.gpsimd.tensor_tensor(rs[:], ve[:], half_neg[:], ALU.pow).then_inc(done, 1)

            def gate(at):
                g = gates[at.ring(2)]
                pool.wait_ge(gate_exp, at.done())
                alone(pool, pool_passed)
                nc.gpsimd.tensor_scalar(g[:, 2, :], g[:, 1, :], 1.0, None, ALU.add).then_inc(gate_sum, 1)
                pool.wait_ge(gate_inv, at.done())
                nc.gpsimd.tensor_tensor(g[:, 4, :], g[:, 1, :], g[:, 3, :], ALU.mult)
                nc.gpsimd.tensor_scalar(token[:], token[:], float(S), None, ALU.add).then_inc(gate_chain, 1)
                pool.wait_ge(gate_chain, at.done())
                pair = rows[at.ring(2)]
                alone(pool, pool_passed)
                nc.gpsimd.tensor_copy(pair[0][:, :, C], token[:])
                nc.gpsimd.tensor_copy(pair[1][:, :, C], token[:])
                nc.gpsimd.tensor_copy(pair[0][:, :, C + 1], g[:, 3, :])
                nc.gpsimd.tensor_copy(pair[1][:, :, C + 1], g[:, 4, :]).then_inc(row_copied, 1)

            def place(at):
                pool.wait_ge(row_copied, at.done(2))
                pool.wait_ge(pos_ready, at.done())
                alone(pool, pool_passed)
                for k in range(TOPK):
                    for g in range(GROUPS):
                        n = TEXT if g == 2 else GROUP
                        pool.indirect_dma_start(
                            rows_dram, bass.IndirectOffsetOnAxis(
                                ap=posi[at.ring(2)][0:n, k * GROUPS + g:k * GROUPS + g + 1], axis=0),
                            rows[at.ring(2)][k][0:n, g, :], None).then_inc(rows_out[at.ring(2)], 16)

            def body(i):
                five, four, three = i.back(5), i.back(4), i.back(3)
                if i.exists(IMAGES):
                    power(i, rstd_chain, mean_var[0], var_eps[0], rstd[0], stats_ready, rstd_ready)
                if four.exists(IMAGES):
                    pool.wait_ge(norm2_ready, four.done())
                    nc.gpsimd.tensor_tensor(nrm[:, 1, :], nrm[:, 0, :], half_pos[:, 0:GROUPS], ALU.pow
                                            ).then_inc(norm_ready, 1)
                if five.exists(IMAGES):
                    place(five)
                if i.exists(IMAGES):
                    pool.wait_ge(xn_ready, i.done(GROUPS))
                    h = resid[i.ring(4)]
                    for g in range(2):
                        nc.gpsimd.tensor_tensor(h[:, g, :], h[:, g, :], b_out[:], ALU.add)
                    nc.gpsimd.tensor_tensor(h[0:TEXT, 2, :], h[0:TEXT, 2, :], b_out[0:TEXT, :], ALU.add
                                            ).then_inc(resid_biased, 1)
                if three.exists(IMAGES):
                    r = three.ring(2)
                    pool.wait_ge(rden_in[three.ring(2)], three.uses(2, 64))
                    if three.past(2):
                        pool.wait_ge(made["out2"], three.back(2).done())
                    nc.gpsimd.tensor_tensor(attn_t[r][:, :, 0:S], heads_t[r][:], rden_all[r][:], ALU.mult
                                            ).then_inc(attn_ready, 1)
                if i.exists(IMAGES):
                    weights(i)
                if three.exists(IMAGES):
                    power(three, rstd2_chain, mean_var[1], var_eps[1], rstd[1], stats2_ready, rstd2_ready)
                if four.exists(IMAGES):
                    gate(four)
                if three.exists(IMAGES):
                    pool.wait_ge(xn2_ready, three.done(GROUPS))
                    alone(pool, pool_passed)
                    pair = rows[three.ring(2)]
                    nc.gpsimd.tensor_copy(pair[1][:, :, 0:C], pair[0][:, :, 0:C]).then_inc(row_copied, 1)

            iterations(pool, body)

        @block.vector
        def _(dve):
            step = Counter()

            for r in range(4):
                nc.vector.memset(resid[r][64:GROUP, 2, :], 0.0).then_inc(pads_zeroed, 1)
            for r in range(4):
                nc.vector.memset(stack[r][:, :, S:PAD], 0.0)
                nc.vector.memset(stack[r][SCORE_ROWS:, HEADS:, 0:S], 1.0)
                nc.vector.memset(values[r][:, :, :, D:2 * D], 1.0)
            for r in range(2):
                nc.vector.memset(attn_t[r][:, :, S:PAD], 0.0)
                nc.vector.memset(xn_t[r][HALF:HALF + 1, 1, :], 1.0)
            nc.vector.memset(ones[:], 1.0)
            nc.vector.memset(w_route[:, :, ROUTE - 1:ROUTE], 1.0 / C).then_inc(setup_chain, 1)
            dve.wait_ge(setup_chain, step.next())
            dve.wait_ge(const_in, 16 * (CONSTS - 1))
            nc.vector.tensor_tensor(emb_sq[:], emb_all[:], emb_all[:], ALU.mult).then_inc(setup_chain, 1)
            dve.wait_ge(setup_chain, step.next())
            nc.vector.tensor_reduce(gain[:, 0, :], emb_sq[:], AX, ALU.add).then_inc(gain_sq, 1)
            dve.wait_ge(gain_root, 1)
            nc.vector.tensor_scalar(gain[:, 2, :], gain[:, 1, :], 0.02, 0.02, ALU.mult, ALU.add
                                    ).then_inc(setup_chain, 1)
            dve.wait_ge(setup_chain, step.next())
            nc.vector.tensor_scalar(gain[:, 3, :], gain[:, 1, :], 1e-12, None, ALU.max).then_inc(setup_chain, 1)
            dve.wait_ge(setup_chain, step.next())
            nc.vector.reciprocal(gain[:, 3, :], gain[:, 3, :]).then_inc(setup_chain, 1)
            dve.wait_ge(setup_chain, step.next())
            nc.vector.tensor_tensor(emb_t[:], emb_t[:], gain[0:PROBE, 3, :], ALU.mult).then_inc(emb_ready, 1)
            nc.vector.tensor_tensor(bias8[:], energy[:], fatigue[:], ALU.subtract).then_inc(setup_chain, 1)
            dve.wait_ge(setup_chain, step.next())
            nc.vector.tensor_scalar(bias8[:], bias8[:], 0.1, None, ALU.mult).then_inc(setup_chain, 1)
            dve.wait_ge(setup_chain, step.next())
            dve.wait_ge(align_made, 1)
            lo = EXPERTS + PROBE
            nc.vector.tensor_copy(w_route[:, 0, lo:lo + EXPERTS], ps[0:HALF, 7, 0:EXPERTS])
            nc.vector.tensor_copy(w_route[:, 1, lo:lo + EXPERTS], ps[0:HALF, 7, EXPERTS:2 * EXPERTS]
                                  ).then_inc(setup_done, 1)

            shift_c = [Counter(3) for _ in range(2)]
            ROUTE_STEPS = 19
            place_c = Counter(3)

            def tok(at, g):
                dve.wait_ge(made[f"tok{g}"], at.done())
                if g == 0:
                    if at.past(4):
                        dve.wait_ge(taken["out2"], at.back(4).done())
                nc.vector.tensor_tensor(resid[at.ring(4)][:, g, :], bank(f"tok{g}")[0:GROUP, 0:C], b_tok[:], ALU.add
                                        ).then_inc(taken[f"tok{g}"], 1)

            def group_stats(at, h, k, chain, groups):
                for g in groups:
                    nc.vector.bn_stats(stats[k][:, g, :], h[:, g, :]).then_inc(chain, 1)

            def mean_and_variance(at, k, chain, ready):
                dve.wait_ge(chain, at.done(3))
                alone(dve, dve_passed)
                for g in range(GROUPS):
                    last = nc.vector.bn_aggr(mean_var[k][:, g, :], stats[k][:, g, :])
                last.then_inc(ready, 1)

            def normalise(at, h, k, dst, g, rstd_done, done):
                if g == 0:
                    dve.wait_ge(rstd_done, at.done())
                nc.vector.tensor_scalar(dst[:, g, 0:C], h[:, g, :], mean_var[k][:, g, 0:1],
                                        rstd[k][:, g:g + 1], ALU.subtract, ALU.mult).then_inc(done, 1)

            def remainder(at, m):
                dve.wait_ge(part1_ready, at.done(3, m + 1))
                if m == 0:
                    if at.past(1):
                        dve.wait_ge(part3_ready, at.back(1).done())
                nc.vector.tensor_tensor(rest[:, m, :], bank(f"qk{m}")[:, 0:S], parts[at.ring(2)][:, m, :], ALU.subtract
                                        ).then_inc(taken[f"qk{m}"], 1)

            def third_part(at):
                dve.wait_ge(part2_ready, at.done())
                p = parts[at.ring(2)]
                nc.vector.tensor_tensor(p[:, 6:9, :], rest[:], p[:, 3:6, :], ALU.subtract).then_inc(part3_ready, 1)

            def maximum(at, chunk):
                dve.wait_ge(max_made, at.done(CHUNKS, chunk + 1))
                h, g = chunk // GROUPS, chunk % GROUPS
                nc.vector.tensor_reduce(maxima[:, g, h:h + 1], ps[0:GROUP, chunk % 2, 0:S], AX, ALU.max
                                        ).then_inc(max_taken, 1)

            def shift_part(at, half, n):
                c, m = shift_c[half], maxima[:, :, 6 * half:6 * half + 6]
                s, r = shift[half], shift_rest[half]
                if n == 0:
                    dve.wait_ge(max_taken, at.done(CHUNKS, 18 * (half + 1)))
                    if at.past(1):
                        dve.wait_ge(made[f"shift{half}"], at.back(1).done())
                    nc.vector.tensor_scalar(s[:, :, 0:6], m, -1.0, None, ALU.mult).then_inc(shift_chain[half], 1)
                    return
                c.start(at, n - 1)
                dve.wait_ge(shift_chain[half], c.next())
                if n == 1:
                    nc.vector.scalar_tensor_tensor(r[:], m, -1.0, s[:, :, 0:6], ALU.mult, ALU.subtract
                                                   ).then_inc(shift_chain[half], 1)
                if n == 2:
                    nc.vector.tensor_copy(s[:, :, 6:12], r[:]).then_inc(shift_chain[half], 1)
                if n == 3:
                    nc.vector.tensor_tensor(s[:, :, 12:18], r[:], s[:, :, 6:12], ALU.subtract
                                            ).then_inc(shift_ready[half], 1)

            def invert(at):
                dve.wait_ge(den_in, at.done(16))
                if at.past(1):
                    dve.wait_ge(rden_out, at.back(1).done(16))
                nc.vector.reciprocal(rden[:], den[:]).then_inc(den_inverse, 1)

            def attention_out(at, name, groups):
                dve.wait_ge(made[name], at.done())
                if name == "out01":
                    dve.wait_ge(resid_biased, at.done())
                    if at.past(2):
                        dve.wait_ge(h2_out[at.back(2).ring(2)], at.back(2).uses(2, 32))
                n = len(groups)
                lo, hi = groups[0], groups[-1] + 1
                nc.vector.tensor_tensor(h2[at.ring(2)][:, lo:hi, :],
                                        bank(name)[0:GROUP, 0:n * C].rearrange("p (g c) -> p g c", g=n),
                                        resid[at.ring(4)][:, lo:hi, :], ALU.add).then_inc(taken[name], 1)

            b3 = [GROUP, GROUPS, EXPERTS]

            def over_experts(v):
                return v[:, :, None].broadcast_to(b3)

            def over_groups(v):
                return v[:, None, :].broadcast_to(b3)

            hot0 = hot[:, 0, :].rearrange("p (g e) -> p g e", g=GROUPS)
            hot1 = hot[:, 1, :].rearrange("p (g e) -> p g e", g=GROUPS)

            def route_copy(at):
                dve.wait_ge(made["route"], at.done())
                nc.vector.tensor_copy(routed[:], bank("route")[0:GROUP, 0:GROUPS * ROUTE].rearrange(
                    "p (g n) -> p g n", g=GROUPS)).then_inc(taken["route"], 1)

            def route_sums(at, n):
                if n == 0:
                    dve.wait_ge(taken["route"], at.done())
                    probe = routed[:, :, EXPERTS:lo]
                    nc.vector.tensor_tensor(sq[:], probe, probe, ALU.mult).then_inc(route_chain, 1)
                    nc.vector.tensor_tensor(tmp8[:], over_experts(routed[:, :, ROUTE - 1]),
                                            over_groups(gain[:, 2, :]), ALU.mult).then_inc(route_chain, 1)
                if n == 1:
                    route_after(at, 2)
                    nc.vector.tensor_reduce(nrm[:, 0, :], sq[:], AX, ALU.add).then_inc(norm2_ready, 1)
                    nc.vector.tensor_tensor(logit[:], routed[:, :, 0:EXPERTS], tmp8[:], ALU.add
                                            ).then_inc(route_chain, 1)

            def route_after(at, n):
                dve.wait_ge(route_chain, at.done(ROUTE_STEPS, n))

            def route_logits(at, n):
                if n == 0:
                    dve.wait_ge(norm_ready, at.done())
                    nc.vector.tensor_scalar(nrm[:, 2, :], nrm[:, 1, :], 1e-12, None, ALU.max
                                            ).then_inc(route_chain, 1)
                if n == 1:
                    route_after(at, 4)
                    nc.vector.reciprocal(nrm[:, 3, :], nrm[:, 2, :]).then_inc(route_chain, 1)
                if n == 2:
                    route_after(at, 5)
                    nc.vector.tensor_tensor(align[:], routed[:, :, lo:lo + EXPERTS], over_experts(nrm[:, 3, :]),
                                            ALU.mult).then_inc(route_chain, 1)
                if n == 3:
                    route_after(at, 6)
                    nc.vector.scalar_tensor_tensor(logit[:], align[:], 0.02, logit[:], ALU.mult, ALU.add
                                                   ).then_inc(route_chain, 1)
                if n == 4:
                    route_after(at, 7)
                    nc.vector.tensor_tensor(logit[:], logit[:], over_groups(bias8[:]), ALU.add
                                            ).then_inc(route_chain, 1)

            def choose(at, scores, k, n):
                route_after(at, 8 + 6 * k + n)
                if n == 0:
                    nc.vector.tensor_reduce(top[:, k, :], scores[:], AX, ALU.max).then_inc(route_chain, 1)
                if n == 1:
                    nc.vector.tensor_tensor(tmp8[:], scores[:], over_experts(top[:, k, :]), ALU.is_equal
                                            ).then_inc(route_chain, 1)
                if n == 2:
                    nc.vector.tensor_tensor(tmp8[:], tmp8[:], over_groups(ramp[:]), ALU.mult
                                            ).then_inc(route_chain, 1)
                if n == 3:
                    nc.vector.tensor_reduce(pick[:, k, :], tmp8[:], AX, ALU.min).then_inc(route_chain, 1)
                if n == 4:
                    nc.vector.tensor_tensor(hot[:, k, :].rearrange("p (g e) -> p g e", g=GROUPS),
                                            over_groups(ramp[:]), over_experts(pick[:, k, :]), ALU.is_equal
                                            ).then_inc(route_chain, 1)

            def mask_first(at):
                route_after(at, 13)
                nc.vector.scalar_tensor_tensor(masked[:], hot0, -3e38, logit[:], ALU.mult, ALU.add
                                               ).then_inc(route_chain, 1)

            def choices(at):
                route_after(at, ROUTE_STEPS)
                if at.past(1):
                    dve.wait_ge(made["rank"], at.back(1).done())
                nc.vector.tensor_tensor(chosen[:], hot0, hot1, ALU.add).then_inc(chosen_ready, 1)
                if at.past(2):
                    dve.wait_ge(rows_out[at.back(2).ring(2)], at.back(2).uses(2, 96))
                nc.vector.tensor_tensor(gates[at.ring(2)][:, 0, :], top[:, 1, :], top[:, 0, :], ALU.subtract
                                        ).then_inc(top_gap, 1)

            def place(at, n):
                ge = GROUPS * EXPERTS
                counts = bank("rank")[0:GROUP]
                if n == 0:
                    dve.wait_ge(made["rank"], at.done())
                    nc.vector.tensor_tensor(pos[:].rearrange("p (g e) -> p g e", g=GROUPS),
                                            counts[:, 0:ge].rearrange("p (g e) -> p g e", g=GROUPS),
                                            over_groups(base[:]), ALU.add).then_inc(place_chain, 1)
                    return
                place_c.start(at, n - 1)
                dve.wait_ge(place_chain, place_c.next())
                if n == 1:
                    nc.vector.tensor_tensor(base[:], base[:], counts[:, ge:ge + EXPERTS], ALU.add
                                            ).then_inc(taken["rank"], 1)
                    nc.vector.tensor_tensor(pos2[:], hot[:], pos[:, None, :].broadcast_to([GROUP, 2, ge]), ALU.mult
                                            ).then_inc(place_chain, 1)
                if n == 2:
                    nc.vector.tensor_reduce(posf[:], pos2[:].rearrange("p k (g e) -> p (k g) e", g=GROUPS),
                                            AX, ALU.add).then_inc(place_chain, 1)
                if n == 3:
                    nc.vector.tensor_copy(posi[at.ring(2)][:], posf[:]).then_inc(pos_ready, 1)

            def gate_inverse(at):
                dve.wait_ge(gate_sum, at.done())
                g = gates[at.ring(2)]
                nc.vector.reciprocal(g[:, 3, :], g[:, 2, :]).then_inc(gate_inv, 1)

            def body(i):
                one, two, three, four = (i.back(k) for k in (1, 2, 3, 4))
                here = i.exists(IMAGES)
                for chunk in range(CHUNKS):
                    if one.exists(IMAGES):
                        maximum(one, chunk)
                    if here:
                        if chunk in (0, 1):
                            tok(i, chunk)
                        if chunk == 1:
                            dve.wait_ge(text_in[i.ring(2)], i.uses(2, 16))
                            if i.past(1):
                                dve.wait_ge(rstd_ready, i.back(1).done())
                            group_stats(i, resid[i.ring(4)], 0, stats_chain, (2,))
                        if chunk == 2:
                            dve.wait_ge(taken["tok1"], i.done())
                            group_stats(i, resid[i.ring(4)], 0, stats_chain, (0, 1))
                        if chunk == 3:
                            mean_and_variance(i, 0, stats_chain, stats_ready)
                        if chunk in (8, 9, 10):
                            if chunk == 8 and i.past(1):
                                dve.wait_ge(made["xt1"], i.back(1).done())
                            normalise(i, resid[i.ring(4)], 0, xn, chunk - 8, rstd_ready, xn_ready)
                        if chunk in (15, 16, 17):
                            remainder(i, chunk - 15)
                        if chunk == 19:
                            third_part(i)
                    if one.exists(IMAGES):
                        if chunk in (19, 20, 21, 22):
                            shift_part(one, 0, chunk - 19)
                    if two.exists(IMAGES):
                        if chunk in (1, 3, 5, 7):
                            shift_part(two, 1, chunk // 2)
                    if three.exists(IMAGES):
                        if chunk == 10:
                            invert(three)
                        if chunk == 25:
                            attention_out(three, "out01", (0, 1))
                        if chunk == 27:
                            attention_out(three, "out2", (2,))
                        if chunk == 28:
                            dve.wait_ge(taken["out01"], three.done())
                            if three.past(1):
                                dve.wait_ge(rstd2_ready, three.back(1).done())
                        if chunk == 30:
                            dve.wait_ge(taken["out2"], three.done())
                        if chunk in (28, 29, 30):
                            group_stats(three, h2[three.ring(2)], 1, stats2_chain, (chunk - 28,))
                        if chunk == 31:
                            mean_and_variance(three, 1, stats2_chain, stats2_ready)
                    if four.exists(IMAGES):
                        if chunk == 6:
                            route_copy(four)
                        if chunk in (7, 8):
                            route_sums(four, chunk - 7)
                        if chunk in (11, 12, 13):
                            route_logits(four, chunk - 11)
                        if chunk in (14, 15):
                            route_logits(four, chunk - 11)
                        if chunk in (16, 17, 18, 19, 20):
                            choose(four, logit, 0, chunk - 16)
                        if chunk == 21:
                            mask_first(four)
                        if chunk in (22, 23, 24, 25, 26):
                            choose(four, masked, 1, chunk - 22)
                        if chunk == 27:
                            choices(four)
                        if chunk in (31, 32, 33, 34):
                            place(four, chunk - 31)
                        if chunk == 35:
                            gate_inverse(four)
                    if three.exists(IMAGES) and chunk in (33, 34, 35):
                        if chunk == 33 and three.past(2):
                            dve.wait_ge(rows_out[three.back(2).ring(2)], three.back(2).uses(2, 96))
                        normalise(three, h2[three.ring(2)], 1, rows[three.ring(2)][0], chunk - 33,
                                  rstd2_ready, xn2_ready)

            iterations(dve, body)

        @block.scalar
        def _(act):
            def take(at, name, dst, src, sem_done=None):
                act.wait_ge(made[name], at.done())
                nc.scalar.activation(dst, src, ACT.Copy).then_inc(taken[name] if sem_done is None else sem_done, 1)

            def body(i):
                one, two, three, four = (i.back(k) for k in (1, 2, 3, 4))
                here = i.exists(IMAGES)
                r = i.ring(2)

                for chunk in range(CHUNKS):
                    if three.exists(IMAGES) and chunk == 2:
                        take(three, "pv2", heads_t[three.ring(2)][:, 2, :], bank("pv2")[:, 0:S])
                    if four.exists(IMAGES) and chunk in (3, 4):
                        if chunk == 3 and four.past(1):
                            act.wait_ge(made["route"], four.back(1).done())
                        k = chunk - 3
                        take(four, f"x2t{k}", xn2_t[:, k, :], bank(f"x2t{k}")[0:HALF, 0:PAD])
                    for at, half, when in ((one, 0, 24), (two, 1, 8)):
                        if at.exists(IMAGES) and chunk == when:
                            if at.past(1):
                                act.wait_ge(shift_in[half], at.back(1).done(48))
                            take(at, f"shift{half}", shift_t[half][:],
                                 bank(f"shift{half}").bitcast(BF16)[0:18, 0:S])
                    if here:
                        if chunk == 12:
                            if i.past(2):
                                act.wait_ge(made["v2"], i.back(2).done())
                        if chunk in (12, 13):
                            k = chunk - 12
                            take(i, f"xt{k}", xn_t[r][0:HALF, k, :], bank(f"xt{k}")[0:HALF, 0:PAD])
                        if chunk == 14:
                            if i.past(2):
                                act.wait_ge(parts_out[i.back(2).ring(2)], i.back(2).uses(2, 16))
                        if chunk in (14, 15, 16):
                            m = chunk - 14
                            take(i, f"qk{m}", parts[r][:, m, :], bank(f"qk{m}")[:, 0:S], part1_ready)
                        if chunk == 18:
                            act.wait_ge(taken["qk2"], i.done())
                            nc.scalar.activation(parts[r][:, 3:6, :], rest[:], ACT.Copy).then_inc(part2_ready, 1)
                        if chunk == 19:
                            if i.past(4):
                                act.wait_ge(made["pv2"], i.back(4).done())
                            take(i, "v01", values[i.ring(4)][:, 0:2, :, 0:D],
                                 bank("v01")[0:GROUP, 0:2 * C].rearrange("p (g h d) -> p g h d", g=2, h=HEADS))
                        if chunk == 21:
                            take(i, "v2", values[i.ring(4)][:, 2, :, 0:D],
                                 bank("v2")[0:GROUP, 0:C].rearrange("p (h d) -> p h d", h=HEADS))
                    if four.exists(IMAGES) and chunk == 29:
                        act.wait_ge(top_gap, four.done())
                        g = gates[four.ring(2)]
                        nc.scalar.activation(g[:, 1, :], g[:, 0, :], ACT.Exp).then_inc(gate_exp, 1)
                    if two.exists(IMAGES):
                        if chunk == 18:
                            if two.past(2):
                                act.wait_ge(attn_ready, two.back(2).done())
                            take(two, "pv0", heads_t[two.ring(2)][:, 0, :], bank("pv0")[:, 0:S])
                        if chunk == 29:
                            take(two, "pv1", heads_t[two.ring(2)][:, 1, :], bank("pv1")[:, 0:S])
                        act.wait_ge(key_made, two.done(CHUNKS, chunk + 1))
                        if chunk == 0 and two.past(1):
                            act.wait_ge(made["pv1"], two.back(1).done())
                        if chunk == 12 and two.past(1):
                            act.wait_ge(made["pv2"], two.back(1).done())
                        if chunk == 24:
                            act.wait_ge(made["pv0"], two.done())
                        h, g = chunk // GROUPS, chunk % GROUPS
                        buf = probs[(4 * two.ring(2) + h) % 8]
                        nc.scalar.activation(buf[:, g, :], ps[0:GROUP, 2 + chunk % 2, 0:S], ACT.Exp,
                                             scale=D ** -0.5).then_inc(exp_done, 1)

            iterations(act, body)

        @block.tensor
        def _(pe):
            pe.wait_ge(emb_ready, 1)
            for k in range(2):
                last = nc.tensor.matmul(ps[0:HALF, 7, k * EXPERTS:(k + 1) * EXPERTS],
                                        probe_w[:, k * HALF:(k + 1) * HALF], emb_t[:], start=True, stop=True)
            last.then_inc(align_made, 1)
            pe.wait_ge(setup_done, 1)

            def transposes(src, at, name):
                for g in range(GROUPS):
                    last = nc.tensor.transpose(bank(name)[0:HALF, g * GROUP:(g + 1) * GROUP], src(g),
                                               ident[0:GROUP, 0:GROUP])
                last.then_inc(made[name], 1)

            def product(at, name):
                r = at.ring(2)
                to = bank(name)
                if name in ("tok0", "tok1"):
                    g = int(name[3])
                    if g == 0:
                        pe.wait_ge(patches_in[at.ring(2)], at.uses(2, 16))
                    n = PIXELS // 128
                    for k in range(n):
                        last = nc.tensor.matmul(to[0:GROUP, 0:C], patches[r][:, k, g * GROUP:(g + 1) * GROUP],
                                                w_tok[:, k, :], start=(k == 0), stop=(k == n - 1))
                elif name in ("xt0", "xt1"):
                    k = int(name[2])
                    pe.wait_ge(xn_ready, at.done(GROUPS))
                    return transposes(lambda g: xn[:, g, k * HALF:(k + 1) * HALF], at, name)
                elif name in ("x2t0", "x2t1"):
                    k = int(name[3])
                    pe.wait_ge(xn2_ready, at.done(GROUPS))
                    return transposes(lambda g: rows[r][0][:, g, k * HALF:(k + 1) * HALF], at, name)
                elif name in ("qk0", "qk1", "qk2"):
                    m = int(name[2])
                    pe.wait_ge(taken["xt1"], at.done())
                    for k in range(2):
                        last = nc.tensor.matmul(to[:, 0:S], w_qkv[0:HALF + k, k, m * 128:(m + 1) * 128],
                                                xn_t[r][0:HALF + k, k, 0:S], start=(k == 0), stop=(k == 1))
                elif name in ("v01", "v2"):
                    groups = (0, 1) if name == "v01" else (2,)
                    for n, g in enumerate(groups):
                        for k in range(2):
                            last = nc.tensor.matmul(to[0:GROUP, n * C:(n + 1) * C],
                                                    xn_t[r][0:HALF + k, k, g * GROUP:(g + 1) * GROUP],
                                                    w_qkv[0:HALF + k, k, 2 * C:3 * C], start=(k == 0), stop=(k == 1))
                elif name in ("shift0", "shift1"):
                    half = int(name[5])
                    pe.wait_ge(shift_ready[half], at.done())
                    for g in range(GROUPS):
                        last = nc.tensor.transpose(to.bitcast(BF16)[:, g * GROUP:(g + 1) * GROUP], shift[half][:, g, :],
                                                   identb[0:GROUP, 0:GROUP])
                elif name in ("out01", "out2"):
                    groups = (0, 1) if name == "out01" else (2,)
                    pe.wait_ge(attn_ready, at.done())
                    for n, g in enumerate(groups):
                        for k in range(GROUPS):
                            last = nc.tensor.matmul(to[0:GROUP, n * C:(n + 1) * C],
                                                    attn_t[r][:, k, g * GROUP:(g + 1) * GROUP], w_out[:, k, :],
                                                    start=(k == 0), stop=(k == GROUPS - 1))
                elif name == "route":
                    pe.wait_ge(taken["x2t1"], at.done())
                    for g in range(GROUPS):
                        for k in range(2):
                            last = nc.tensor.matmul(to[0:GROUP, g * ROUTE:(g + 1) * ROUTE],
                                                    xn2_t[:, k, g * GROUP:(g + 1) * GROUP], w_route[:, k, :],
                                                    start=(k == 0), stop=(k == 1))
                elif name == "rank":
                    pe.wait_ge(chosen_ready, at.done())
                    rows_of = (GROUP, GROUP, TEXT)
                    for g in range(GROUPS):
                        dst = to[0:GROUP, g * EXPERTS:(g + 1) * EXPERTS]
                        n = rows_of[g]
                        nc.tensor.matmul(dst, before[0:n, :], chosen[0:n, g, :], start=True, stop=(g == 0))
                        for e in range(g):
                            nc.tensor.matmul(dst, ones[:], chosen[:, e, :], start=False, stop=(e == g - 1))
                    for g in range(GROUPS):
                        last = nc.tensor.matmul(to[0:GROUP, GROUPS * EXPERTS:(GROUPS + 1) * EXPERTS],
                                                ones[0:rows_of[g], :], chosen[0:rows_of[g], g, :],
                                                start=(g == 0), stop=(g == GROUPS - 1))
                elif name in ("pv0", "pv1", "pv2"):
                    g = int(name[2])
                    pe.wait_ge(exp_done, at.done(CHUNKS, 12 * (g + 1)))
                    if g == 0:
                        pe.wait_ge(taken["v2"], at.done())
                    for k in range(GROUPS):
                        n = TEXT if k == 2 else GROUP
                        for j in range(4):
                            h = 4 * g + j
                            last = nc.tensor.matmul(to[32 * j:32 * j + 32, 0:S], values[at.ring(4)][0:n, k, h, :],
                                                    probs[(4 * at.ring(2) + h) % 8][0:n, k, :],
                                                    start=(k == 0), stop=(k == GROUPS - 1), skip_group_check=True)
                last.then_inc(made[name], 1)

            def product_before(i, n):
                while True:
                    n -= MIX
                    if n < 0:
                        n, i = n + len(STEPS), i.back(1)
                        if i.loop is None and i.j < 0:
                            return None, None
                    name, at = STEPS[n][1], i.back(STEPS[n][2])
                    if at.exists(IMAGES):
                        return name, at

            def body(i):
                one, two = i.back(1), i.back(2)
                for chunk in range(CHUNKS):
                    h, g = chunk // GROUPS, chunk % GROUPS
                    for n, (before_chunk, name, lag) in enumerate(STEPS):
                        if before_chunk == chunk and i.back(lag).exists(IMAGES):
                            previous, image = product_before(i, n)
                            if previous:
                                pe.wait_ge(taken[previous], image.done())
                            product(i.back(lag), name)
                    if one.exists(IMAGES):
                        if chunk == 0:
                            pe.wait_ge(stack_in[one.ring(4)], one.uses(4, 160))
                        if positive(count := one.done(CHUNKS, chunk - 1)):
                            pe.wait_ge(max_taken, count)
                        st = stack[one.ring(4)]
                        nc.tensor.matmul(ps[0:GROUP, chunk % 2, 0:S],
                                         st[0:SCORE_ROWS, h, g * GROUP:(g + 1) * GROUP],
                                         st[0:SCORE_ROWS, HEADS + h, 0:S], start=True, stop=True
                                         ).then_inc(max_made, 1)
                    if two.exists(IMAGES):
                        if chunk in (0, CHUNKS // 2):
                            half = chunk // (CHUNKS // 2)
                            pe.wait_ge(shift_in[half], two.done(48))
                        if positive(count := two.done(CHUNKS, chunk - 1)):
                            pe.wait_ge(exp_done, count)
                        st = stack[two.ring(4)]
                        nc.tensor.matmul(ps[0:GROUP, 2 + chunk % 2, 0:S],
                                         st[:, HEADS + h, g * GROUP:(g + 1) * GROUP],
                                         st[:, h, 0:S], start=True, stop=True).then_inc(key_made, 1)

            iterations(pe, body)
        phase1.close()

        ends = kept("ends", [GROUP, EXPERTS], I32)
        many = kept("many", [GROUP, EXPERTS, MAXT])
        plan = kept("plan", [GROUP, 8, EXPERTS])
        cell = kept("cell", [GROUP, 6])
        table = kept("table", [GROUP, 2], I32)
        table_row = kept("table_row", [1, 2 * TILES], I32)
        w1 = [kept(f"w1_{r}", [HALF, 2, HID]) for r in range(2)]
        w2 = [kept(f"w2_{r}", [128, HCH, C]) for r in range(2)]
        b1 = [kept(f"b1_{r}", [128, HCH]) for r in range(2)]
        b2 = [kept(f"b2_{r}", [128, C]) for r in range(2)]
        x_row = [kept(f"x_row{r}", [128, 2, ROW]) for r in range(4)]
        x_t = [kept(f"x_t{r}", [HALF, 2, TILE]) for r in range(2)]
        relu = [kept(f"relu{r}", [128, TILE]) for r in range(4)]
        hidden = [kept(f"hidden{r}", [128, HCH, TILE]) for r in range(2)]
        y_bias = kept("y_bias", [128, 2, C])
        y_gated = [kept(f"y_gated{r}", [128, 2, C]) for r in range(2)]
        token_no = [kept(f"token_no{r}", [128, 2], I32) for r in range(2)]
        ps_xt = ps[0:HALF, 0, :].rearrange("p (k t) -> p k t", k=2)
        ps_hid = [ps[:, 1 + n, 0:TILE] for n in range(4)]
        ps_y = ps[:, 5:7, 0:C]

        w1_in, w2_in, b1_in, b2_in = (sems(n, 2) for n in ("w1_in", "w2_in", "b1_in", "b2_in"))
        x_in = sems("x_in", 4)
        xt_made, xt_taken = sem("xt_made"), sem("xt_taken")
        hid_made, relu_done, hid_ready = sem("hid_made"), sem("relu_done"), sem("hid_ready")
        y_made, y_taken, y_ready = sem("y_made"), sem("y_taken"), sem("y_ready")
        scattered = sem("scattered")

        block2 = ctx.enter_context(nc.Block())

        @block2.sync
        def _(sp):
            sp.wait_ge(ends_ready, 1)
            for e in range(EXPERTS):
                row = sp.value_load(ends[0:1, e:e + 1], min_val=e * CAP, max_val=e * CAP + N)
                sp.dma_start(rows_dram[bass.ds(row, TILE), :].rearrange("(p a) f -> p a f", a=2), empty[:]
                             ).then_inc(ends_out, 16)
            sp.dma_start(rows_dram[ZERO_ROW:ZERO_ROW + TILE, :].rearrange("(p a) f -> p a f", a=2), empty[:]
                         ).then_inc(ends_out, 16)
            sp.wait_ge(table_ready, 1)
            sp.dma_start(table_dram, table[0:TILES, :]).then_inc(table_out, 16)
            sp.wait_ge(table_out, 16)
            sp.dma_start(table_row[:], table_dram.rearrange("k n -> (k n)")[None, :]).then_inc(table_in, 16)
            sp.wait_ge(table_in, 16)
            sp.wait_ge(ends_out, 16 * (EXPERTS + 1))

            def body(at):
                if not at.exists(TILES):
                    return
                r, two = at.ring(2), at.back(2)
                e = sp.value_load(table_row[0:1, bass.ds(at.times(2), 1)], min_val=0, max_val=EXPERTS - 1)
                row = sp.value_load(table_row[0:1, bass.ds(at.times(2, 1), 1)], min_val=0, max_val=ZERO_ROW)
                if at.past(4):
                    sp.wait_ge(y_ready, at.back(4).done())
                alone(sp, sp_passed)
                sp.dma_start(x_row[at.ring(4)][:], rows_dram[bass.ds(row, TILE), :].rearrange("(p a) f -> p a f", a=2)
                             ).then_inc(x_in[at.ring(4)], 16)
                if at.past(2):
                    sp.wait_ge(relu_done, two.done(HCH))
                alone(sp, sp_passed)
                sp.dma_start(w1[r][:], w1_dram[bass.ds(e, 1)].rearrange("o (k p) h -> p (o k) h", p=HALF)
                             ).then_inc(w1_in[r], 16)
                sp.dma_start(b1[r][:], a["b1_t"][bass.ds(e, 1)].rearrange("o p j -> (o p) j")).then_inc(b1_in[r], 16)
                if at.past(2):
                    sp.wait_ge(y_taken, two.done())
                alone(sp, sp_passed)
                sp.dma_start(w2[r][:], w2_dram[bass.ds(e, 1)].rearrange("o (j p) c -> p (o j) c", p=128)
                             ).then_inc(w2_in[r], 16)
                sp.dma_start(b2[r][:], a["L0_ffn_b2"][bass.ds(e, 1)].rearrange("o c -> (o c)").partition_broadcast(128)
                             ).then_inc(b2_in[r], 16)

            tiles(sp, body)

        @block2.vector
        def _(dve):
            step = Counter()

            nc.vector.tensor_copy(ends[:], base[:]).then_inc(ends_ready, 1)
            t = slice(0, TILES)
            count, tiles_of, upto, behind, mine, first, part, ones8 = (plan[t, n, :] for n in range(8))
            nc.vector.memset(ones8, 1.0).then_inc(plan_chain, 1)
            dve.wait_ge(plan_chain, step.next())
            nc.vector.tensor_tensor(count, base[t, :], region[t, :], ALU.subtract).then_inc(plan_chain, 1)
            dve.wait_ge(plan_chain, step.next())
            shape = [TILES, EXPERTS, MAXT]
            nc.vector.tensor_tensor(many[t], count[:, :, None].broadcast_to(shape),
                                         steps256[t, None, :].broadcast_to(shape), ALU.is_gt).then_inc(plan_chain, 1)
            dve.wait_ge(plan_chain, step.next())
            nc.vector.tensor_reduce(tiles_of, many[t], AX, ALU.add).then_inc(plan_chain, 1)
            dve.wait_ge(plan_chain, step.next())
            nc.vector.tensor_tensor_scan(upto, ones8, tiles_of, 0.0, ALU.mult, ALU.add).then_inc(plan_chain, 1)
            dve.wait_ge(plan_chain, step.next())
            nc.vector.tensor_scalar(behind, upto, tile_no[t, 0:1], None, ALU.is_le).then_inc(plan_chain, 1)
            dve.wait_ge(plan_chain, step.next())
            nc.vector.tensor_reduce(cell[t, 0:1], behind, AX, ALU.add).then_inc(plan_chain, 1)
            dve.wait_ge(plan_chain, step.next())
            nc.vector.tensor_scalar(mine, ramp[t, :], float(EXPERTS), cell[t, 0:1], ALU.add, ALU.is_equal
                                    ).then_inc(plan_chain, 1)
            dve.wait_ge(plan_chain, step.next())
            nc.vector.tensor_tensor(first, tiles_of, upto, ALU.subtract).then_inc(plan_chain, 1)
            dve.wait_ge(plan_chain, step.next())
            nc.vector.scalar_tensor_tensor(first, first, float(TILE), region[t, :], ALU.mult, ALU.add
                                           ).then_inc(plan_chain, 1)
            dve.wait_ge(plan_chain, step.next())
            nc.vector.tensor_tensor(part, mine, first, ALU.mult).then_inc(plan_chain, 1)
            dve.wait_ge(plan_chain, step.next())
            nc.vector.tensor_reduce(cell[t, 1:2], part, AX, ALU.add).then_inc(plan_chain, 1)
            dve.wait_ge(plan_chain, step.next())
            nc.vector.tensor_reduce(cell[t, 2:3], mine, AX, ALU.add).then_inc(plan_chain, 1)
            dve.wait_ge(plan_chain, step.next())
            nc.vector.tensor_tensor(part, mine, ramp[t, :], ALU.mult).then_inc(plan_chain, 1)
            dve.wait_ge(plan_chain, step.next())
            nc.vector.tensor_reduce(cell[t, 3:4], part, AX, ALU.add).then_inc(plan_chain, 1)
            dve.wait_ge(plan_chain, step.next())
            nc.vector.scalar_tensor_tensor(cell[t, 4:5], cell[t, 2:3], tile_no[t, 1:2], cell[t, 1:2],
                                                ALU.mult, ALU.add).then_inc(plan_chain, 1)
            dve.wait_ge(plan_chain, step.next())
            nc.vector.tensor_scalar(table[t, 1:2], cell[t, 4:5], float(ZERO_ROW), None, ALU.add
                                    ).then_inc(plan_chain, 1)
            dve.wait_ge(plan_chain, step.next())
            nc.vector.scalar_tensor_tensor(table[t, 0:1], cell[t, 2:3], float(EXPERTS), cell[t, 3:4],
                                           ALU.mult, ALU.add).then_inc(table_ready, 1)

            def square(at):
                for j in range(HCH):
                    dve.wait_ge(relu_done, at.done(HCH, j + 1))
                    if j == 0:
                        if at.past(2):
                            dve.wait_ge(y_made, at.back(2).done())
                    rl = relu[(2 * at.ring(2) + j) % 4]
                    nc.vector.tensor_tensor(hidden[at.ring(2)][:, j, :], rl[:], rl[:], ALU.mult
                                            ).then_inc(hid_ready, 1)

            def output(at):
                r = at.ring(2)
                dve.wait_ge(b2_in[at.ring(2)], at.uses(2, 16))
                dve.wait_ge(y_made, at.done())
                if at.past(1):
                    dve.wait_ge(y_ready, at.back(1).done())
                nc.vector.tensor_tensor(y_bias[:], ps_y, b2[r][:, None, :].broadcast_to([128, 2, C]), ALU.add
                                        ).then_inc(y_taken, 1)
                dve.wait_ge(y_taken, at.done())
                if at.past(2):
                    dve.wait_ge(scattered, at.back(2).done(32))
                nc.vector.tensor_copy(token_no[r][:], x_row[at.ring(4)][:, :, C])
                for half in range(2):
                    last = nc.vector.tensor_scalar(y_gated[r][:, half, :], y_bias[:, half, :],
                                                   x_row[at.ring(4)][:, half, C + 1:C + 2], None, ALU.mult)
                last.then_inc(y_ready, 1)

            def body(at):
                if at.exists(TILES):
                    square(at)
                if at.back(1).exists(TILES):
                    output(at.back(1))

            tiles(dve, body)

        @block2.scalar
        def _(act):
            def rows_t(at):
                if at.past(2):
                    act.wait_ge(hid_made, at.back(2).done(HCH))
                act.wait_ge(xt_made, at.done())
                nc.scalar.activation(x_t[at.ring(2)][:], ps_xt, ACT.Copy).then_inc(xt_taken, 1)

            def body(at):
                if at.loop is None and at.j == 0:
                    rows_t(at)
                if at.exists(TILES):
                    act.wait_ge(b1_in[at.ring(2)], at.uses(2, 16))
                    for j in range(HCH):
                        act.wait_ge(hid_made, at.done(HCH, j + 1))
                        if positive(count := at.done(HCH, j - 3)):
                            act.wait_ge(hid_ready, count)
                        nc.scalar.activation(relu[(2 * at.ring(2) + j) % 4][:], ps_hid[(2 * at.ring(2) + j) % 4],
                                             ACT.Relu, bias=b1[at.ring(2)][:, j:j + 1]).then_inc(relu_done, 1)
                if at.back(-1).exists(TILES):
                    rows_t(at.back(-1))

            tiles(act, body)

        @block2.tensor
        def _(pe):
            def rows_t(at):
                r = at.ring(2)
                pe.wait_ge(x_in[at.ring(4)], at.uses(4, 16))
                if at.past(1):
                    pe.wait_ge(xt_taken, at.back(1).done())
                for k in range(2):
                    for half in range(2):
                        last = nc.tensor.transpose(ps_xt[:, k, half * 128:(half + 1) * 128],
                                                   x_row[at.ring(4)][:, half, k * HALF:(k + 1) * HALF], ident[:])
                last.then_inc(xt_made, 1)

            def hidden_layer(at):
                r = at.ring(2)
                pe.wait_ge(w1_in[at.ring(2)], at.uses(2, 16))
                pe.wait_ge(xt_taken, at.done())
                for j in range(HCH):
                    if positive(count := at.done(HCH, j - 3)):
                        pe.wait_ge(relu_done, count)
                    for k in range(2):
                        last = nc.tensor.matmul(ps_hid[(2 * r + j) % 4], w1[r][:, k, j * 128:(j + 1) * 128],
                                                x_t[r][:, k, :], start=(k == 0), stop=(k == 1))
                    last.then_inc(hid_made, 1)

            def output(at):
                r = at.ring(2)
                pe.wait_ge(w2_in[at.ring(2)], at.uses(2, 16))
                pe.wait_ge(hid_ready, at.done(HCH))
                if at.past(1):
                    pe.wait_ge(y_taken, at.back(1).done())
                for half in range(2):
                    for j in range(HCH):
                        last = nc.tensor.matmul(ps_y[:, half, :], hidden[r][:, j, half * 128:(half + 1) * 128],
                                                w2[r][:, j, :], start=(j == 0), stop=(j == HCH - 1))
                last.then_inc(y_made, 1)

            def body(at):
                if at.loop is None and at.j == 0:
                    rows_t(at)
                if at.exists(TILES):
                    hidden_layer(at)
                if at.back(-1).exists(TILES):
                    rows_t(at.back(-1))
                if at.back(1).exists(TILES):
                    output(at.back(1))

            tiles(pe, body)

        @block2.gpsimd
        def _(pool):
            def body(at):
                if not at.back(1).exists(TILES):
                    return
                at = at.back(1)
                if at.past(1):
                    pool.wait_ge(scattered, at.back(1).done(32))
                pool.wait_ge(y_ready, at.done())
                alone(pool, pool_passed)
                for half in range(2):
                    pool.indirect_dma_start(
                        out_rows, bass.IndirectOffsetOnAxis(ap=token_no[at.ring(2)][:, half:half + 1], axis=0),
                        y_gated[at.ring(2)][:, half, :], None, bounds_check=N - 1, oob_is_err=False,
                        compute_op=ALU.add).then_inc(scattered, 16)

            tiles(pool, body)
            pool.wait_ge(scattered, 32 * TILES)


def kernel(**inputs):
    import numpy as np
    import concourse.bacc as bacc
    from concourse.bass_utils import run_bass_kernel_spmd
    import ml_dtypes

    x = {k: np.ascontiguousarray(v) for k, v in inputs.items()}
    images = x.pop("x")
    side = 14
    px = images.shape[2] // side
    arrays = {
        "patches": images.reshape(IMAGES, 3, side, px, side, px).transpose(0, 1, 3, 5, 2, 4).reshape(
            IMAGES, PIXELS, PATCHES),
        "txt": x["txt"],
        "w_tok_t": x["L0_tok_W"].T,
        "L0_tok_b": x["L0_tok_b"],
        "w_qkv_t": x["L0_attn_w_qkv"].T,
        "L0_attn_b_qkv": x["L0_attn_b_qkv"],
        "w_out_t": x["L0_attn_w_out"].T,
        "L0_attn_b_out": x["L0_attn_b_out"],
        "router_t": x["L0_ffn_router_w"].T,
        "probe_t": x["L0_ffn_probe_w"].T,
        "L0_ffn_probe_w": x["L0_ffn_probe_w"],
        "L0_ffn_router_emb": x["L0_ffn_router_emb"],
        "emb_t": x["L0_ffn_router_emb"].T,
        "b1_t": x["L0_ffn_b1"].reshape(EXPERTS, HCH, 128).transpose(0, 2, 1),
        "L0_ffn_b2": x["L0_ffn_b2"],
        "m_gate1_rows": np.repeat(x["L0_ffn_m_gate1"], 128 // EXPERTS)[:, None],
        "m_gate2_rows": np.repeat(x["L0_ffn_m_gate2"], 128 // EXPERTS)[:, None],
        "ident": np.eye(128, dtype=np.float32),
        "identb": np.eye(128, dtype=ml_dtypes.bfloat16),
        "before": np.triu(np.ones((GROUP, GROUP)), 1).astype(ml_dtypes.bfloat16),
        "ramp": np.arange(EXPERTS, dtype=np.float32) - EXPERTS,
        "region": np.arange(EXPERTS, dtype=np.float32) * CAP,
        "steps256": np.arange(MAXT, dtype=np.float32) * TILE,
        "place0": (np.arange(GROUPS)[None, :] * GROUP + np.arange(GROUP)[:, None]).astype(np.float32),
        "tile_no": np.stack([np.arange(GROUP), np.arange(GROUP) * TILE - ZERO_ROW], 1).astype(np.float32),
    }
    for n in ("fatigue", "energy", "w_fast1", "w_slow1", "h_fast1", "w_fast2", "w_slow2", "h_fast2"):
        arrays[f"L0_ffn_{n}"] = x[f"L0_ffn_{n}"]
    arrays = {k: np.ascontiguousarray(v) for k, v in arrays.items()}
    nc = bacc.Bacc("TRN2", target_bir_lowering=False, num_devices=1)
    aps = {k: nc.dram_tensor(f"in_{k}", v.shape, mybir.dt.from_np(v.dtype), kind="ExternalInput").ap()
           for k, v in arrays.items()}
    out = nc.dram_tensor("out", (IMAGES, S, C), F32, kind="ExternalOutput").ap()
    build(nc, aps, out)
    r = run_bass_kernel_spmd(nc, [{f"in_{k}": v for k, v in arrays.items()}], core_ids=[0])
    return r.results[0]["out"]
```

```python
from contextlib import ExitStack

import concourse.bass as bass
from concourse import mybir

F32 = mybir.dt.float32
BF16 = mybir.dt.bfloat16
I32 = mybir.dt.int32
ALU = mybir.AluOpType
ACT = mybir.ActivationFunctionType
AX = mybir.AxisListType.X

IMAGES, PATCHES, TEXT, PIXELS = 32, 196, 77, 768
C, HEADS, D = 192, 12, 16
S = PATCHES + TEXT
GROUP = PATCHES // 2
GROUPS = 3
PAD = GROUP * GROUPS
HALF = C // 2
N = IMAGES * S
EXPERTS, HID, PROBE = 8, 768, 24
LN_EPS = 1e-5
TERMS = [(0, 0), (1, 1), (0, 1), (1, 0), (0, 2), (2, 0)]
SCORE_ROWS = D * len(TERMS)
SHIFT_ROWS = 3
ROUTE = EXPERTS + PROBE + EXPERTS + 1
TILE = 256
TOPK = 2
TILES = (TOPK * N - EXPERTS) // TILE + EXPERTS
CAP = N + TILE
ZERO_ROW = EXPERTS * CAP
ROW = C + 2
NO_TOKEN = float(N)
WCOLS = EXPERTS * C * HID // (128 * IMAGES)
HCH = HID // 128
MAXT = (N + TILE - 1) // TILE


class At:

    def __init__(self, loop, j, unroll):
        self.loop, self.j, self.unroll = loop, j, unroll

    def back(self, k):
        return At(self.loop, self.j - k, self.unroll)

    def ring(self, n):
        return self.j % n

    def exists(self, limit):
        return self.loop is not None or 0 <= self.j < limit

    def past(self, k):
        return self.loop is not None or self.j >= k

    def times(self, per, plus=0):
        if self.loop is None:
            return per * self.j + plus
        return self.loop * (per * self.unroll) + (per * self.j + plus)

    def done(self, per=1, n=None):
        return self.times(per, per if n is None else n)

    def uses(self, n, per):
        if self.loop is None:
            return (self.j // n + 1) * per
        return self.loop * (self.unroll // n * per) + (self.j // n + 1) * per


def positive(count):
    return not isinstance(count, int) or count > 0


def alone(eng, passed):
    eng.sem_inc(passed, 1)


class Counter:

    def __init__(self, per=0):
        self.per, self.at, self.k = per, At(None, 0, 1), 0

    def start(self, at, k=0):
        self.at, self.k = at, k

    def next(self):
        self.k += 1
        assert not self.per or self.k <= self.per
        return self.at.times(self.per, self.k)


CHUNKS = HEADS * GROUPS
STEPS = [
    (0, "tok1", 0, 3), (3, "pv2", 3, 3), (5, "x2t0", 4, 1), (6, "x2t1", 4, 1), (8, "route", 4, 3),
    (9, "shift1", 2, 1), (11, "xt0", 0, 1), (11, "xt1", 0, 1), (13, "qk0", 0, 2), (15, "qk1", 0, 2),
    (17, "qk2", 0, 2), (19, "pv0", 2, 3), (21, "v01", 0, 2), (23, "v2", 0, 1), (24, "shift0", 1, 1),
    (25, "out01", 3, 3), (28, "out2", 3, 1), (29, "rank", 4, 1), (29, "pv1", 2, 3), (32, "tok0", -1, 3),
]
MIX = 4
assert len(STEPS) % MIX == 0
NAMES = [name for _, name, _, _ in STEPS]
LAST_LAG = 5
ITERATIONS = IMAGES + LAST_LAG
UNROLL = 4
LOOP_FROM, LOOP_TIMES = 5, 6
TILES_FROM = 5
TILES_TIMES = (TILES - TILES_FROM) // UNROLL


def iterations(eng, body):
    for i in range(LOOP_FROM):
        body(At(None, i, UNROLL))
    with eng.Fori(0, LOOP_TIMES, 1) as loop:
        for j in range(UNROLL):
            body(At(loop, LOOP_FROM + j, UNROLL))
    for i in range(LOOP_FROM + UNROLL * LOOP_TIMES, ITERATIONS):
        body(At(None, i, UNROLL))


def tiles(eng, body):
    for k in range(TILES_FROM):
        body(At(None, k, UNROLL))
    with eng.Fori(0, TILES_TIMES, 1) as loop:
        for j in range(UNROLL):
            body(At(loop, TILES_FROM + j, UNROLL))
    for k in range(TILES_FROM + UNROLL * TILES_TIMES, TILES + 1):
        body(At(None, k, UNROLL))


def build(nc, a, out):
    ctx = ExitStack()
    with ctx:
        phase1 = ExitStack()

        def kept(name, shape, dt=F32):
            return ctx.enter_context(nc.sbuf_tensor(name, shape, dt))

        def sb(name, shape, dt=F32):
            return phase1.enter_context(nc.sbuf_tensor(name, shape, dt))

        def sem(name):
            return ctx.enter_context(nc.semaphore(name))

        def sems(name, n):
            return [sem(f"{name}{i}") for i in range(n)]

        qk_dram = nc.dram_tensor("qk_parts", (2, 3, 2 * C, S), BF16).ap()
        den_dram = nc.dram_tensor("denominators", (2, 4, GROUPS, S), F32).ap()
        rden_dram = nc.dram_tensor("inverse_denominators", (2, 4, GROUPS, S), F32).ap()
        rows_dram = nc.dram_tensor("expert_rows", (ZERO_ROW + TILE, ROW), F32).ap()
        w1_dram = nc.dram_tensor("w1", (EXPERTS, C, HID), F32).ap()
        w2_dram = nc.dram_tensor("w2", (EXPERTS, HID, C), F32).ap()
        table_dram = nc.dram_tensor("tile_table", (TILES, 2), I32).ap()
        out_rows = out.rearrange("b s c -> (b s) c")

        ident = kept("ident", [128, 128])
        ramp = kept("ramp", [GROUP, EXPERTS])
        region = kept("region", [GROUP, EXPERTS])
        steps256 = kept("steps256", [GROUP, MAXT])
        tile_no = kept("tile_no", [GROUP, 2])
        base = kept("base", [GROUP, EXPERTS])
        empty = kept("empty", [128, 2, ROW])
        ends = kept("ends", [GROUP, EXPERTS], I32)
        many = kept("many", [GROUP, EXPERTS, MAXT])
        plan = kept("plan", [GROUP, 8, EXPERTS])
        cell = kept("cell", [GROUP, 6])
        table = kept("table", [GROUP, 2], I32)
        table_row = kept("table_row", [1, 2 * TILES], I32)

        identb = sb("identb", [128, 128], BF16)
        before = sb("before", [GROUP, GROUP], BF16)
        ones = sb("ones", [GROUP, GROUP], BF16)
        place0 = sb("place0", [GROUP, GROUPS])
        half_neg = sb("half_neg", [GROUP, GROUPS])
        half_pos = sb("half_pos", [GROUP, EXPERTS])
        w_tok = sb("w_tok", [128, PIXELS // 128, C])
        b_tok = sb("b_tok", [GROUP, C])
        w_qkv = sb("w_qkv", [HALF + 1, 2, 3 * C])
        w_out = sb("w_out", [128, GROUPS, C])
        w_route = sb("w_route", [HALF, 2, ROUTE])
        probe_w = sb("probe_w", [PROBE, C])
        emb_t = sb("emb_t", [PROBE, EXPERTS])
        emb_all = sb("emb_all", [GROUP, EXPERTS, PROBE])
        emb_sq = sb("emb_sq", [GROUP, EXPERTS, PROBE])
        gain = sb("gain", [GROUP, 4, EXPERTS])
        fatigue = sb("fatigue", [GROUP, EXPERTS])
        energy = sb("energy", [GROUP, EXPERTS])
        bias8 = sb("bias8", [GROUP, EXPERTS])
        m_gate = sb("m_gate", [128, 2])

        patches = [sb(f"patches{r}", [128, PIXELS // 128, PATCHES]) for r in range(2)]
        resid = [sb(f"resid{r}", [GROUP, GROUPS, C]) for r in range(4)]
        stats = [sb(f"stats{r}", [GROUP, GROUPS, 6]) for r in range(2)]
        mean_var = [sb(f"mean_var{r}", [GROUP, GROUPS, 2]) for r in range(2)]
        var_eps = [sb(f"var_eps{r}", [GROUP, GROUPS]) for r in range(2)]
        rstd = [sb(f"rstd{r}", [GROUP, GROUPS]) for r in range(2)]
        minus_mean = [sb(f"minus_mean{r}", [GROUP, 2, GROUPS]) for r in range(2)]
        xn = sb("xn", [GROUP, GROUPS, C])
        xn_t = [sb(f"xn_t{r}", [HALF + 1, 2, PAD]) for r in range(2)]
        parts = [sb(f"parts{r}", [128, 9, S], BF16) for r in range(2)]
        rest = sb("rest", [128, 3, S])
        stack = [sb(f"stack{r}", [SCORE_ROWS + SHIFT_ROWS, 2 * HEADS, PAD], BF16) for r in range(4)]
        values = [sb(f"values{r}", [GROUP, GROUPS, HEADS, 32]) for r in range(4)]
        maxima = sb("maxima", [GROUP, GROUPS, HEADS])
        shift = [sb(f"shift{r}", [GROUP, GROUPS, 128], BF16) for r in range(2)]
        shift_rest = [sb(f"shift_rest{r}", [GROUP, GROUPS, 6]) for r in range(2)]
        shift_t = [sb(f"shift_t{r}", [18, S], BF16) for r in range(2)]
        probs = [sb(f"probs{r}", [GROUP, GROUPS, S]) for r in range(8)]
        heads_t = [sb(f"heads_t{r}", [128, GROUPS, S]) for r in range(2)]
        den = sb("den", [126, 26])
        rden = sb("rden", [126, 26])
        rden_all = [sb(f"rden_all{r}", [128, GROUPS, S]) for r in range(2)]
        attn_t = [sb(f"attn_t{r}", [128, GROUPS, PAD]) for r in range(2)]
        h2 = [sb(f"h2{r}", [GROUP, GROUPS, C]) for r in range(2)]
        rows = [[sb(f"rows{r}{k}", [GROUP, GROUPS, ROW]) for k in range(2)] for r in range(2)]
        xn2_t = sb("xn2_t", [HALF, 2, PAD])
        routed = sb("routed", [GROUP, GROUPS, ROUTE])
        sq = sb("sq", [GROUP, GROUPS, PROBE])
        nrm = sb("nrm", [GROUP, 4, GROUPS])
        logit = sb("logit", [GROUP, GROUPS, EXPERTS])
        align = sb("align", [GROUP, GROUPS, EXPERTS])
        tmp8 = sb("tmp8", [GROUP, GROUPS, EXPERTS])
        masked = sb("masked", [GROUP, GROUPS, EXPERTS])
        top = sb("top", [GROUP, 2, GROUPS])
        pick = sb("pick", [GROUP, 2, GROUPS])
        hot = sb("hot", [GROUP, 2, GROUPS * EXPERTS])
        chosen = sb("chosen", [GROUP, GROUPS, EXPERTS], BF16)
        gates = [sb(f"gates{r}", [GROUP, 5, GROUPS]) for r in range(2)]
        token = sb("token", [GROUP, GROUPS])
        pos = sb("pos", [GROUP, GROUPS * EXPERTS])
        pos2 = sb("pos2", [GROUP, 2, GROUPS * EXPERTS])
        posf = sb("posf", [GROUP, 2 * GROUPS])
        posi = [sb(f"posi{r}", [GROUP, 2 * GROUPS], I32) for r in range(2)]
        w_in = [[sb(f"w_in{r}{k}", [128, WCOLS]) for k in range(6)] for r in range(1)]
        w_sum = [[sb(f"w_sum{r}{k}", [128, WCOLS]) for k in range(2)] for r in range(1)]

        ps = ctx.enter_context(nc.psum_tensor("ps", [128, 8, 512], F32))

        def bank(name):
            return ps[:, 4 + NAMES.index(name) % MIX, :]

        made = {name: sem(f"made_{name}") for name in NAMES}
        taken = {name: sem(f"taken_{name}") for name in NAMES}
        first_in = sem("first_in")
        const_in = sem("const_in")
        sp_passed, pool_passed, dve_passed = sem("sp_passed"), sem("pool_passed"), sem("dve_passed")
        weights_zeroed = sem("weights_zeroed")
        route_w_in = sem("route_w_in")
        stack_padded = sem("stack_padded")
        bias_row_ready = sem("bias_row_ready")
        setup_chain = sem("setup_chain")
        gain_sq = sem("gain_sq")
        gain_root = sem("gain_root")
        emb_ready = sem("emb_ready")
        align_made = sem("align_made")
        setup_done = sem("setup_done")
        pool_setup = sem("pool_setup")
        pads_zeroed = sem("pads_zeroed")
        patches_in = sems("patches_in", 2)
        text_in = sems("text_in", 2)
        stats_chain = sem("stats_chain")
        stats_ready = sem("stats_ready")
        rstd_chain = sem("rstd_chain")
        rstd_ready = sem("rstd_ready")
        xn_ready = sem("xn_ready")
        part1_ready = sem("part1_ready")
        part2_ready = sem("part2_ready")
        part3_ready = sem("part3_ready")
        parts_out = sems("parts_out", 2)
        stack_in = sems("stack_in", 4)
        max_made = sem("max_made")
        max_taken = sem("max_taken")
        shift_chain = sems("shift_chain", 2)
        shift_ready = sems("shift_ready", 2)
        shift_in = sems("shift_in", 2)
        key_made = sem("key_made")
        exp_done = sem("exp_done")
        den_out = sem("den_out")
        den_in = sem("den_in")
        den_inverse = sem("den_inverse")
        rden_out = sem("rden_out")
        rden_in = sems("rden_in", 2)
        attn_ready = sem("attn_ready")
        h2_out = sems("h2_out", 2)
        stats2_chain = sem("stats2_chain")
        stats2_ready = sem("stats2_ready")
        rstd2_chain = sem("rstd2_chain")
        rstd2_ready = sem("rstd2_ready")
        xn2_ready = sem("xn2_ready")
        row_copied = sem("row_copied")
        row_marked = sem("row_marked")
        norm2_ready = sem("norm2_ready")
        norm_ready = sem("norm_ready")
        route_chain = sem("route_chain")
        chosen_ready = sem("chosen_ready")
        top_gap = sem("top_gap")
        gate_exp = sem("gate_exp")
        gate_sum = sem("gate_sum")
        gate_inv = sem("gate_inv")
        gate_chain = sem("gate_chain")
        place_chain = sem("place_chain")
        pos_ready = sem("pos_ready")
        rows_out = sems("rows_out", 2)
        w_loaded = sem("w_loaded")
        w_chain = sem("w_chain")
        w_scaled = sem("w_scaled")
        w_summed = sem("w_summed")
        w_stored = sem("w_stored")
        empty_ready = sem("empty_ready")
        empty_out = sem("empty_out")
        plan_chain = sem("plan_chain")
        ends_ready = sem("ends_ready")
        table_ready = sem("table_ready")
        table_out = sem("table_out")
        table_in = sem("table_in")
        ends_out = sem("ends_out")

        CONSTS = 27
        FILLS = 8
        flat_w = {}
        for k, n in enumerate(("w_fast", "w_slow", "h_fast")):
            for layer in range(2):
                flat_w[layer, k] = a[f"L0_ffn_{n}{layer + 1}"].rearrange("e a b -> (e a b)").rearrange(
                    "(p f) -> p f", p=128)
        w1_flat = w1_dram.rearrange("e a b -> (e a b)").rearrange("(p f) -> p f", p=128)
        w2_flat = w2_dram.rearrange("e a b -> (e a b)").rearrange("(p f) -> p f", p=128)
        image_in = a["patches"].rearrange("b (k p) t -> b p k t", p=128)

        block = phase1.enter_context(nc.Block())

        @block.sync
        def _(sp):
            loads = [0]

            def load(dst, src, signal=const_in):
                if signal is const_in:
                    loads[0] += 1
                sp.dma_start(dst, src).then_inc(signal, 16)

            def image_loads(at):
                if at.past(2):
                    sp.wait_ge(made["tok1"], at.back(2).done())
                src = image_in[at.j] if at.loop is None else image_in[bass.ds(at.times(1), 1)].rearrange(
                    "b p k t -> (b p) k t")
                sp.dma_start(patches[at.ring(2)][:], src).then_inc(patches_in[at.ring(2)], 16)

            def text_load(at):
                if at.past(4):
                    sp.wait_ge(taken["out2"], at.back(4).done())
                src = a["txt"][at.j] if at.loop is None else a["txt"][bass.ds(at.times(1), 1)].rearrange(
                    "b t c -> (b t) c")
                sp.dma_start(resid[at.ring(4)][0:TEXT, 2, :], src).then_inc(text_in[at.ring(2)], 16)

            def weight_loads(at):
                if at.past(1):
                    sp.wait_ge(w_summed, at.back(1).done(2))
                for layer in range(2):
                    for k in range(3):
                        sp.dma_start(w_in[0][3 * layer + k][:],
                                     flat_w[layer, k][:, bass.ds(at.times(WCOLS), WCOLS)]).then_inc(w_loaded, 16)

            load(w_tok[:], a["w_tok_t"].rearrange("(k p) h -> p k h", p=128), first_in)
            image_loads(At(None, 0, UNROLL))
            load(b_tok[:], a["L0_tok_b"].partition_broadcast(GROUP), first_in)
            sp.wait_ge(pads_zeroed, 4)
            text_load(At(None, 0, UNROLL))
            load(ident[:], a["ident"])
            image_loads(At(None, 1, UNROLL))
            load(identb[:], a["identb"])
            load(before[:], a["before"])
            load(w_qkv[0:HALF, :, :], a["w_qkv_t"].rearrange("(k p) n -> p k n", p=HALF))
            load(w_qkv[HALF:HALF + 1, 1, :], a["L0_attn_b_qkv"][None, :])
            load(ramp[:], a["ramp"].partition_broadcast(GROUP))
            load(region[:], a["region"].partition_broadcast(GROUP))
            load(steps256[:], a["steps256"].partition_broadcast(GROUP))
            load(place0[:], a["place0"])
            load(tile_no[:], a["tile_no"])
            load(base[:], a["region"].partition_broadcast(GROUP))
            load(emb_all[:].rearrange("p e d -> p (e d)"),
                 a["L0_ffn_router_emb"].rearrange("e d -> (e d)").partition_broadcast(GROUP))
            load(emb_t[:], a["emb_t"])
            load(probe_w[:], a["L0_ffn_probe_w"])
            load(fatigue[:], a["L0_ffn_fatigue"].partition_broadcast(GROUP))
            load(energy[:], a["L0_ffn_energy"].partition_broadcast(GROUP))
            sp.wait_ge(weights_zeroed, 1)
            load(w_out[D:D + 1, 0, :], a["L0_attn_b_out"][None, :])
            for j in range(4):
                load(w_out[32 * j:32 * j + D, :, :],
                     a["w_out_t"].rearrange("(g j r) n -> j r g n", j=4, r=D)[j])
            for layer in range(2):
                load(m_gate[:, layer:layer + 1], a[f"m_gate{layer + 1}_rows"])
            for k in range(2):
                load(w_route[:, k, 0:EXPERTS], a["router_t"][k * HALF:(k + 1) * HALF, :])
                load(w_route[:, k, EXPERTS:EXPERTS + PROBE], a["probe_t"][k * HALF:(k + 1) * HALF, :])
            assert loads[0] == CONSTS, loads
            text_load(At(None, 1, UNROLL))
            weight_loads(At(None, 0, UNROLL))

            def shift_rows(at, half):
                sp.wait_ge(taken[f"shift{half}"], at.done())
                for k in range(SHIFT_ROWS):
                    row = SCORE_ROWS + k
                    sp.dma_start(stack[at.ring(4)][row:row + 1, 6 * half:6 * half + 6, 0:S],
                                 shift_t[half][6 * k:6 * k + 6, :]).then_inc(shift_in[half], 16)

            def denominators(at):
                r = at.ring(2)
                for g in range(GROUPS):
                    sp.wait_ge(taken[f"pv{g}"], at.done())
                sp.dma_start(den_dram[r], heads_t[r][D:128:32, :, :]).then_inc(den_out, 16)
                sp.wait_ge(den_out, at.done(16))
                sp.dma_start(den[:], den_dram[r].rearrange("j g t -> (j g t)").rearrange(
                    "(p f) -> p f", p=126)).then_inc(den_in, 16)

            def inverses(at):
                r = at.ring(2)
                sp.wait_ge(den_inverse, at.done())
                sp.dma_start(rden_dram[r].rearrange("j g t -> (j g t)").rearrange("(p f) -> p f", p=126),
                             rden[:]).then_inc(rden_out, 16)
                sp.wait_ge(rden_out, at.done(16))
                for j in range(4):
                    sp.dma_start(rden_all[r][32 * j:32 * j + D + 1, :, :].rearrange("p g t -> p (g t)"),
                                 rden_dram[r, j].rearrange("g t -> (g t)").partition_broadcast(D + 1)
                                 ).then_inc(rden_in[r], 16)

            def parts_store(at):
                r = at.ring(2)
                sp.wait_ge(part3_ready, at.done(3))
                if at.loop is None and at.j == 0:
                    sp.wait_ge(stack_padded, 1)
                alone(sp, sp_passed)
                if at.past(2):
                    sp.wait_ge(stack_in[at.back(2).ring(4)], at.back(2).uses(4, 160))
                alone(sp, sp_passed)
                sp.dma_start(qk_dram[r].rearrange("a (m p) t -> p (a m) t", p=128), parts[r][:]
                             ).then_inc(parts_out[r], 16)

            def stack_loads(at):
                r = at.ring(2)
                sp.wait_ge(parts_out[at.ring(2)], at.uses(2, 16))
                alone(sp, sp_passed)
                if at.past(4):
                    sp.wait_ge(key_made, at.back(4).done(CHUNKS))
                view = qk_dram[r].rearrange("a (h d) t -> a d h t", d=D)
                for t, (q_part, k_part) in enumerate(TERMS):
                    dst = stack[at.ring(4)][D * t:D * t + D, :, 0:S]
                    if q_part == k_part:
                        sp.dma_start(dst, view[q_part]).then_inc(stack_in[at.ring(4)], 16)
                    else:
                        sp.dma_start(dst[:, 0:HEADS, :], view[q_part][:, 0:HEADS, :]
                                     ).then_inc(stack_in[at.ring(4)], 16)
                        sp.dma_start(dst[:, HEADS:, :], view[k_part][:, HEADS:, :]
                                     ).then_inc(stack_in[at.ring(4)], 16)

            def h2_store(at):
                sp.wait_ge(taken["out2"], at.done())
                sp.wait_ge(taken["out01"], at.done())
                r = at.ring(2)
                dst = out[at.j] if at.loop is None else out[bass.ds(at.times(1), 1)].rearrange("b s c -> (b s) c")
                sp.dma_start(dst[0:PATCHES, :].rearrange("(g p) c -> p g c", p=GROUP), h2[r][:, 0:2, :]
                             ).then_inc(h2_out[r], 16)
                sp.dma_start(dst[PATCHES:S, :], h2[r][0:TEXT, 2, :]).then_inc(h2_out[r], 16)

            def weight_stores(at):
                sp.wait_ge(w_summed, at.done(2))
                for layer, flat in enumerate((w1_flat, w2_flat)):
                    sp.dma_start(flat[:, bass.ds(at.times(WCOLS), WCOLS)], w_sum[0][layer][:]
                                 ).then_inc(w_stored, 16)

            def body(i):
                if i.back(3).exists(IMAGES):
                    denominators(i.back(3))
                if i.loop is not None or 2 <= i.j + 1 < IMAGES:
                    image_loads(i.back(-1))
                if i.back(2).exists(IMAGES):
                    shift_rows(i.back(2), 1)
                if i.back(3).exists(IMAGES):
                    inverses(i.back(3))
                if i.exists(IMAGES):
                    parts_store(i)
                if i.back(1).exists(IMAGES):
                    shift_rows(i.back(1), 0)
                if i.exists(IMAGES):
                    stack_loads(i)
                if i.back(3).exists(IMAGES):
                    h2_store(i.back(3))
                if i.loop is not None or 2 <= i.j + 1 < IMAGES:
                    text_load(i.back(-1))
                if i.exists(IMAGES):
                    weight_stores(i)
                    if i.loop is not None or i.j + 1 < IMAGES:
                        weight_loads(i.back(-1))

            iterations(sp, body)
            sp.wait_ge(ends_ready, 1)
            for e in range(EXPERTS):
                row = sp.value_load(ends[0:1, e:e + 1], min_val=e * CAP, max_val=e * CAP + N)
                sp.dma_start(rows_dram[bass.ds(row, TILE), :].rearrange("(p a) f -> p a f", a=2), empty[:]
                             ).then_inc(ends_out, 16)
            sp.dma_start(rows_dram[ZERO_ROW:ZERO_ROW + TILE, :].rearrange("(p a) f -> p a f", a=2), empty[:]
                         ).then_inc(ends_out, 16)
            sp.wait_ge(table_ready, 1)
            sp.dma_start(table_dram, table[0:TILES, :]).then_inc(table_out, 16)
            sp.wait_ge(table_out, 16)
            sp.dma_start(table_row[:], table_dram.rearrange("k n -> (k n)")[None, :]).then_inc(table_in, 16)
            sp.wait_ge(table_in, 16)
            sp.wait_ge(ends_out, 16 * (EXPERTS + 1))
            for r in range(2):
                sp.wait_ge(h2_out[r], 32 * IMAGES // 2)
                sp.wait_ge(rows_out[r], 96 * IMAGES // 2)
            sp.wait_ge(w_stored, 32 * IMAGES)

        @block.gpsimd
        def _(pool):
            filled = [0]

            def fill(dst, value):
                nc.gpsimd.memset(dst, value).then_inc(pool_setup, 1)
                filled[0] += 1
                pool.wait_ge(pool_setup, filled[0])

            fill(w_out[:], 0.0)
            nc.gpsimd.memset(half_neg[:], -0.5).then_inc(weights_zeroed, 1)
            pool.wait_ge(weights_zeroed, 1)
            fill(half_pos[:], 0.5)
            for r in range(2):
                fill(rden_all[r][:], 0.0)
                fill(shift[r][:], 0.0)
            fill(empty[:], 0.0)
            fill(empty[:, :, C:C + 1], NO_TOKEN)
            assert filled[0] == FILLS

            def setup():
                pool.wait_ge(const_in, 16 * CONSTS)
                nc.gpsimd.tensor_scalar(token[:], place0[:], -float(S), None, ALU.add).then_inc(pool_setup, 1)
                pool.wait_ge(pool_setup, FILLS + 1)
                pool.wait_ge(gain_sq, 1)
                nc.gpsimd.tensor_tensor(gain[:, 1, :], gain[:, 0, :], half_pos[:], ALU.pow).then_inc(gain_root, 1)

            def weights(at):
                if at.past(1):
                    pool.wait_ge(w_stored, at.back(1).done(32))
                for layer in range(2):
                    fast, slow, h_fast = w_in[0][3 * layer:3 * layer + 3]
                    total = w_sum[0][layer]
                    pool.wait_ge(w_scaled, at.done(2, layer + 1))
                    nc.gpsimd.tensor_tensor(slow[:], slow[:], fast[:], ALU.add).then_inc(w_chain, 1)
                    pool.wait_ge(w_chain, at.done(2, layer + 1))
                    nc.gpsimd.tensor_tensor(total[:], slow[:], h_fast[:], ALU.add).then_inc(w_summed, 1)

            def power(at, chain, k, ready, done, used):
                mv, ve, rs, nm = mean_var[k], var_eps[k], rstd[k], minus_mean[k]
                pool.wait_ge(ready, at.done())
                alone(pool, pool_passed)
                nc.gpsimd.tensor_scalar(ve[:], mv[:, :, 1], LN_EPS, None, ALU.add)
                nc.gpsimd.tensor_scalar(nm[:, 0, :], mv[:, :, 0], -1.0, None, ALU.mult).then_inc(chain, 1)
                pool.wait_ge(chain, at.done(2, 1))
                if at.past(1):
                    pool.wait_ge(used, at.back(1).done(GROUPS))
                nc.gpsimd.tensor_tensor(rs[:], ve[:], half_neg[:], ALU.pow).then_inc(chain, 1)
                pool.wait_ge(chain, at.done(2))
                nc.gpsimd.tensor_tensor(nm[:, 1, :], nm[:, 0, :], rs[:], ALU.mult).then_inc(done, 1)

            def gate(at):
                g = gates[at.ring(2)]
                pool.wait_ge(gate_exp, at.done())
                alone(pool, pool_passed)
                nc.gpsimd.tensor_scalar(g[:, 2, :], g[:, 1, :], 1.0, None, ALU.add).then_inc(gate_sum, 1)

            def gate_rows(at):
                g = gates[at.ring(2)]
                pool.wait_ge(gate_inv, at.done())
                nc.gpsimd.tensor_tensor(g[:, 4, :], g[:, 1, :], g[:, 3, :], ALU.mult)
                nc.gpsimd.tensor_scalar(token[:], token[:], float(S), None, ALU.add).then_inc(gate_chain, 1)
                pool.wait_ge(gate_chain, at.done())
                pair = rows[at.ring(2)]
                alone(pool, pool_passed)
                nc.gpsimd.tensor_copy(pair[0][:, :, C], token[:])
                nc.gpsimd.tensor_copy(pair[1][:, :, C], token[:])
                nc.gpsimd.tensor_copy(pair[0][:, :, C + 1], g[:, 3, :])
                nc.gpsimd.tensor_copy(pair[1][:, :, C + 1], g[:, 4, :]).then_inc(row_marked, 1)

            def place(at, k):
                if k == 0:
                    pool.wait_ge(row_copied, at.done())
                    pool.wait_ge(row_marked, at.done())
                    pool.wait_ge(pos_ready, at.done())
                    alone(pool, pool_passed)
                for g in range(GROUPS):
                    n = TEXT if g == 2 else GROUP
                    pool.indirect_dma_start(
                        rows_dram, bass.IndirectOffsetOnAxis(
                            ap=posi[at.ring(2)][0:n, k * GROUPS + g:k * GROUPS + g + 1], axis=0),
                        rows[at.ring(2)][k][0:n, g, :], None).then_inc(rows_out[at.ring(2)], 16)

            def body(i):
                five, four, three = i.back(5), i.back(4), i.back(3)
                if i.exists(IMAGES):
                    power(i, rstd_chain, 0, stats_ready, rstd_ready, xn_ready)
                if i.loop is None and i.j == 0:
                    setup()
                if four.exists(IMAGES):
                    pool.wait_ge(xn2_ready, four.done(GROUPS))
                    alone(pool, pool_passed)
                    pair = rows[four.ring(2)]
                    nc.gpsimd.tensor_copy(pair[1][:, :, 0:C], pair[0][:, :, 0:C]).then_inc(row_copied, 1)
                if five.exists(IMAGES):
                    gate_rows(five)
                    place(five, 0)
                if four.exists(IMAGES):
                    pool.wait_ge(norm2_ready, four.done())
                    nc.gpsimd.tensor_tensor(nrm[:, 1, :], nrm[:, 0, :], half_pos[:, 0:GROUPS], ALU.pow
                                            ).then_inc(norm_ready, 1)
                if five.exists(IMAGES):
                    place(five, 1)
                if three.exists(IMAGES):
                    r = three.ring(2)
                    pool.wait_ge(rden_in[three.ring(2)], three.uses(2, 64))
                    if three.past(2):
                        pool.wait_ge(made["out2"], three.back(2).done())
                    nc.gpsimd.tensor_tensor(attn_t[r][:, :, 0:S], heads_t[r][:], rden_all[r][:], ALU.mult
                                            ).then_inc(attn_ready, 1)
                if i.exists(IMAGES):
                    weights(i)
                if three.exists(IMAGES):
                    power(three, rstd2_chain, 1, stats2_ready, rstd2_ready, xn2_ready)
                if four.exists(IMAGES):
                    gate(four)

            iterations(pool, body)

        @block.vector
        def _(dve):
            for r in range(4):
                nc.vector.memset(resid[r][64:GROUP, 2, :], 0.0).then_inc(pads_zeroed, 1)
            for r in range(2):
                last = nc.vector.memset(xn_t[r][HALF:HALF + 1, 1, :], 1.0)
            last.then_inc(bias_row_ready, 1)

            lo = EXPERTS + PROBE

            def stack_ones(r):
                nc.vector.memset(stack[r][SCORE_ROWS:, HEADS:, 0:S], 1.0)

            for r in range(4):
                last = nc.vector.memset(stack[r][:, :, S:PAD], 0.0)
            last.then_inc(stack_padded, 1)
            stack_ones(0)

            def more_ones():
                stack_ones(1)
                for r in range(4):
                    nc.vector.memset(values[r][:, :, :, D:2 * D], 1.0)
                for r in range(2):
                    nc.vector.memset(attn_t[r][:, :, S:PAD], 0.0)

            def setup():
                step = Counter()
                nc.vector.memset(ones[:], 1.0)
                nc.vector.memset(w_route[:, :, ROUTE - 1:ROUTE], 1.0 / C).then_inc(setup_chain, 1)
                dve.wait_ge(setup_chain, step.next())
                dve.wait_ge(const_in, 16 * CONSTS)
                nc.vector.tensor_tensor(emb_sq[:], emb_all[:], emb_all[:], ALU.mult).then_inc(setup_chain, 1)
                dve.wait_ge(setup_chain, step.next())
                nc.vector.tensor_reduce(gain[:, 0, :], emb_sq[:], AX, ALU.add).then_inc(gain_sq, 1)
                dve.wait_ge(gain_root, 1)
                nc.vector.tensor_scalar(gain[:, 2, :], gain[:, 1, :], 0.02, 0.02, ALU.mult, ALU.add
                                        ).then_inc(setup_chain, 1)
                dve.wait_ge(setup_chain, step.next())
                nc.vector.tensor_scalar(gain[:, 3, :], gain[:, 1, :], 1e-12, None, ALU.max).then_inc(setup_chain, 1)
                dve.wait_ge(setup_chain, step.next())
                nc.vector.reciprocal(gain[:, 3, :], gain[:, 3, :]).then_inc(setup_chain, 1)
                dve.wait_ge(setup_chain, step.next())
                nc.vector.tensor_tensor(emb_t[:], emb_t[:], gain[0:PROBE, 3, :], ALU.mult).then_inc(emb_ready, 1)
                nc.vector.tensor_tensor(bias8[:], energy[:], fatigue[:], ALU.subtract).then_inc(setup_chain, 1)
                dve.wait_ge(setup_chain, step.next())
                nc.vector.tensor_scalar(bias8[:], bias8[:], 0.1, None, ALU.mult).then_inc(setup_chain, 1)
                dve.wait_ge(setup_chain, step.next())
                dve.wait_ge(align_made, 1)
                nc.vector.tensor_copy(w_route[:, 0, lo:lo + EXPERTS], ps[0:HALF, 0, 0:EXPERTS])
                nc.vector.tensor_copy(w_route[:, 1, lo:lo + EXPERTS], ps[0:HALF, 0, EXPERTS:2 * EXPERTS]
                                      ).then_inc(setup_done, 1)

            shift_c = [Counter(3) for _ in range(2)]
            ROUTE_STEPS = 19
            CHOICE = {14: (0,), 15: (1,), 16: (2,), 18: (3,), 19: (4,), 20: (5,), 22: (6, 7), 23: (8, 9),
                      24: (10, 11), 25: (12, 13), 26: (14, 15), 27: (16,)}
            place_c = Counter(3)

            def tok(at, g):
                dve.wait_ge(made[f"tok{g}"], at.done())
                if g == 0:
                    if at.past(4):
                        dve.wait_ge(taken["out2"], at.back(4).done())
                nc.vector.tensor_tensor(resid[at.ring(4)][:, g, :], bank(f"tok{g}")[0:GROUP, 0:C], b_tok[:], ALU.add
                                        ).then_inc(taken[f"tok{g}"], 1)

            def group_stats(at, h, k, chain, groups):
                for g in groups:
                    nc.vector.bn_stats(stats[k][:, g, :], h[:, g, :]).then_inc(chain, 1)

            def mean_and_variance(at, k, chain, ready):
                dve.wait_ge(chain, at.done(3))
                alone(dve, dve_passed)
                for g in range(GROUPS):
                    last = nc.vector.bn_aggr(mean_var[k][:, g, :], stats[k][:, g, :])
                last.then_inc(ready, 1)

            def remainder(at, m):
                dve.wait_ge(part1_ready, at.done(3, m + 1))
                if m == 0:
                    if at.past(1):
                        dve.wait_ge(part3_ready, at.back(1).done(3))
                nc.vector.tensor_tensor(rest[:, m, :], bank(f"qk{m}")[:, 0:S], parts[at.ring(2)][:, m, :], ALU.subtract
                                        ).then_inc(taken[f"qk{m}"], 1)

            def third_part(at, m):
                dve.wait_ge(part2_ready, at.done(3, m + 1))
                p = parts[at.ring(2)]
                nc.vector.tensor_tensor(p[:, 6 + m, :], rest[:, m, :], p[:, 3 + m, :], ALU.subtract
                                        ).then_inc(part3_ready, 1)

            def maximum(at, chunk):
                dve.wait_ge(max_made, at.done(CHUNKS, chunk + 1))
                h, g = chunk // GROUPS, chunk % GROUPS
                nc.vector.tensor_reduce(maxima[:, g, h:h + 1], ps[0:GROUP, chunk % 2, 0:S], AX, ALU.max
                                        ).then_inc(max_taken, 1)

            def shift_part(at, half, n):
                c, m = shift_c[half], maxima[:, :, 6 * half:6 * half + 6]
                s, r = shift[half], shift_rest[half]
                if n == 0:
                    dve.wait_ge(max_taken, at.done(CHUNKS, 18 * (half + 1)))
                    if at.past(1):
                        dve.wait_ge(made[f"shift{half}"], at.back(1).done())
                    nc.vector.tensor_scalar(s[:, :, 0:6], m, -1.0, None, ALU.mult).then_inc(shift_chain[half], 1)
                    return
                c.start(at, n - 1)
                dve.wait_ge(shift_chain[half], c.next())
                if n == 1:
                    nc.vector.scalar_tensor_tensor(r[:], m, -1.0, s[:, :, 0:6], ALU.mult, ALU.subtract
                                                   ).then_inc(shift_chain[half], 1)
                if n == 2:
                    nc.vector.tensor_copy(s[:, :, 6:12], r[:]).then_inc(shift_chain[half], 1)
                if n == 3:
                    nc.vector.tensor_tensor(s[:, :, 12:18], r[:], s[:, :, 6:12], ALU.subtract
                                            ).then_inc(shift_ready[half], 1)

            def invert(at):
                dve.wait_ge(den_in, at.done(16))
                if at.past(1):
                    dve.wait_ge(rden_out, at.back(1).done(16))
                nc.vector.reciprocal(rden[:], den[:]).then_inc(den_inverse, 1)

            def attention_out(at, name, groups):
                dve.wait_ge(made[name], at.done())
                if name == "out01":
                    if at.past(2):
                        dve.wait_ge(h2_out[at.back(2).ring(2)], at.back(2).uses(2, 32))
                n = len(groups)
                lo, hi = groups[0], groups[-1] + 1
                nc.vector.tensor_tensor(h2[at.ring(2)][:, lo:hi, :],
                                        bank(name)[0:GROUP, 0:n * C].rearrange("p (g c) -> p g c", g=n),
                                        resid[at.ring(4)][:, lo:hi, :], ALU.add).then_inc(taken[name], 1)

            b3 = [GROUP, GROUPS, EXPERTS]

            def over_experts(v):
                return v[:, :, None].broadcast_to(b3)

            def over_groups(v):
                return v[:, None, :].broadcast_to(b3)

            hot0 = hot[:, 0, :].rearrange("p (g e) -> p g e", g=GROUPS)
            hot1 = hot[:, 1, :].rearrange("p (g e) -> p g e", g=GROUPS)

            def route_copy(at):
                dve.wait_ge(made["route"], at.done())
                nc.vector.tensor_copy(routed[:], bank("route")[0:GROUP, 0:GROUPS * ROUTE].rearrange(
                    "p (g n) -> p g n", g=GROUPS)).then_inc(taken["route"], 1)

            def route_sums(at, n):
                if n == 0:
                    dve.wait_ge(taken["route"], at.done())
                    probe = routed[:, :, EXPERTS:lo]
                    nc.vector.tensor_tensor(sq[:], probe, probe, ALU.mult).then_inc(route_chain, 1)
                    nc.vector.tensor_tensor(tmp8[:], over_experts(routed[:, :, ROUTE - 1]),
                                            over_groups(gain[:, 2, :]), ALU.mult).then_inc(route_chain, 1)
                if n == 1:
                    route_after(at, 2)
                    nc.vector.tensor_reduce(nrm[:, 0, :], sq[:], AX, ALU.add).then_inc(norm2_ready, 1)
                    nc.vector.tensor_tensor(logit[:], routed[:, :, 0:EXPERTS], tmp8[:], ALU.add
                                            ).then_inc(route_chain, 1)

            def route_after(at, n):
                dve.wait_ge(route_chain, at.done(ROUTE_STEPS, n))

            def route_logits(at, n):
                if n == 0:
                    dve.wait_ge(norm_ready, at.done())
                    nc.vector.tensor_scalar(nrm[:, 2, :], nrm[:, 1, :], 1e-12, None, ALU.max
                                            ).then_inc(route_chain, 1)
                if n == 1:
                    route_after(at, 4)
                    nc.vector.reciprocal(nrm[:, 3, :], nrm[:, 2, :]).then_inc(route_chain, 1)
                if n == 2:
                    route_after(at, 5)
                    nc.vector.tensor_tensor(align[:], routed[:, :, lo:lo + EXPERTS], over_experts(nrm[:, 3, :]),
                                            ALU.mult).then_inc(route_chain, 1)
                if n == 3:
                    route_after(at, 6)
                    nc.vector.scalar_tensor_tensor(logit[:], align[:], 0.02, logit[:], ALU.mult, ALU.add
                                                   ).then_inc(route_chain, 1)
                if n == 4:
                    route_after(at, 7)
                    nc.vector.tensor_tensor(logit[:], logit[:], over_groups(bias8[:]), ALU.add
                                            ).then_inc(route_chain, 1)

            def choose(at, scores, k, n):
                route_after(at, 8 + 6 * k + n)
                if n == 0:
                    nc.vector.tensor_reduce(top[:, k, :], scores[:], AX, ALU.max).then_inc(route_chain, 1)
                if n == 1:
                    nc.vector.tensor_tensor(tmp8[:], scores[:], over_experts(top[:, k, :]), ALU.is_equal
                                            ).then_inc(route_chain, 1)
                if n == 2:
                    nc.vector.tensor_tensor(tmp8[:], tmp8[:], over_groups(ramp[:]), ALU.mult
                                            ).then_inc(route_chain, 1)
                if n == 3:
                    nc.vector.tensor_reduce(pick[:, k, :], tmp8[:], AX, ALU.min).then_inc(route_chain, 1)
                if n == 4:
                    nc.vector.tensor_tensor(hot[:, k, :].rearrange("p (g e) -> p g e", g=GROUPS),
                                            over_groups(ramp[:]), over_experts(pick[:, k, :]), ALU.is_equal
                                            ).then_inc(route_chain, 1)

            def mask_first(at):
                route_after(at, 13)
                nc.vector.scalar_tensor_tensor(masked[:], hot0, -3e38, logit[:], ALU.mult, ALU.add
                                               ).then_inc(route_chain, 1)

            def choices(at):
                route_after(at, ROUTE_STEPS)
                if at.past(1):
                    dve.wait_ge(made["rank"], at.back(1).done())
                nc.vector.tensor_tensor(chosen[:], hot0, hot1, ALU.add).then_inc(chosen_ready, 1)
                if at.past(2):
                    dve.wait_ge(rows_out[at.back(2).ring(2)], at.back(2).uses(2, 96))
                nc.vector.tensor_tensor(gates[at.ring(2)][:, 0, :], top[:, 1, :], top[:, 0, :], ALU.subtract
                                        ).then_inc(top_gap, 1)

            def place(at, n):
                ge = GROUPS * EXPERTS
                counts = bank("rank")[0:GROUP]
                if n == 0:
                    dve.wait_ge(made["rank"], at.done())
                    nc.vector.tensor_tensor(pos[:].rearrange("p (g e) -> p g e", g=GROUPS),
                                            counts[:, 0:ge].rearrange("p (g e) -> p g e", g=GROUPS),
                                            over_groups(base[:]), ALU.add).then_inc(place_chain, 1)
                    return
                place_c.start(at, n - 1)
                dve.wait_ge(place_chain, place_c.next())
                if n == 1:
                    nc.vector.tensor_tensor(base[:], base[:], counts[:, ge:ge + EXPERTS], ALU.add
                                            ).then_inc(taken["rank"], 1)
                    nc.vector.tensor_tensor(pos2[:], hot[:], pos[:, None, :].broadcast_to([GROUP, 2, ge]), ALU.mult
                                            ).then_inc(place_chain, 1)
                if n == 2:
                    nc.vector.tensor_reduce(posf[:], pos2[:].rearrange("p k (g e) -> p (k g) e", g=GROUPS),
                                            AX, ALU.add).then_inc(place_chain, 1)
                if n == 3:
                    nc.vector.tensor_copy(posi[at.ring(2)][:], posf[:]).then_inc(pos_ready, 1)

            def gate_inverse(at):
                dve.wait_ge(gate_sum, at.done())
                g = gates[at.ring(2)]
                nc.vector.reciprocal(g[:, 3, :], g[:, 2, :]).then_inc(gate_inv, 1)

            def body(i):
                one, two, three, four, five = (i.back(k) for k in (1, 2, 3, 4, 5))
                here = i.exists(IMAGES)
                if i.loop is None and i.j == 0:
                    dve.wait_ge(first_in, 32)
                    tok(i, 0)
                for chunk in range(CHUNKS):
                    if one.exists(IMAGES):
                        maximum(one, chunk)
                    if here:
                        if chunk == 0:
                            dve.wait_ge(text_in[i.ring(2)], i.uses(2, 16))
                            group_stats(i, resid[i.ring(4)], 0, stats_chain, (2,))
                        if chunk == 1:
                            dve.wait_ge(taken["tok0"], i.done())
                            group_stats(i, resid[i.ring(4)], 0, stats_chain, (0,))
                        if chunk == 2:
                            tok(i, 1)
                        if chunk == 3:
                            dve.wait_ge(taken["tok1"], i.done())
                            group_stats(i, resid[i.ring(4)], 0, stats_chain, (1,))
                        if chunk == 4:
                            if i.past(1):
                                dve.wait_ge(rstd_ready, i.back(1).done())
                            mean_and_variance(i, 0, stats_chain, stats_ready)
                        if chunk in (15, 17, 19):
                            remainder(i, chunk // 2 - 7)
                        if chunk in (17, 19, 21):
                            third_part(i, chunk // 2 - 8)
                    if i.back(-1).exists(IMAGES) and chunk == 34:
                        tok(i.back(-1), 0)
                    if i.loop is None and i.j == 0 and chunk == 5:
                        more_ones()
                    if i.loop is None and i.j == 0 and chunk in (15, 17):
                        stack_ones(chunk // 2 - 5)
                    if i.loop is None and i.j == 0 and chunk == 21:
                        setup()
                    if one.exists(IMAGES):
                        if chunk in (18, 20, 21, 22):
                            shift_part(one, 0, (18, 20, 21, 22).index(chunk))
                    if two.exists(IMAGES):
                        if chunk in (1, 3, 5, 7):
                            shift_part(two, 1, chunk // 2)
                    if three.exists(IMAGES):
                        if chunk == 11:
                            invert(three)
                        if chunk == 27:
                            attention_out(three, "out01", (0, 1))
                        if chunk == 28:
                            attention_out(three, "out2", (2,))
                        if chunk in (29, 30):
                            dve.wait_ge(taken["out2"], three.done())
                            group_stats(three, h2[three.ring(2)], 1, stats2_chain, ((0, 1), (2,))[chunk - 29])
                        if chunk == 31:
                            if three.past(1):
                                dve.wait_ge(rstd2_ready, three.back(1).done())
                            mean_and_variance(three, 1, stats2_chain, stats2_ready)
                    if four.exists(IMAGES):
                        if chunk == 10:
                            route_copy(four)
                        if chunk in (11, 12):
                            route_sums(four, chunk - 11)
                        for n in CHOICE.get(chunk, ()):
                            if n < 5:
                                route_logits(four, n)
                            elif n < 10:
                                choose(four, logit, 0, n - 5)
                            elif n == 10:
                                mask_first(four)
                            elif n < 16:
                                choose(four, masked, 1, n - 11)
                            else:
                                choices(four)
                        if chunk in (30, 31, 32, 33):
                            place(four, chunk - 30)
                    if five.exists(IMAGES) and chunk == 2:
                        gate_inverse(five)

            iterations(dve, body)

            dve.wait_ge(taken["rank"], IMAGES)
            step = Counter()
            nc.vector.tensor_copy(ends[:], base[:]).then_inc(ends_ready, 1)
            t = slice(0, TILES)
            count, tiles_of, upto, behind, mine, first, part, ones8 = (plan[t, n, :] for n in range(8))
            nc.vector.memset(ones8, 1.0).then_inc(plan_chain, 1)
            dve.wait_ge(plan_chain, step.next())
            nc.vector.tensor_tensor(count, base[t, :], region[t, :], ALU.subtract).then_inc(plan_chain, 1)
            dve.wait_ge(plan_chain, step.next())
            shape = [TILES, EXPERTS, MAXT]
            nc.vector.tensor_tensor(many[t], count[:, :, None].broadcast_to(shape),
                                         steps256[t, None, :].broadcast_to(shape), ALU.is_gt).then_inc(plan_chain, 1)
            dve.wait_ge(plan_chain, step.next())
            nc.vector.tensor_reduce(tiles_of, many[t], AX, ALU.add).then_inc(plan_chain, 1)
            dve.wait_ge(plan_chain, step.next())
            nc.vector.tensor_tensor_scan(upto, ones8, tiles_of, 0.0, ALU.mult, ALU.add).then_inc(plan_chain, 1)
            dve.wait_ge(plan_chain, step.next())
            nc.vector.tensor_scalar(behind, upto, tile_no[t, 0:1], None, ALU.is_le).then_inc(plan_chain, 1)
            dve.wait_ge(plan_chain, step.next())
            nc.vector.tensor_reduce(cell[t, 0:1], behind, AX, ALU.add).then_inc(plan_chain, 1)
            dve.wait_ge(plan_chain, step.next())
            nc.vector.tensor_scalar(mine, ramp[t, :], float(EXPERTS), cell[t, 0:1], ALU.add, ALU.is_equal
                                    ).then_inc(plan_chain, 1)
            dve.wait_ge(plan_chain, step.next())
            nc.vector.tensor_tensor(first, tiles_of, upto, ALU.subtract).then_inc(plan_chain, 1)
            dve.wait_ge(plan_chain, step.next())
            nc.vector.scalar_tensor_tensor(first, first, float(TILE), region[t, :], ALU.mult, ALU.add
                                           ).then_inc(plan_chain, 1)
            dve.wait_ge(plan_chain, step.next())
            nc.vector.tensor_tensor(part, mine, first, ALU.mult).then_inc(plan_chain, 1)
            dve.wait_ge(plan_chain, step.next())
            nc.vector.tensor_reduce(cell[t, 1:2], part, AX, ALU.add).then_inc(plan_chain, 1)
            dve.wait_ge(plan_chain, step.next())
            nc.vector.tensor_reduce(cell[t, 2:3], mine, AX, ALU.add).then_inc(plan_chain, 1)
            dve.wait_ge(plan_chain, step.next())
            nc.vector.tensor_tensor(part, mine, ramp[t, :], ALU.mult).then_inc(plan_chain, 1)
            dve.wait_ge(plan_chain, step.next())
            nc.vector.tensor_reduce(cell[t, 3:4], part, AX, ALU.add).then_inc(plan_chain, 1)
            dve.wait_ge(plan_chain, step.next())
            nc.vector.scalar_tensor_tensor(cell[t, 4:5], cell[t, 2:3], tile_no[t, 1:2], cell[t, 1:2],
                                                ALU.mult, ALU.add).then_inc(plan_chain, 1)
            dve.wait_ge(plan_chain, step.next())
            nc.vector.tensor_scalar(table[t, 1:2], cell[t, 4:5], float(ZERO_ROW), None, ALU.add
                                    ).then_inc(plan_chain, 1)
            dve.wait_ge(plan_chain, step.next())
            nc.vector.scalar_tensor_tensor(table[t, 0:1], cell[t, 2:3], float(EXPERTS), cell[t, 3:4],
                                           ALU.mult, ALU.add).then_inc(table_ready, 1)

        @block.scalar
        def _(act):
            def take(at, name, dst, src, sem_done=None):
                act.wait_ge(made[name], at.done())
                nc.scalar.activation(dst, src, ACT.Copy).then_inc(taken[name] if sem_done is None else sem_done, 1)

            def normalise(at, h, k, dst, g, rstd_done, done):
                if g == 0:
                    act.wait_ge(rstd_done, at.done())
                nc.scalar.activation(dst[:, g, 0:C], h[:, g, :], ACT.Identity, scale=rstd[k][:, g:g + 1],
                                     bias=minus_mean[k][:, 1, g:g + 1]).then_inc(done, 1)

            def body(i):
                one, two, three, four = (i.back(k) for k in (1, 2, 3, 4))
                here = i.exists(IMAGES)
                r = i.ring(2)

                for chunk in range(CHUNKS):
                    if three.exists(IMAGES) and chunk == 5:
                        take(three, "pv2", heads_t[three.ring(2)][:, 2, :], bank("pv2")[:, 0:S])
                    if four.exists(IMAGES) and chunk in (0, 1, 2):
                        if chunk == 0 and four.past(2):
                            act.wait_ge(rows_out[four.back(2).ring(2)], four.back(2).uses(2, 96))
                        normalise(four, h2[four.ring(2)], 1, rows[four.ring(2)][0], chunk,
                                  rstd2_ready, xn2_ready)
                    if four.exists(IMAGES) and chunk in (5, 6):
                        if chunk == 5 and four.past(1):
                            act.wait_ge(made["route"], four.back(1).done())
                        k = chunk - 5
                        take(four, f"x2t{k}", xn2_t[:, k, :], bank(f"x2t{k}")[0:HALF, 0:PAD])
                    for at, half, when in ((one, 0, 24), (two, 1, 9)):
                        if at.exists(IMAGES) and chunk == when:
                            if at.past(1):
                                act.wait_ge(shift_in[half], at.back(1).done(48))
                            take(at, f"shift{half}", shift_t[half][:],
                                 bank(f"shift{half}").bitcast(BF16)[0:18, 0:S])
                    if here:
                        if chunk in (7, 8, 9):
                            if chunk == 7 and i.past(1):
                                act.wait_ge(made["xt1"], i.back(1).done())
                            normalise(i, resid[i.ring(4)], 0, xn, chunk - 7, rstd_ready, xn_ready)
                        if chunk == 11:
                            if i.past(2):
                                act.wait_ge(made["v2"], i.back(2).done())
                        if chunk == 11:
                            for k in range(2):
                                take(i, f"xt{k}", xn_t[r][0:HALF, k, :], bank(f"xt{k}")[0:HALF, 0:PAD])
                        if chunk == 14:
                            if i.past(2):
                                act.wait_ge(parts_out[i.back(2).ring(2)], i.back(2).uses(2, 16))
                        if chunk in (14, 16, 18):
                            m = chunk // 2 - 7
                            take(i, f"qk{m}", parts[r][:, m, :], bank(f"qk{m}")[:, 0:S], part1_ready)
                        if chunk in (16, 18, 20):
                            m = chunk // 2 - 8
                            act.wait_ge(taken[f"qk{m}"], i.done())
                            nc.scalar.activation(parts[r][:, 3 + m, :], rest[:, m, :], ACT.Copy).then_inc(part2_ready, 1)
                        if chunk == 22:
                            if i.past(4):
                                act.wait_ge(made["pv2"], i.back(4).done())
                            take(i, "v01", values[i.ring(4)][:, 0:2, :, 0:D],
                                 bank("v01")[0:GROUP, 0:2 * C].rearrange("p (g h d) -> p g h d", g=2, h=HEADS))
                        if chunk in (24, 25):
                            act.wait_ge(w_loaded, i.done(96))
                            if i.loop is None and i.j == 0:
                                act.wait_ge(const_in, 16 * CONSTS)
                            layer = chunk - 24
                            slow = w_in[0][3 * layer + 1]
                            nc.scalar.activation(slow[:], slow[:], ACT.Copy, scale=m_gate[:, layer:layer + 1]
                                                 ).then_inc(w_scaled, 1)
                        if chunk == 23:
                            take(i, "v2", values[i.ring(4)][:, 2, :, 0:D],
                                 bank("v2")[0:GROUP, 0:C].rearrange("p (h d) -> p h d", h=HEADS))
                    if four.exists(IMAGES) and chunk == 29:
                        act.wait_ge(top_gap, four.done())
                        g = gates[four.ring(2)]
                        nc.scalar.activation(g[:, 1, :], g[:, 0, :], ACT.Exp).then_inc(gate_exp, 1)
                    if two.exists(IMAGES):
                        if chunk == 21:
                            if two.past(2):
                                act.wait_ge(attn_ready, two.back(2).done())
                            take(two, "pv0", heads_t[two.ring(2)][:, 0, :], bank("pv0")[:, 0:S])
                        if chunk == 31:
                            take(two, "pv1", heads_t[two.ring(2)][:, 1, :], bank("pv1")[:, 0:S])
                        act.wait_ge(key_made, two.done(CHUNKS, chunk + 1))
                        if chunk == 0 and two.past(1):
                            act.wait_ge(made["pv1"], two.back(1).done())
                        if chunk == 12 and two.past(1):
                            act.wait_ge(made["pv2"], two.back(1).done())
                        if chunk == 24:
                            act.wait_ge(made["pv0"], two.done())
                        h, g = chunk // GROUPS, chunk % GROUPS
                        buf = probs[(4 * two.ring(2) + h) % 8]
                        nc.scalar.activation(buf[:, g, :], ps[0:GROUP, 2 + chunk % 2, 0:S], ACT.Exp,
                                             scale=D ** -0.5).then_inc(exp_done, 1)

            iterations(act, body)

        @block.tensor
        def _(pe):
            def alignment():
                pe.wait_ge(emb_ready, 1)
                for k in range(2):
                    last = nc.tensor.matmul(ps[0:HALF, 0, k * EXPERTS:(k + 1) * EXPERTS],
                                            probe_w[:, k * HALF:(k + 1) * HALF], emb_t[:], start=True, stop=True)
                last.then_inc(align_made, 1)
                pe.wait_ge(setup_done, 1)

            def transposes(src, at, name):
                for g in range(GROUPS):
                    last = nc.tensor.transpose(bank(name)[0:HALF, g * GROUP:(g + 1) * GROUP], src(g),
                                               ident[0:GROUP, 0:GROUP])
                last.then_inc(made[name], 1)

            def product(at, name, part, parts):
                r = at.ring(2)
                to = bank(name)

                def share(n):
                    return range(part * n // parts, (part + 1) * n // parts)

                if name in ("tok0", "tok1"):
                    g = int(name[3])
                    if g == 0 and part == 0:
                        pe.wait_ge(patches_in[at.ring(2)], at.uses(2, 16))
                    n = PIXELS // 128
                    for k in share(n):
                        last = nc.tensor.matmul(to[0:GROUP, 0:C], patches[r][:, k, g * GROUP:(g + 1) * GROUP],
                                                w_tok[:, k, :], start=(k == 0), stop=(k == n - 1))
                elif name in ("xt0", "xt1"):
                    k = int(name[2])
                    pe.wait_ge(xn_ready, at.done(GROUPS))
                    return transposes(lambda g: xn[:, g, k * HALF:(k + 1) * HALF], at, name)
                elif name in ("x2t0", "x2t1"):
                    k = int(name[3])
                    pe.wait_ge(xn2_ready, at.done(GROUPS))
                    return transposes(lambda g: rows[r][0][:, g, k * HALF:(k + 1) * HALF], at, name)
                elif name in ("qk0", "qk1", "qk2"):
                    m = int(name[2])
                    if part == 0:
                        pe.wait_ge(taken["xt1"], at.done())
                    for k in share(2):
                        last = nc.tensor.matmul(to[:, 0:S], w_qkv[0:HALF + k, k, m * 128:(m + 1) * 128],
                                                xn_t[r][0:HALF + k, k, 0:S], start=(k == 0), stop=(k == 1))
                elif name in ("v01", "v2"):
                    groups = (0, 1) if name == "v01" else (2,)
                    for n in share(len(groups)):
                        g = groups[n]
                        for k in range(2):
                            last = nc.tensor.matmul(to[0:GROUP, n * C:(n + 1) * C],
                                                    xn_t[r][0:HALF + k, k, g * GROUP:(g + 1) * GROUP],
                                                    w_qkv[0:HALF + k, k, 2 * C:3 * C], start=(k == 0), stop=(k == 1))
                elif name in ("shift0", "shift1"):
                    half = int(name[5])
                    pe.wait_ge(shift_ready[half], at.done())
                    for g in range(GROUPS):
                        last = nc.tensor.transpose(to.bitcast(BF16)[:, g * GROUP:(g + 1) * GROUP],
                                                   shift[half][:, g, :], identb[0:GROUP, 0:GROUP])
                elif name in ("pv0", "pv1", "pv2"):
                    g = int(name[2])
                    if part == 0:
                        pe.wait_ge(exp_done, at.done(CHUNKS, 12 * (g + 1)))
                        if g == 0:
                            pe.wait_ge(taken["v2"], at.done())
                    for k in share(GROUPS):
                        n = TEXT if k == 2 else GROUP
                        for j in range(4):
                            h = 4 * g + j
                            last = nc.tensor.matmul(to[32 * j:32 * j + 32, 0:S], values[at.ring(4)][0:n, k, h, :],
                                                    probs[(4 * at.ring(2) + h) % 8][0:n, k, :],
                                                    start=(k == 0), stop=(k == GROUPS - 1), skip_group_check=True)
                elif name in ("out01", "out2"):
                    groups = (0, 1) if name == "out01" else (2,)
                    if part == 0:
                        pe.wait_ge(attn_ready, at.done())
                    for m in share(len(groups) * GROUPS):
                        n, k = m // GROUPS, m % GROUPS
                        g = groups[n]
                        last = nc.tensor.matmul(to[0:GROUP, n * C:(n + 1) * C],
                                                attn_t[r][:, k, g * GROUP:(g + 1) * GROUP], w_out[:, k, :],
                                                start=(k == 0), stop=(k == GROUPS - 1))
                elif name == "route":
                    if part == 0:
                        pe.wait_ge(taken["x2t1"], at.done())
                    for g in share(GROUPS):
                        for k in range(2):
                            last = nc.tensor.matmul(to[0:GROUP, g * ROUTE:(g + 1) * ROUTE],
                                                    xn2_t[:, k, g * GROUP:(g + 1) * GROUP], w_route[:, k, :],
                                                    start=(k == 0), stop=(k == 1))
                elif name == "rank":
                    pe.wait_ge(chosen_ready, at.done())
                    rows_of = (GROUP, GROUP, TEXT)
                    for g in range(GROUPS):
                        dst = to[0:GROUP, g * EXPERTS:(g + 1) * EXPERTS]
                        n = rows_of[g]
                        nc.tensor.matmul(dst, before[0:n, :], chosen[0:n, g, :], start=True, stop=(g == 0))
                        for e in range(g):
                            nc.tensor.matmul(dst, ones[:], chosen[:, e, :], start=False, stop=(e == g - 1))
                    for g in range(GROUPS):
                        last = nc.tensor.matmul(to[0:GROUP, GROUPS * EXPERTS:(GROUPS + 1) * EXPERTS],
                                                ones[0:rows_of[g], :], chosen[0:rows_of[g], g, :],
                                                start=(g == 0), stop=(g == GROUPS - 1))
                if part == parts - 1:
                    last.then_inc(made[name], 1)

            def product_before(i, n):
                while True:
                    n -= MIX
                    if n < 0:
                        n, i = n + len(STEPS), i.back(1)
                        if i.loop is None and i.j < 0:
                            return ("tok0", At(None, 0, UNROLL)) if n % MIX == NAMES.index("tok0") % MIX else (None, None)
                    name, at = STEPS[n][1], i.back(STEPS[n][2])
                    if at.exists(IMAGES):
                        return name, at

            def body(i):
                one, two = i.back(1), i.back(2)
                if i.loop is None and i.j == 0:
                    pe.wait_ge(first_in, 32)
                    product(i, "tok0", 0, 1)
                if i.loop is None and i.j == 1:
                    alignment()
                for chunk in range(CHUNKS):
                    h, g = chunk // GROUPS, chunk % GROUPS
                    if i.loop is None and i.j == 0 and chunk == 11:
                        pe.wait_ge(const_in, 16 * CONSTS)
                        pe.wait_ge(bias_row_ready, 1)
                    for n, (first, name, lag, parts) in enumerate(STEPS):
                        if first <= chunk < first + parts and i.back(lag).exists(IMAGES):
                            if chunk == first:
                                previous, image = product_before(i, n)
                                if previous:
                                    pe.wait_ge(taken[previous], image.done())
                            product(i.back(lag), name, chunk - first, parts)
                    if one.exists(IMAGES):
                        if chunk == 0:
                            pe.wait_ge(stack_in[one.ring(4)], one.uses(4, 160))
                        if positive(count := one.done(CHUNKS, chunk - 1)):
                            pe.wait_ge(max_taken, count)
                        st = stack[one.ring(4)]
                        nc.tensor.matmul(ps[0:GROUP, chunk % 2, 0:S],
                                         st[0:SCORE_ROWS, h, g * GROUP:(g + 1) * GROUP],
                                         st[0:SCORE_ROWS, HEADS + h, 0:S], start=True, stop=True
                                         ).then_inc(max_made, 1)
                    if two.exists(IMAGES):
                        if chunk in (0, CHUNKS // 2):
                            half = chunk // (CHUNKS // 2)
                            pe.wait_ge(shift_in[half], two.done(48))
                        if positive(count := two.done(CHUNKS, chunk - 1)):
                            pe.wait_ge(exp_done, count)
                        st = stack[two.ring(4)]
                        nc.tensor.matmul(ps[0:GROUP, 2 + chunk % 2, 0:S],
                                         st[:, HEADS + h, g * GROUP:(g + 1) * GROUP],
                                         st[:, h, 0:S], start=True, stop=True).then_inc(key_made, 1)

            iterations(pe, body)
        phase1.close()

        w1 = [kept(f"w1_{r}", [HALF, 2, HID]) for r in range(2)]
        w2 = [kept(f"w2_{r}", [128, HCH, C]) for r in range(2)]
        b1 = [kept(f"b1_{r}", [128, HCH]) for r in range(2)]
        b2 = [kept(f"b2_{r}", [128, C]) for r in range(2)]
        x_row = [kept(f"x_row{r}", [128, 2, ROW]) for r in range(4)]
        x_t = [kept(f"x_t{r}", [HALF, 2, TILE]) for r in range(2)]
        relu = [kept(f"relu{r}", [128, TILE]) for r in range(4)]
        hidden = [kept(f"hidden{r}", [128, HCH, TILE]) for r in range(2)]
        y_bias = kept("y_bias", [128, 2, C])
        y_gated = [kept(f"y_gated{r}", [128, 2, C]) for r in range(2)]
        token_no = [kept(f"token_no{r}", [128, 2], I32) for r in range(2)]
        ps_xt = ps[0:HALF, 0, :].rearrange("p (k t) -> p k t", k=2)
        ps_hid = [ps[:, 1 + n, 0:TILE] for n in range(4)]
        ps_y = ps[:, 5:7, 0:C]

        w1_in, w2_in, b1_in, b2_in = (sems(n, 2) for n in ("w1_in", "w2_in", "b1_in", "b2_in"))
        x_in = sems("x_in", 4)
        xt_made, xt_taken = sem("xt_made"), sem("xt_taken")
        hid_made, relu_done, hid_ready = sem("hid_made"), sem("relu_done"), sem("hid_ready")
        y_made, y_taken, y_ready = sem("y_made"), sem("y_taken"), sem("y_ready")
        scattered = sem("scattered")

        block2 = ctx.enter_context(nc.Block())

        @block2.sync
        def _(sp):
            def row_load(at):
                row = sp.value_load(table_row[0:1, bass.ds(at.times(2, 1), 1)], min_val=0, max_val=ZERO_ROW)
                if at.past(4):
                    sp.wait_ge(y_ready, at.back(4).done())
                alone(sp, sp_passed)
                sp.dma_start(x_row[at.ring(4)][:], rows_dram[bass.ds(row, TILE), :].rearrange("(p a) f -> p a f", a=2)
                             ).then_inc(x_in[at.ring(4)], 16)

            def body(at):
                if not at.exists(TILES):
                    return
                r, two = at.ring(2), at.back(2)
                if at.loop is None and at.j == 0:
                    row_load(at)
                if at.back(-1).exists(TILES):
                    row_load(at.back(-1))
                e = sp.value_load(table_row[0:1, bass.ds(at.times(2), 1)], min_val=0, max_val=EXPERTS - 1)
                if at.past(2):
                    sp.wait_ge(relu_done, two.done(HCH))
                alone(sp, sp_passed)
                sp.dma_start(w1[r][:], w1_dram[bass.ds(e, 1)].rearrange("o (k p) h -> p (o k) h", p=HALF)
                             ).then_inc(w1_in[r], 16)
                sp.dma_start(b1[r][:], a["b1_t"][bass.ds(e, 1)].rearrange("o p j -> (o p) j")).then_inc(b1_in[r], 16)
                if at.past(2):
                    sp.wait_ge(y_taken, two.done())
                alone(sp, sp_passed)
                sp.dma_start(w2[r][:], w2_dram[bass.ds(e, 1)].rearrange("o (j p) c -> p (o j) c", p=128)
                             ).then_inc(w2_in[r], 16)
                sp.dma_start(b2[r][:], a["L0_ffn_b2"][bass.ds(e, 1)].rearrange("o c -> (o c)").partition_broadcast(128)
                             ).then_inc(b2_in[r], 16)

            tiles(sp, body)

        @block2.vector
        def _(dve):
            def square(at):
                for j in range(HCH):
                    dve.wait_ge(relu_done, at.done(HCH, j + 1))
                    if j == 0:
                        if at.past(2):
                            dve.wait_ge(y_made, at.back(2).done())
                    rl = relu[(2 * at.ring(2) + j) % 4]
                    nc.vector.tensor_tensor(hidden[at.ring(2)][:, j, :], rl[:], rl[:], ALU.mult
                                            ).then_inc(hid_ready, 1)

            def output(at):
                r = at.ring(2)
                dve.wait_ge(b2_in[at.ring(2)], at.uses(2, 16))
                dve.wait_ge(y_made, at.done())
                if at.past(1):
                    dve.wait_ge(y_ready, at.back(1).done())
                nc.vector.tensor_tensor(y_bias[:], ps_y, b2[r][:, None, :].broadcast_to([128, 2, C]), ALU.add
                                        ).then_inc(y_taken, 1)
                dve.wait_ge(y_taken, at.done())
                if at.past(2):
                    dve.wait_ge(scattered, at.back(2).done(32))
                nc.vector.tensor_copy(token_no[r][:], x_row[at.ring(4)][:, :, C])
                for half in range(2):
                    last = nc.vector.tensor_scalar(y_gated[r][:, half, :], y_bias[:, half, :],
                                                   x_row[at.ring(4)][:, half, C + 1:C + 2], None, ALU.mult)
                last.then_inc(y_ready, 1)

            def body(at):
                if at.exists(TILES):
                    square(at)
                if at.back(1).exists(TILES):
                    output(at.back(1))

            tiles(dve, body)

        @block2.scalar
        def _(act):
            def rows_t(at):
                if at.past(2):
                    act.wait_ge(hid_made, at.back(2).done(HCH))
                act.wait_ge(xt_made, at.done())
                nc.scalar.activation(x_t[at.ring(2)][:], ps_xt, ACT.Copy).then_inc(xt_taken, 1)

            def body(at):
                if at.loop is None and at.j == 0:
                    rows_t(at)
                if at.exists(TILES):
                    act.wait_ge(b1_in[at.ring(2)], at.uses(2, 16))
                    for j in range(HCH):
                        act.wait_ge(hid_made, at.done(HCH, j + 1))
                        if positive(count := at.done(HCH, j - 3)):
                            act.wait_ge(hid_ready, count)
                        nc.scalar.activation(relu[(2 * at.ring(2) + j) % 4][:], ps_hid[(2 * at.ring(2) + j) % 4],
                                             ACT.Relu, bias=b1[at.ring(2)][:, j:j + 1]).then_inc(relu_done, 1)
                if at.back(-1).exists(TILES):
                    rows_t(at.back(-1))

            tiles(act, body)

        @block2.tensor
        def _(pe):
            def rows_t(at):
                r = at.ring(2)
                pe.wait_ge(x_in[at.ring(4)], at.uses(4, 16))
                if at.past(1):
                    pe.wait_ge(xt_taken, at.back(1).done())
                for k in range(2):
                    for half in range(2):
                        last = nc.tensor.transpose(ps_xt[:, k, half * 128:(half + 1) * 128],
                                                   x_row[at.ring(4)][:, half, k * HALF:(k + 1) * HALF], ident[:])
                last.then_inc(xt_made, 1)

            def hidden_layer(at):
                r = at.ring(2)
                pe.wait_ge(w1_in[at.ring(2)], at.uses(2, 16))
                pe.wait_ge(xt_taken, at.done())
                for j in range(HCH):
                    if positive(count := at.done(HCH, j - 3)):
                        pe.wait_ge(relu_done, count)
                    for k in range(2):
                        last = nc.tensor.matmul(ps_hid[(2 * r + j) % 4], w1[r][:, k, j * 128:(j + 1) * 128],
                                                x_t[r][:, k, :], start=(k == 0), stop=(k == 1))
                    last.then_inc(hid_made, 1)

            def output(at):
                r = at.ring(2)
                pe.wait_ge(w2_in[at.ring(2)], at.uses(2, 16))
                pe.wait_ge(hid_ready, at.done(HCH))
                if at.past(1):
                    pe.wait_ge(y_taken, at.back(1).done())
                for half in range(2):
                    for j in range(HCH):
                        last = nc.tensor.matmul(ps_y[:, half, :], hidden[r][:, j, half * 128:(half + 1) * 128],
                                                w2[r][:, j, :], start=(j == 0), stop=(j == HCH - 1))
                last.then_inc(y_made, 1)

            def body(at):
                if at.loop is None and at.j == 0:
                    rows_t(at)
                if at.exists(TILES):
                    hidden_layer(at)
                if at.back(-1).exists(TILES):
                    rows_t(at.back(-1))
                if at.back(1).exists(TILES):
                    output(at.back(1))

            tiles(pe, body)

        @block2.gpsimd
        def _(pool):
            def body(at):
                if not at.back(1).exists(TILES):
                    return
                at = at.back(1)
                if at.past(1):
                    pool.wait_ge(scattered, at.back(1).done(32))
                pool.wait_ge(y_ready, at.done())
                alone(pool, pool_passed)
                for half in range(2):
                    pool.indirect_dma_start(
                        out_rows, bass.IndirectOffsetOnAxis(ap=token_no[at.ring(2)][:, half:half + 1], axis=0),
                        y_gated[at.ring(2)][:, half, :], None, bounds_check=N - 1, oob_is_err=False,
                        compute_op=ALU.add).then_inc(scattered, 16)

            tiles(pool, body)
            pool.wait_ge(scattered, 32 * TILES)


def kernel(**inputs):
    import numpy as np
    import concourse.bacc as bacc
    from concourse.bass_utils import run_bass_kernel_spmd
    import ml_dtypes

    x = {k: np.ascontiguousarray(v) for k, v in inputs.items()}
    images = x.pop("x")
    side = 14
    px = images.shape[2] // side
    arrays = {
        "patches": images.reshape(IMAGES, 3, side, px, side, px).transpose(0, 1, 3, 5, 2, 4).reshape(
            IMAGES, PIXELS, PATCHES),
        "txt": x["txt"],
        "w_tok_t": x["L0_tok_W"].T,
        "L0_tok_b": x["L0_tok_b"],
        "w_qkv_t": x["L0_attn_w_qkv"].T,
        "L0_attn_b_qkv": x["L0_attn_b_qkv"],
        "w_out_t": x["L0_attn_w_out"].T,
        "L0_attn_b_out": x["L0_attn_b_out"],
        "router_t": x["L0_ffn_router_w"].T,
        "probe_t": x["L0_ffn_probe_w"].T,
        "L0_ffn_probe_w": x["L0_ffn_probe_w"],
        "L0_ffn_router_emb": x["L0_ffn_router_emb"],
        "emb_t": x["L0_ffn_router_emb"].T,
        "b1_t": x["L0_ffn_b1"].reshape(EXPERTS, HCH, 128).transpose(0, 2, 1),
        "L0_ffn_b2": x["L0_ffn_b2"],
        "m_gate1_rows": np.repeat(x["L0_ffn_m_gate1"], 128 // EXPERTS)[:, None],
        "m_gate2_rows": np.repeat(x["L0_ffn_m_gate2"], 128 // EXPERTS)[:, None],
        "ident": np.eye(128, dtype=np.float32),
        "identb": np.eye(128, dtype=ml_dtypes.bfloat16),
        "before": np.triu(np.ones((GROUP, GROUP)), 1).astype(ml_dtypes.bfloat16),
        "ramp": np.arange(EXPERTS, dtype=np.float32) - EXPERTS,
        "region": np.arange(EXPERTS, dtype=np.float32) * CAP,
        "steps256": np.arange(MAXT, dtype=np.float32) * TILE,
        "place0": (np.arange(GROUPS)[None, :] * GROUP + np.arange(GROUP)[:, None]).astype(np.float32),
        "tile_no": np.stack([np.arange(GROUP), np.arange(GROUP) * TILE - ZERO_ROW], 1).astype(np.float32),
    }
    for n in ("fatigue", "energy", "w_fast1", "w_slow1", "h_fast1", "w_fast2", "w_slow2", "h_fast2"):
        arrays[f"L0_ffn_{n}"] = x[f"L0_ffn_{n}"]
    arrays = {k: np.ascontiguousarray(v) for k, v in arrays.items()}
    nc = bacc.Bacc("TRN2", target_bir_lowering=False, num_devices=1)
    aps = {k: nc.dram_tensor(f"in_{k}", v.shape, mybir.dt.from_np(v.dtype), kind="ExternalInput").ap()
           for k, v in arrays.items()}
    out = nc.dram_tensor("out", (IMAGES, S, C), F32, kind="ExternalOutput").ap()
    build(nc, aps, out)
    r = run_bass_kernel_spmd(nc, [{f"in_{k}": v for k, v in arrays.items()}], core_ids=[0])
    return r.results[0]["out"]
```
